# Optimizing a Trainium2 kernel written in Bass

```python
import numpy as np
import jax
import jax.numpy as jnp

def _softmax(x, axis=-1):
    return jax.nn.softmax(x, axis=axis)

def _gelu(x):
    return jax.nn.gelu(x, approximate=True)

def _silu(x):
    return jax.nn.silu(x)

def _sigmoid(x):
    return jax.nn.sigmoid(x)

def _layernorm(x, axis=-1, eps=1e-05):
    m = jnp.mean(x, axis=axis, keepdims=True)
    v = jnp.var(x, axis=axis, keepdims=True)
    return (x - m) / jnp.sqrt(v + eps)

def _scatter_add(tgt, idx, src, axis=0):
    return tgt.at[idx].add(src)

def _segment_sum(src, seg, n):
    return jax.ops.segment_sum(src, seg, n)
kernel_name = 'mk_hybrid_d1_jaxref_r4_93f9a0'

def setup_inputs(seed: int=0):
    np.random.seed(seed)
    _w = jnp.asarray

    def _L0_attn_a_setup():
        import jax, jax.numpy as jnp
        import numpy as np
        NUM_HEADS = 16
        STREAMING_WINDOW = 256

        def _h2o_forward(hidden_states, Wq, Wk, Wv, Wo):
            B, S, H = hidden_states.shape
            nh = NUM_HEADS
            hd = H // nh
            W = STREAMING_WINDOW

            def proj(w):
                y = jnp.einsum('bsh,oh->bso', hidden_states, w)
                return y.reshape(B, S, nh, hd).transpose(0, 2, 1, 3)
            q = proj(Wq)
            k = proj(Wk)
            v = proj(Wv)
            scale = 1.0 / np.sqrt(hd)
            neg = jnp.finfo(hidden_states.dtype).min
            outs = []
            for start in range(0, S, W):
                end = min(start + W, S)
                ws = end - start
                wq = q[:, :, start:end, :]
                wk = k[:, :, :end, :]
                wv = v[:, :, :end, :]
                scores = jnp.einsum('bhqd,bhkd->bhqk', wq, wk) * scale
                mask = jnp.triu(jnp.ones((ws, end), dtype=bool), k=1)
                scores = jnp.where(mask[None, None], neg, scores)
                attn = jax.nn.softmax(scores, axis=-1)
                outs.append(jnp.einsum('bhqk,bhkd->bhqd', attn, wv))
            out = jnp.concatenate(outs, axis=2)
            out = out.transpose(0, 2, 1, 3).reshape(B, S, H)
            return jnp.einsum('bsh,oh->bso', out, Wo)
        key = jax.random.key(seed)
        ks = jax.random.split(key, 5)
        B, S, H = (1, 512, 256)
        hidden_states = jax.random.normal(ks[0], (B, S, H), dtype=jnp.float32)
        Wq = jax.random.normal(ks[1], (H, H), dtype=jnp.float32) * 0.02
        Wk = jax.random.normal(ks[2], (H, H), dtype=jnp.float32) * 0.02
        Wv = jax.random.normal(ks[3], (H, H), dtype=jnp.float32) * 0.02
        Wo = jax.random.normal(ks[4], (H, H), dtype=jnp.float32) * 0.02
        return {'hidden_states': hidden_states, 'Wq': Wq, 'Wk': Wk, 'Wv': Wv, 'Wo': Wo}
    _L0_attn_a_in = _L0_attn_a_setup()

    def _L0_attn_b_setup():
        import jax, jax.numpy as jnp
        import numpy as np
        from jax import lax
        B, L, D = (2, 1024, 256)
        ORDER = 2
        EMB = 3
        FO = 64
        K = 3

        def _implicit_filter(seq_len, freqs_i, w1, b1, w2, b2, w3, b3, decay_i):
            t = jnp.linspace(0.0, 1.0, seq_len)
            ang = 2.0 * jnp.pi * freqs_i[None, :] * t[:, None]
            enc = jnp.concatenate([jnp.sin(ang), jnp.cos(ang), t[:, None]], axis=-1)
            h = jax.nn.gelu(enc @ w1 + b1, approximate=False)
            h = jax.nn.gelu(h @ w2 + b2, approximate=False)
            h = h @ w3 + b3
            window = jnp.exp(-jnp.abs(decay_i)[None, :] * t[:, None] * seq_len)
            return h * window

        def _fft_conv(v, h):
            seq_len = v.shape[1]
            fft_len = 1 << (2 * seq_len - 1).bit_length()
            v_f = jnp.fft.rfft(v, n=fft_len, axis=1)
            h_f = jnp.fft.rfft(h, n=fft_len, axis=0)[None]
            y = jnp.fft.irfft(v_f * h_f, n=fft_len, axis=1)
            return y[:, :seq_len, :]

        def _gated_control(u, kw, kb, gw, gb):
            xc = lax.conv_general_dilated(u, kw, window_strides=(1,), padding=[(K // 2, K // 2)], dimension_numbers=('NWC', 'WIO', 'NWC'), feature_group_count=u.shape[-1]) + kb
            gate = jax.nn.sigmoid(xc @ gw + gb)
            return xc * gate
        key = jax.random.key(seed)
        ks = jax.random.split(key, 10)
        f32 = jnp.float32
        rn = lambda k, shape, s=0.02: jax.random.normal(k, shape, dtype=f32) * s
        return {'x': jax.random.normal(ks[0], (B, L, D), dtype=f32), 'in_proj_w': rn(ks[1], (D, (ORDER + 1) * D)), 'in_proj_b': jnp.zeros(((ORDER + 1) * D,), f32), 'out_proj_w': rn(ks[2], (D, D)), 'out_proj_b': jnp.zeros((D,), f32), 'freqs': rn(ks[3], (ORDER, EMB), 0.01), 'mlp_w1': rn(ks[4], (ORDER, 2 * EMB + 1, FO), 0.1), 'mlp_b1': jnp.zeros((ORDER, FO), f32), 'mlp_w2': rn(ks[5], (ORDER, FO, FO), 0.1), 'mlp_b2': jnp.zeros((ORDER, FO), f32), 'mlp_w3': rn(ks[6], (ORDER, FO, D), 0.1), 'mlp_b3': jnp.zeros((ORDER, D), f32), 'decay': jnp.full((ORDER, D), 0.5, f32), 'conv_w': rn(ks[7], (ORDER, K, 1, D), 0.1), 'conv_b': jnp.zeros((ORDER, D), f32), 'gate_w': rn(ks[8], (ORDER, D, D)), 'gate_b': jnp.zeros((ORDER, D), f32)}
    _L0_attn_b_in = _L0_attn_b_setup()

    def _L0_ffn_setup():
        import jax, jax.numpy as jnp
        import numpy as np
        D_MODEL = 256
        HIDDEN = 1024
        N_ROUTING = 2
        key = jax.random.key(seed)
        ks = jax.random.split(key, 10)
        s = 0.02
        x = jax.random.normal(ks[0], (4, 1024, D_MODEL), dtype=jnp.float32)
        gate_w = jax.random.normal(ks[1], (N_ROUTING, D_MODEL), dtype=jnp.float32) * s
        w1 = jax.random.normal(ks[2], (N_ROUTING, D_MODEL, HIDDEN), dtype=jnp.float32) * s
        b1 = jax.random.normal(ks[3], (N_ROUTING, HIDDEN), dtype=jnp.float32) * s
        w2 = jax.random.normal(ks[4], (N_ROUTING, HIDDEN, D_MODEL), dtype=jnp.float32) * s
        b2 = jax.random.normal(ks[5], (N_ROUTING, D_MODEL), dtype=jnp.float32) * s
        sw1 = jax.random.normal(ks[6], (D_MODEL, HIDDEN), dtype=jnp.float32) * s
        sb1 = jax.random.normal(ks[7], (HIDDEN,), dtype=jnp.float32) * s
        sw2 = jax.random.normal(ks[8], (HIDDEN, D_MODEL), dtype=jnp.float32) * s
        sb2 = jax.random.normal(ks[9], (D_MODEL,), dtype=jnp.float32) * s
        return {'x': x, 'gate_w': gate_w, 'w1': w1, 'b1': b1, 'w2': w2, 'b2': b2, 'sw1': sw1, 'sb1': sb1, 'sw2': sw2, 'sb2': sb2}
    _L0_ffn_in = _L0_ffn_setup()
    _d = {'L0_attn_a_hidden_states': _L0_attn_a_in['hidden_states'], 'L0_attn_a_Wq': _L0_attn_a_in['Wq'], 'L0_attn_a_Wk': _L0_attn_a_in['Wk'], 'L0_attn_a_Wv': _L0_attn_a_in['Wv'], 'L0_attn_a_Wo': _L0_attn_a_in['Wo'], 'L0_attn_b_in_proj_w': _L0_attn_b_in['in_proj_w'], 'L0_attn_b_in_proj_b': _L0_attn_b_in['in_proj_b'], 'L0_attn_b_out_proj_w': _L0_attn_b_in['out_proj_w'], 'L0_attn_b_out_proj_b': _L0_attn_b_in['out_proj_b'], 'L0_attn_b_freqs': _L0_attn_b_in['freqs'], 'L0_attn_b_mlp_w1': _L0_attn_b_in['mlp_w1'], 'L0_attn_b_mlp_b1': _L0_attn_b_in['mlp_b1'], 'L0_attn_b_mlp_w2': _L0_attn_b_in['mlp_w2'], 'L0_attn_b_mlp_b2': _L0_attn_b_in['mlp_b2'], 'L0_attn_b_mlp_w3': _L0_attn_b_in['mlp_w3'], 'L0_attn_b_mlp_b3': _L0_attn_b_in['mlp_b3'], 'L0_attn_b_decay': _L0_attn_b_in['decay'], 'L0_attn_b_conv_w': _L0_attn_b_in['conv_w'], 'L0_attn_b_conv_b': _L0_attn_b_in['conv_b'], 'L0_attn_b_gate_w': _L0_attn_b_in['gate_w'], 'L0_attn_b_gate_b': _L0_attn_b_in['gate_b'], 'L0_ffn_gate_w': _L0_ffn_in['gate_w'], 'L0_ffn_w1': _L0_ffn_in['w1'], 'L0_ffn_b1': _L0_ffn_in['b1'], 'L0_ffn_w2': _L0_ffn_in['w2'], 'L0_ffn_b2': _L0_ffn_in['b2'], 'L0_ffn_sw1': _L0_ffn_in['sw1'], 'L0_ffn_sb1': _L0_ffn_in['sb1'], 'L0_ffn_sw2': _L0_ffn_in['sw2'], 'L0_ffn_sb2': _L0_ffn_in['sb2']}
    _x0 = _d['L0_attn_a_hidden_states']
    _d['L0_attn_a_hidden_states'] = jax.random.normal(jax.random.fold_in(jax.random.key(seed), 1), (8, 1024, 256), dtype=_x0.dtype)
    del _x0
    return _d

def reference(L0_attn_a_hidden_states, L0_attn_a_Wq, L0_attn_a_Wk, L0_attn_a_Wv, L0_attn_a_Wo, L0_attn_b_in_proj_w, L0_attn_b_in_proj_b, L0_attn_b_out_proj_w, L0_attn_b_out_proj_b, L0_attn_b_freqs, L0_attn_b_mlp_w1, L0_attn_b_mlp_b1, L0_attn_b_mlp_w2, L0_attn_b_mlp_b2, L0_attn_b_mlp_w3, L0_attn_b_mlp_b3, L0_attn_b_decay, L0_attn_b_conv_w, L0_attn_b_conv_b, L0_attn_b_gate_w, L0_attn_b_gate_b, L0_ffn_gate_w, L0_ffn_w1, L0_ffn_b1, L0_ffn_w2, L0_ffn_b2, L0_ffn_sw1, L0_ffn_sb1, L0_ffn_sw2, L0_ffn_sb2):

    def _L0_attn_a_ref(hidden_states, Wq, Wk, Wv, Wo):
        import jax, jax.numpy as jnp
        import numpy as np
        NUM_HEADS = 16
        STREAMING_WINDOW = 256

        def _h2o_forward(hidden_states, Wq, Wk, Wv, Wo):
            B, S, H = hidden_states.shape
            nh = NUM_HEADS
            hd = H // nh
            W = STREAMING_WINDOW

            def proj(w):
                y = jnp.einsum('bsh,oh->bso', hidden_states, w)
                return y.reshape(B, S, nh, hd).transpose(0, 2, 1, 3)
            q = proj(Wq)
            k = proj(Wk)
            v = proj(Wv)
            scale = 1.0 / np.sqrt(hd)
            neg = jnp.finfo(hidden_states.dtype).min
            outs = []
            for start in range(0, S, W):
                end = min(start + W, S)
                ws = end - start
                wq = q[:, :, start:end, :]
                wk = k[:, :, :end, :]
                wv = v[:, :, :end, :]
                scores = jnp.einsum('bhqd,bhkd->bhqk', wq, wk) * scale
                mask = jnp.triu(jnp.ones((ws, end), dtype=bool), k=1)
                scores = jnp.where(mask[None, None], neg, scores)
                attn = jax.nn.softmax(scores, axis=-1)
                outs.append(jnp.einsum('bhqk,bhkd->bhqd', attn, wv))
            out = jnp.concatenate(outs, axis=2)
            out = out.transpose(0, 2, 1, 3).reshape(B, S, H)
            return jnp.einsum('bsh,oh->bso', out, Wo)
        return _h2o_forward(hidden_states, Wq, Wk, Wv, Wo)

    def _L0_attn_b_ref(x, in_proj_w, in_proj_b, out_proj_w, out_proj_b, freqs, mlp_w1, mlp_b1, mlp_w2, mlp_b2, mlp_w3, mlp_b3, decay, conv_w, conv_b, gate_w, gate_b):
        import jax, jax.numpy as jnp
        import numpy as np
        from jax import lax
        B, L, D = (2, 1024, 256)
        ORDER = 2
        EMB = 3
        FO = 64
        K = 3

        def _implicit_filter(seq_len, freqs_i, w1, b1, w2, b2, w3, b3, decay_i):
            t = jnp.linspace(0.0, 1.0, seq_len)
            ang = 2.0 * jnp.pi * freqs_i[None, :] * t[:, None]
            enc = jnp.concatenate([jnp.sin(ang), jnp.cos(ang), t[:, None]], axis=-1)
            h = jax.nn.gelu(enc @ w1 + b1, approximate=False)
            h = jax.nn.gelu(h @ w2 + b2, approximate=False)
            h = h @ w3 + b3
            window = jnp.exp(-jnp.abs(decay_i)[None, :] * t[:, None] * seq_len)
            return h * window

        def _fft_conv(v, h):
            seq_len = v.shape[1]
            fft_len = 1 << (2 * seq_len - 1).bit_length()
            v_f = jnp.fft.rfft(v, n=fft_len, axis=1)
            h_f = jnp.fft.rfft(h, n=fft_len, axis=0)[None]
            y = jnp.fft.irfft(v_f * h_f, n=fft_len, axis=1)
            return y[:, :seq_len, :]

        def _gated_control(u, kw, kb, gw, gb):
            xc = lax.conv_general_dilated(u, kw, window_strides=(1,), padding=[(K // 2, K // 2)], dimension_numbers=('NWC', 'WIO', 'NWC'), feature_group_count=u.shape[-1]) + kb
            gate = jax.nn.sigmoid(xc @ gw + gb)
            return xc * gate
        _, seq_len, d = x.shape
        proj = x @ in_proj_w + in_proj_b
        v = proj[..., :d]
        for i in range(ORDER):
            ctrl = proj[..., (i + 1) * d:(i + 2) * d]
            h = _implicit_filter(seq_len, freqs[i], mlp_w1[i], mlp_b1[i], mlp_w2[i], mlp_b2[i], mlp_w3[i], mlp_b3[i], decay[i])
            v = _fft_conv(v, h)
            v = v * _gated_control(ctrl, conv_w[i], conv_b[i], gate_w[i], gate_b[i])
        return v @ out_proj_w + out_proj_b

    def _L0_ffn_ref(x, gate_w, w1, b1, w2, b2, sw1, sb1, sw2, sb2):
        import jax, jax.numpy as jnp
        import numpy as np
        D_MODEL = 256
        HIDDEN = 1024
        N_ROUTING = 2
        B, S, D = x.shape
        xf = x.reshape(-1, D)
        gate_scores = xf @ gate_w.T
        gate_probs = jax.nn.softmax(gate_scores, axis=-1)
        top1 = jnp.argmax(gate_probs, axis=-1)
        one_hot = jax.nn.one_hot(top1, N_ROUTING, dtype=xf.dtype)
        masked = xf[None, :, :] * one_hot.T[:, :, None]
        h = jax.nn.relu(jnp.einsum('end,edh->enh', masked, w1) + b1[:, None, :])
        expert_out = jnp.einsum('enh,ehd->end', h, w2) + b2[:, None, :]
        routing_output = expert_out.sum(axis=0)
        shared = jax.nn.relu(xf @ sw1 + sb1) @ sw2 + sb2
        return (routing_output + shared).reshape(B, S, D)
    x = L0_attn_a_hidden_states
    x = x + _L0_attn_a_ref(_layernorm(x, axis=-1), L0_attn_a_Wq, L0_attn_a_Wk, L0_attn_a_Wv, L0_attn_a_Wo)
    x = x + _L0_ffn_ref(_layernorm(x, axis=-1), L0_ffn_gate_w, L0_ffn_w1, L0_ffn_b1, L0_ffn_w2, L0_ffn_b2, L0_ffn_sw1, L0_ffn_sb1, L0_ffn_sw2, L0_ffn_sb2)
    x = x + _L0_attn_b_ref(_layernorm(x, axis=-1), L0_attn_b_in_proj_w, L0_attn_b_in_proj_b, L0_attn_b_out_proj_w, L0_attn_b_out_proj_b, L0_attn_b_freqs, L0_attn_b_mlp_w1, L0_attn_b_mlp_b1, L0_attn_b_mlp_w2, L0_attn_b_mlp_b2, L0_attn_b_mlp_w3, L0_attn_b_mlp_b3, L0_attn_b_decay, L0_attn_b_conv_w, L0_attn_b_conv_b, L0_attn_b_gate_w, L0_attn_b_gate_b)
    x = x + _L0_ffn_ref(_layernorm(x, axis=-1), L0_ffn_gate_w, L0_ffn_w1, L0_ffn_b1, L0_ffn_w2, L0_ffn_b2, L0_ffn_sw1, L0_ffn_sb1, L0_ffn_sw2, L0_ffn_sb2)
    return x

_drawn_inputs = setup_inputs


def setup_inputs(seed=0):
    import zlib

    import numpy as np

    out = dict(_drawn_inputs(seed))
    spreads = {'L0_attn_b_in_proj_b': (0.0, 0.1),
     'L0_attn_b_out_proj_b': (0.0, 0.1),
     'L0_attn_b_mlp_b1': (0.0, 0.1),
     'L0_attn_b_mlp_b2': (0.0, 0.1),
     'L0_attn_b_mlp_b3': (0.0, 0.1),
     'L0_attn_b_decay': (0.5, 0.2),
     'L0_attn_b_conv_b': (0.0, 0.1),
     'L0_attn_b_gate_b': (0.0, 0.1)}
    factors = {}
    for name, (base, spread) in spreads.items():
        noise = np.random.default_rng([zlib.crc32(name.encode()), seed]).standard_normal(out[name].shape)
        drawn = base * np.exp(spread * noise) if base else spread * noise
        out[name] = jnp.asarray(drawn.astype(out[name].dtype))
    for name, factor in factors.items():
        out[name] = (out[name] * factor).astype(out[name].dtype)
    return out
```

```python
import numpy as np
import concourse.bass as bass
from concourse import mybir
from contextlib import ExitStack

F32 = mybir.dt.float32
F32R = mybir.dt.float32r
BF16 = mybir.dt.bfloat16
U32 = mybir.dt.uint32
I32 = mybir.dt.int32
ALU = mybir.AluOpType
ACT = mybir.ActivationFunctionType
AX = mybir.AxisListType

P = 128
B, S, D = 8, 1024, 256
T = B * S
HID = 1024
DH = D // P
TILE = 512
SUB = TILE // P
SLOTS = T + TILE
NTILES = SLOTS // TILE
ROW = 2 * D + 8
HB = HID // P
EPS = 1e-5
MASKED = -1e37


def f32(ap):
    return ap.bitcast(F32)


class Memory:

    def __init__(self, nc, ctx, tag):
        self.nc, self.ctx, self.tag = nc, ctx, tag
        self.sems = []
        ctx.callback(self.clear)

    def sb(self, name, shape, dt=F32):
        return self.ctx.enter_context(self.nc.sbuf_tensor(f"{self.tag}_{name}", shape, dt))

    def ps(self, name, shape, dt=F32):
        return self.ctx.enter_context(self.nc.psum_tensor(f"{self.tag}_{name}", shape, dt))

    def sem(self, name):
        self.sems.append(self.nc.alloc_semaphore(name=f"{self.tag}_{name}"))
        return self.sems[-1]

    def clear(self):
        self.nc.clear_and_free_semaphores(self.sems)
        self.nc.all_engine_barrier()


def feed_forward(nc, tag, consts, rows, count0, w1, b1, w2, b2, sw1, sb1, sw2, sb2, out):
    NETS = 3
    STEPS = 2 * HB
    RING = 4
    LAG = 2
    up_w = [sw1, w1[0], w1[1]]
    down_w = [sw2, w2[0], w2[1]]
    with ExitStack() as ctx:
        m = Memory(nc, ctx, tag)
        w_raw = m.sb("w_raw", [P, 2, DH * HID])
        up_hi = m.sb("up_hi", [P, NETS, DH, HID], F32R)
        up_lo = m.sb("up_lo", [P, NETS, DH, HID], F32R)
        dn_hi = m.sb("dn_hi", [P, NETS, HB, D], F32R)
        dn_lo = m.sb("dn_lo", [P, NETS, HB, D], F32R)
        xn = m.sb("xn", [P, SUB, D])
        res = m.sb("res", [P, SUB, ROW])
        xt_hi = m.sb("xt_hi", [P, DH, TILE], F32R)
        xt_lo = m.sb("xt_lo", [P, DH, TILE], F32R)
        h_f = m.sb("h_f", [P, RING, TILE])
        h_hi = m.sb("h_hi", [P, RING, TILE], F32R)
        h_lo = m.sb("h_lo", [P, RING, TILE], F32R)
        y_sb = m.sb("y_sb", [P, SUB, D])
        token = m.sb("token", [P, SUB], U32)
        b_up = m.sb("b_up", [P, NETS, HB])
        b_tile = m.sb("b_tile", [P, NTILES, HB])
        c_hid = m.sb("c_hid", [P, 2, HB])
        c_wide = m.sb("c_wide", [P, 2, HB, P])
        row_b = m.sb("row_b", [P, NETS, D])
        konst = m.sb("konst", [P, 2, D])
        k_tile = m.sb("k_tile", [P, D])
        flag = m.sb("flag", [P, NTILES])
        nflag = m.sb("nflag", [P, NTILES])
        flag_u = m.sb("flag_u", [P, NTILES], U32)
        start = m.sb("start", [P, NTILES])
        n0 = m.sb("n0", [P, 1])
        up_ps = m.ps("up_ps", [P, RING, TILE])
        t_ps = m.ps("t_ps", [P, DH, TILE])
        y_ps = m.ps("y_ps", [P, SUB, D])

        w_loaded = [m.sem(f"w_loaded{n}") for n in range(2)]
        w_hi = m.sem("w_hi")
        w_lo = m.sem("w_lo")
        b_loaded = m.sem("b_loaded")
        tiles_known = m.sem("tiles_known")
        starts_made = m.sem("starts_made")
        const_hid = m.sem("const_hid")
        const_y = m.sem("const_y")
        const_done = m.sem("const_done")
        xn_loaded = m.sem("xn_loaded")
        res_loaded = m.sem("res_loaded")
        transposed = m.sem("transposed")
        xt_hi_done = m.sem("xt_hi_done")
        xt_lo_done = m.sem("xt_lo_done")
        up_done = m.sem("up_done")
        h_act = m.sem("h_act")
        h_hi_done = m.sem("h_hi_done")
        h_lo_done = m.sem("h_lo_done")
        down_done = m.sem("down_done")
        y_done = m.sem("y_done")
        base_done = m.sem("base_done")
        base_step = m.sem("base_step")
        y_stored = m.sem("y_stored")
        held = m.sem("held")

        tile_rows = rows.rearrange("(t s p) c -> t p s c", p=P, s=SUB)

        with nc.Block() as block:

            @block.sync
            def _(sp):
                for n in range(2 * NETS):
                    net, down = divmod(n, 2)
                    if n >= 2:
                        sp.wait_ge(w_lo, n - 1)
                    src = (down_w if down else up_w)[net].rearrange("(c p) n -> p c n", p=P)
                    dst = w_raw[:, n % 2, :].rearrange("p (c n) -> p c n", c=HB if down else DH)
                    sp.dma_start(dst, src).then_inc(w_loaded[n % 2], 16)
                    if n == 0:
                        sp.dma_start(xn[:, :, :], tile_rows[0, :, :, D:2 * D]).then_inc(xn_loaded, 16)
                        sp.dma_start(res[:, :, :], tile_rows[0]).then_inc(res_loaded, 16)

                def load(i):
                    sp.wait_ge(transposed, DH * i)
                    sp.sem_inc(held, 1)
                    sp.dma_start(xn[:, :, :], rows[bass.ds(i * TILE, TILE), D:2 * D]
                                 .rearrange("(s p) c -> p s c", p=P)).then_inc(xn_loaded, 16)
                    sp.wait_ge(y_done, 1 + i)
                    sp.sem_inc(held, 1)
                    sp.dma_start(res[:, :, :], rows[bass.ds(i * TILE, TILE), :]
                                 .rearrange("(s p) c -> p s c", p=P)).then_inc(res_loaded, 16)

                with sp.Fori(1, NTILES) as i:
                    load(i)

            @block.gpsimd
            def _(pool):
                pool.dma_start(b_up[:, 0, :], sb1).then_inc(b_loaded, 16)
                for e in range(2):
                    pool.dma_start(b_up[:, 1 + e, :], b1[e]).then_inc(b_loaded, 16)
                pool.dma_start(row_b[:, 0, :], sb2.rearrange("(a n) -> a n", a=1).broadcast_to([P, D])).then_inc(b_loaded, 16)
                for e in range(2):
                    pool.dma_start(row_b[:, 1 + e, :], b2[e:e + 1, :].broadcast_to([P, D])).then_inc(b_loaded, 16)
                pool.dma_start(n0[:, :], count0.broadcast_to([P, 1])).then_inc(b_loaded, 16)
                pool.iota(start[:, :], pattern=[[TILE, NTILES]], base=0, channel_multiplier=0,
                          allow_small_or_imprecise_dtypes=True).then_inc(starts_made, 1)

                def scatter(i):
                    for s in range(SUB):
                        if s == 0:
                            pool.wait_ge(y_done, i + 2)
                            pool.sem_inc(held, 1)
                        pool.indirect_dma_start(out, bass.IndirectOffsetOnAxis(token[:, s:s + 1], 0),
                                                y_sb[:, s, :], None, bounds_check=T - 1,
                                                oob_is_err=False).then_inc(y_stored, 16)

                with pool.Fori(0, NTILES) as i:
                    scatter(i)
                pool.wait_ge(y_stored, 16 * SUB * NTILES)

            @block.tensor
            def _(pe):
                pe.sem_inc(down_done, RING)
                pe.sem_inc(up_done, 1)

                def transposes(i):
                    pe.wait_ge(xn_loaded, 16 * i + 16)
                    pe.wait_ge(xt_lo_done, DH * i + 1)
                    for d in range(DH):
                        for s in range(SUB):
                            last = nc.tensor.transpose(t_ps[:, d, s * P:(s + 1) * P],
                                                       xn[:, s, d * P:(d + 1) * P], consts.ident[:, :])
                        last.then_inc(transposed, 1)

                def up(i, s, net):
                    g = i * STEPS + s
                    j = s % HB
                    if s == 0:
                        pe.wait_ge(xt_lo_done, DH * i + DH + 1)
                    pe.wait_ge(h_act, g + 1)
                    terms = [(a, b, d) for d in range(DH) for a, b in
                             ((up_hi, xt_lo), (up_lo, xt_hi), (up_hi, xt_hi))]
                    for n, (a, b, d) in enumerate(terms):
                        last = nc.tensor.matmul(up_ps[:, s % RING, :], a[:, net, d, j * P:(j + 1) * P],
                                                b[:, d, :], start=n == 0, stop=n == len(terms) - 1)
                    last.then_inc(up_done, 1)

                def down(i, s, net):
                    g = i * STEPS + s
                    j = s % HB
                    if s == 0:
                        pe.wait_ge(y_done, i + 1)
                    pe.wait_ge(h_lo_done, g + RING + 1)
                    for t in range(SUB):
                        for n, (a, b) in enumerate(((h_hi, dn_lo), (h_lo, dn_hi), (h_hi, dn_hi))):
                            last = nc.tensor.matmul(y_ps[:, t, :], a[:, s % RING, t * P:(t + 1) * P],
                                                    b[:, net, j, :],
                                                    start=s == 0 and n == 0 and t % 2 == 0,
                                                    stop=s == STEPS - 1 and n == 2, skip_group_check=True)
                    last.then_inc(down_done, 1)

                def steps(i, of, net, more):
                    for s in of:
                        if s < STEPS:
                            up(i, s, net if s >= HB else 0)
                        if s == STEPS - 1 and more:
                            transposes(i + 1)
                        if s >= LAG:
                            down(i, s - LAG, net if s - LAG >= HB else 0)

                expert = pe.alloc_register(f"{tag}_expert")

                def tile(i, more):
                    steps(i, range(HB), 0, more)
                    pe.reg_load(expert, flag_u[0:1, bass.ds(i, 1)])
                    with pe.If_lt(expert, 1):
                        steps(i, range(HB, STEPS + LAG), 1, more)
                    with pe.Else():
                        steps(i, range(HB, STEPS + LAG), 2, more)

                pe.wait_ge(xn_loaded, 16)
                transposes(0)
                for e in range(2):
                    pe.wait_ge(w_lo, 2 * e + 4)
                    pe.wait_ge(const_hid, e + 1)
                    terms = [(j, w) for j in range(HB) for w in (dn_hi, dn_lo)]
                    for n, (j, w) in enumerate(terms):
                        last = nc.tensor.matmul(up_ps[:, e, 0:D], c_wide[:, e, j, :],
                                                f32(w[:, 1 + e, j, :]), start=n == 0, stop=n == len(terms) - 1)
                    last.then_inc(const_y, 1)
                pe.wait_ge(tiles_known, 4)
                pe.wait_ge(const_done, 3)
                with pe.Fori(0, NTILES - 1) as i:
                    tile(i, True)
                tile(NTILES - 1, False)

            @block.scalar
            def _(act):
                act.sem_inc(h_act, RING)

                def split(i):
                    for d in range(DH):
                        act.wait_ge(transposed, DH * i + d + 1)
                        if d == 0:
                            act.wait_ge(up_done, STEPS * i + 1)
                        nc.scalar.activation(xt_hi[:, d, :], t_ps[:, d, :], ACT.Copy).then_inc(xt_hi_done, 1)

                def hidden(i, s):
                    g = i * STEPS + s
                    act.wait_ge(up_done, g + 2)
                    act.wait_ge(h_lo_done, g + 1)
                    bias = b_up[:, 0, s:s + 1] if s < HB else b_tile[:, i, s - HB:s - HB + 1] if isinstance(i, int) \
                        else b_tile[:, bass.ds(i, 1), s - HB:s - HB + 1].rearrange("p a b -> p (a b)")
                    nc.scalar.activation(h_f[:, s % RING, :], up_ps[:, s % RING, :], ACT.Relu,
                                         bias=bias).then_inc(h_act, 1)

                act.wait_ge(b_loaded, 16 * 7)
                split(0)
                act.wait_ge(tiles_known, 4)
                with act.Fori(0, NTILES - 1) as i:
                    for s in range(STEPS):
                        hidden(i, s)
                    split(i + 1)
                for s in range(STEPS):
                    hidden(NTILES - 1, s)

            @block.vector
            def _(dve):
                dve.sem_inc(h_lo_done, RING)
                dve.sem_inc(y_done, 1)
                dve.sem_inc(xt_lo_done, 1)
                for n in range(2 * NETS):
                    net, down = divmod(n, 2)
                    hi, lo = (dn_hi, dn_lo) if down else (up_hi, up_lo)
                    raw = w_raw[:, n % 2, :].rearrange("p (c n) -> p c n", c=HB if down else DH)
                    dve.wait_ge(w_loaded[n % 2], 16 * (n // 2 + 1))
                    nc.vector.tensor_copy(hi[:, net, :, :], raw).then_inc(w_hi, 1)
                    dve.wait_ge(w_hi, n + 1)
                    nc.vector.tensor_tensor(lo[:, net, :, :], raw, f32(hi[:, net, :, :]), ALU.subtract).then_inc(w_lo, 1)
                    if n == 0:
                        dve.wait_ge(b_loaded, 16 * 7)
                        dve.wait_ge(starts_made, 1)
                        nc.vector.tensor_scalar(flag[:, :], start[:, :], n0[:, 0:1], None, ALU.is_ge).then_inc(tiles_known, 1)
                        dve.wait_ge(tiles_known, 1)
                        nc.vector.tensor_copy(flag_u[:, :], flag[:, :])
                        nc.vector.tensor_scalar(nflag[:, :], flag[:, :], -1.0, 1.0, ALU.mult, ALU.add).then_inc(tiles_known, 1)
                        dve.wait_ge(tiles_known, 2)
                        wide = [P, NTILES, HB]
                        nc.vector.tensor_tensor(b_tile[:, :, :], b_up[:, 1:2, :].broadcast_to(wide),
                                                nflag[:, :].unsqueeze(2).broadcast_to(wide), ALU.mult)
                        nc.vector.tensor_tensor(c_wide[:, 0, :, :].rearrange("p a b -> p (a b)")[:, 0:NTILES * HB].rearrange("p (a b) -> p a b", b=HB),
                                                b_up[:, 2:3, :].broadcast_to(wide),
                                                flag[:, :].unsqueeze(2).broadcast_to(wide), ALU.mult).then_inc(tiles_known, 1)
                        dve.wait_ge(tiles_known, 3)
                        nc.vector.tensor_tensor(b_tile[:, :, :], b_tile[:, :, :],
                                                c_wide[:, 0, :, :].rearrange("p a b -> p (a b)")[:, 0:NTILES * HB].rearrange("p (a b) -> p a b", b=HB),
                                                ALU.add).then_inc(tiles_known, 1)
                        dve.wait_ge(tiles_known, 4)
                        nc.vector.tensor_relu(c_hid[:, :, :], b_up[:, 1:3, :]).then_inc(h_hi_done, 1)
                        dve.wait_ge(h_hi_done, 1)
                        for e in range(2):
                            nc.vector.tensor_copy(c_wide[:, e, :, :],
                                                  c_hid[:, e, :].unsqueeze(2).broadcast_to([P, HB, P])).then_inc(const_hid, 1)

                def split(i):
                    for d in range(DH):
                        dve.wait_ge(xt_hi_done, DH * i + d + 1)
                        nc.vector.tensor_tensor(xt_lo[:, d, :], t_ps[:, d, :], f32(xt_hi[:, d, :]),
                                                ALU.subtract).then_inc(xt_lo_done, 1)

                def base(i):
                    at = slice(i, i + 1) if isinstance(i, int) else bass.ds(i, 1)
                    dve.wait_ge(base_step, 3 * i + 1)
                    nc.vector.tensor_scalar(k_tile[:, :], konst[:, 0, :], nflag[:, at], None, ALU.mult).then_inc(base_step, 1)
                    dve.wait_ge(base_step, 3 * i + 2)
                    nc.vector.scalar_tensor_tensor(k_tile[:, :], konst[:, 1, :], flag[:, at], k_tile[:, :],
                                                   ALU.mult, ALU.add).then_inc(base_step, 1)
                    dve.wait_ge(res_loaded, 16 * i + 16)
                    dve.wait_ge(base_step, 3 * i + 3)
                    nc.vector.tensor_tensor(res[:, :, 0:D], res[:, :, 0:D],
                                            k_tile[:, :].unsqueeze(1).broadcast_to([P, SUB, D]), ALU.add).then_inc(base_step, 1)

                def hidden(i, s):
                    g = i * STEPS + s
                    dve.wait_ge(h_act, g + RING + 1)
                    dve.wait_ge(down_done, g + 1)
                    nc.vector.tensor_copy(h_hi[:, s % RING, :], h_f[:, s % RING, :]).then_inc(h_hi_done, 1)
                    dve.wait_ge(h_hi_done, g + 2)
                    nc.vector.tensor_tensor(h_lo[:, s % RING, :], h_f[:, s % RING, :], f32(h_hi[:, s % RING, :]),
                                            ALU.subtract).then_inc(h_lo_done, 1)

                def finish(i):
                    dve.wait_ge(down_done, STEPS * i + STEPS + RING)
                    dve.wait_ge(base_step, 3 * i + 4)
                    dve.wait_ge(y_stored, 16 * SUB * i)
                    nc.vector.tensor_copy(token[:, :], res[:, :, 2 * D:2 * D + 1].rearrange("p s c -> p (s c)").bitcast(U32))
                    nc.vector.tensor_tensor(y_sb[:, :, :], y_ps[:, :, :], res[:, :, 0:D], ALU.add).then_inc(y_done, 1)

                split(0)
                for e in range(2):
                    dve.wait_ge(const_y, 2)
                    if e == 0:
                        nc.vector.tensor_tensor(row_b[:, 1, :], row_b[:, 1, :], row_b[:, 2, :], ALU.add).then_inc(const_done, 1)
                    dve.wait_ge(const_done, 1 + e)
                    nc.vector.scalar_tensor_tensor(konst[:, e, :], up_ps[:, 1 - e, 0:D], 1.0, row_b[:, 1, :],
                                                   ALU.mult, ALU.add).then_inc(const_done, 1)
                dve.wait_ge(const_done, 3)
                nc.vector.tensor_tensor(konst[:, :, :], konst[:, :, :], row_b[:, 0:1, :].broadcast_to([P, 2, D]),
                                        ALU.add).then_inc(base_step, 1)
                def blocks(i):
                    for s in range(STEPS):
                        hidden(i, s)
                        if s == HB - 1:
                            base(i)

                with dve.Fori(0, NTILES - 1) as i:
                    blocks(i)
                    split(i + 1)
                    finish(i)
                blocks(NTILES - 1)
                finish(NTILES - 1)


class Constants:

    def __init__(self, nc, ctx):
        m = Memory(nc, ctx, "c")
        self.ident = m.sb("ident", [P, P])
        self.ident_bf = m.sb("ident_bf", [P, P], BF16)
        self.before = m.sb("before", [P, P])
        self.ones = m.sb("ones", [P, P])
        self.minus_half = m.sb("minus_half", [P, 16])
        self.head_rows = m.sb("head_rows", [P, 8])
        self.mask_q = m.sb("mask_q", [P, 2, 512], BF16)
        self.mask_k = m.sb("mask_k", [P, 512], BF16)
        self.made = m.sem("made")
        self.zeroed = m.sem("zeroed")

    def make(self, nc):
        with nc.Block() as block:
            @block.gpsimd
            def _(pool):
                pool.memset(self.ident[:, :], 0.0).then_inc(self.zeroed, 1)
                pool.memset(self.ones[:, :], 1.0).then_inc(self.zeroed, 1)
                pool.wait_ge(self.zeroed, 2)
                pool.affine_select(out=self.ident[:, :], in_=self.ident[:, :], compare_op=ALU.not_equal, fill=1.0,
                                   base=0, pattern=[[-1, P]], channel_multiplier=1).then_inc(self.made, 1)
                pool.affine_select(out=self.before[:, :], in_=self.ones[:, :], compare_op=ALU.is_gt, fill=0.0,
                                   base=0, pattern=[[1, P]], channel_multiplier=-1).then_inc(self.made, 1)
                pool.wait_ge(self.made, 2)
                pool.tensor_copy(self.ident_bf[:, :], self.ident[:, :]).then_inc(self.made, 1)
                pool.memset(self.minus_half[:, :], -0.5).then_inc(self.made, 1)
                pool.affine_select(out=self.head_rows[:, :], in_=self.ones[:, 0:8], compare_op=ALU.is_ge, fill=0.0,
                                   base=0, pattern=[[-16, 8]], channel_multiplier=1).then_inc(self.made, 1)
                pool.wait_ge(self.made, 5)
                pool.affine_select(out=self.head_rows[:, :], in_=self.head_rows[:, :], compare_op=ALU.is_ge, fill=0.0,
                                   base=15, pattern=[[16, 8]], channel_multiplier=-1).then_inc(self.made, 1)
                pool.memset(self.mask_q[:, :, :], 0.0).then_inc(self.zeroed, 1)
                pool.memset(self.mask_k[:, :], 0.0).then_inc(self.zeroed, 1)
                pool.wait_ge(self.zeroed, 4)
                pool.affine_select(out=self.mask_q[:, 0, :], in_=self.mask_q[:, 0, :], compare_op=ALU.is_ge, fill=MASKED,
                                   base=0, pattern=[[0, 4], [-1, P]], channel_multiplier=1).then_inc(self.made, 1)
                pool.affine_select(out=self.mask_q[:, 1, :], in_=self.mask_q[:, 1, :], compare_op=ALU.is_ge, fill=MASKED,
                                   base=P, pattern=[[0, 2], [-1, 2 * P]], channel_multiplier=1).then_inc(self.made, 1)
                pool.affine_select(out=self.mask_k[:, :], in_=self.mask_k[:, :], compare_op=ALU.is_ge, fill=MASKED,
                                   base=0, pattern=[[0, 4], [1, P]], channel_multiplier=-1).then_inc(self.made, 1)
                pool.wait_ge(self.made, 9)


NT = S // P
HEADS = 16
HD = D // HEADS
WIN = 256
KT = WIN // P
HW = 64
PAIRS = HEADS // 2
OW = 32
GROUPS = HEADS // 4


class LayerNorm:

    def __init__(self, m, name, consts, n):
        self.n, self.consts = n, consts
        self.stat = m.sb(f"{name}_stat", [P, n, 6])
        self.mv = m.sb(f"{name}_mv", [P, n, 2])
        self.rstd = m.sb(f"{name}_rstd", [P, n])
        self.stats_done = m.sem(f"{name}_stats")
        self.aggr_done = m.sem(f"{name}_aggr")
        self.eps_added = m.sem(f"{name}_eps")
        self.rstd_done = m.sem(f"{name}_rstd")
        self.done = m.sem(f"{name}_done")
        self.held = m.sem(f"{name}_held")

    def stats(self, nc, dve, i, x):
        for t in range(self.n):
            nc.vector.bn_stats(self.stat[:, t, :], x[:, t, :]).then_inc(self.stats_done, 1)
        dve.wait_ge(self.stats_done, self.n * i + self.n)
        dve.sem_inc(self.held, 1)
        for t in range(self.n):
            nc.vector.bn_aggr(self.mv[:, t, :], self.stat[:, t, :]).then_inc(self.aggr_done, 1)

    def power(self, nc, pool, i):
        pool.wait_ge(self.aggr_done, self.n * i + self.n)
        pool.sem_inc(self.held, 1)
        nc.gpsimd.tensor_scalar(self.rstd[:, :], self.mv[:, :, 1:2].rearrange("p n a -> p (n a)"), EPS, None,
                                ALU.add).then_inc(self.eps_added, 1)
        pool.wait_ge(self.eps_added, i + 1)
        nc.gpsimd.tensor_tensor(self.rstd[:, :], self.rstd[:, :], self.consts.minus_half[:, 0:self.n],
                                ALU.pow).then_inc(self.rstd_done, 1)

    def apply(self, nc, dve, i, x, out):
        dve.wait_ge(self.rstd_done, i + 1)
        for t in range(self.n):
            nc.vector.tensor_scalar(out[:, t, :], x[:, t, :], self.mv[:, t, 0:1], self.rstd[:, t:t + 1],
                                    ALU.subtract, ALU.mult).then_inc(self.done, 1)


class Route:

    def __init__(self, nc, m, consts, rows, count0):
        self.consts, self.rows, self.count0 = consts, rows, count0
        self.ln = LayerNorm(m, "route", consts, NT)
        self.row = m.sb("row", [P, NT, ROW])
        self.gate = m.sb("gate", [P, 2, D])
        self.gate_d = m.sb("gate_d", [P, D])
        self.prod = m.sb("prod", [P, D])
        self.score = m.sb("score", [P, NT])
        self.to1 = m.sb("to1", [P, NT])
        self.total = m.sb("total", [P, NT])
        self.upto = m.sb("upto", [P, NT])
        self.carry = m.sb("carry", [P, 1])
        self.place = m.sb("place", [P, NT])
        self.back = m.sb("back", [P, NT])
        self.ones_n = m.sb("ones_n", [P, NT])
        self.slot = m.sb("slot", [P, NT], U32)
        self.fill = m.sb("fill", [P, SUB, ROW])
        self.n0 = m.sb("n0", [P, 1])
        self.n0_u = m.sb("n0_u", [P, 1], U32)
        self.gate_loaded = m.sem("gate_loaded")
        self.gate_done = m.sem("gate_done")
        self.x_done = m.sem("x_done")
        self.scored = m.sem("scored")
        self.chosen = m.sem("chosen")
        self.counted = m.sem("counted")
        self.step = m.sem("slot_step")
        self.slots_done = m.sem("slots_done")
        self.sent = m.sem("sent")
        self.held = m.sem("slots_held")
        self.numbered = m.sem("numbered")
        self.finished = m.sem("finished")
        self.end_written = m.sem("end_written")

    def load(self, eng, gate_w):
        for e in range(2):
            eng.dma_start(self.gate[:, e, :], gate_w[e:e + 1, :].broadcast_to([P, D])).then_inc(self.gate_loaded, 16)

    def prepare_pool(self, nc, pool):
        nc.gpsimd.iota(self.place[:, :], pattern=[[P, NT]], base=0, channel_multiplier=1,
                       allow_small_or_imprecise_dtypes=True).then_inc(self.numbered, 1)

    def prepare(self, nc, dve):
        dve.wait_ge(self.gate_loaded, 32)
        nc.vector.tensor_tensor(self.gate_d[:, :], self.gate[:, 1, :], self.gate[:, 0, :], ALU.subtract).then_inc(self.gate_done, 1)
        nc.vector.memset(self.carry[:, :], 0.0).then_inc(self.gate_done, 1)
        nc.vector.memset(self.ones_n[:, :], 1.0).then_inc(self.gate_done, 1)
        nc.vector.memset(self.row[:, :, 2 * D:ROW], 0.0).then_inc(self.gate_done, 1)
        nc.vector.memset(self.fill[:, :, :], 0.0).then_inc(self.gate_done, 1)
        dve.wait_ge(self.gate_done, 5)
        nc.vector.memset(self.fill[:, :, 2 * D:2 * D + 1].bitcast(U32), 2 * T).then_inc(self.gate_done, 1)
        dve.wait_ge(self.gate_done, 6)
        dve.wait_ge(self.numbered, 1)

    def vector_stats(self, nc, dve, i):
        dve.wait_ge(self.x_done, NT * i + NT)
        self.ln.stats(nc, dve, i, self.row[:, :, 0:D])

    def vector_choose(self, nc, dve, i):
        row, ln = self.row, self.ln
        ln.apply(nc, dve, i, row[:, :, 0:D], row[:, :, D:2 * D])
        for t in range(NT):
            dve.wait_ge(ln.done, NT * i + t + 1)
            dve.wait_ge(self.scored, NT * i + t)
            nc.vector.tensor_tensor_reduce(self.prod[:, :], row[:, t, D:2 * D], self.gate_d[:, :], 1.0, 0.0,
                                           ALU.mult, ALU.add, self.score[:, t:t + 1]).then_inc(self.scored, 1)
        dve.wait_ge(self.scored, NT * i + NT)
        nc.vector.tensor_scalar(self.to1[:, :], self.score[:, :], 0.0, None, ALU.is_gt).then_inc(self.chosen, 1)

    def tensor(self, nc, pe, i, ps):
        pe.wait_ge(self.chosen, i + 1)
        nc.tensor.matmul(ps[:, 0, :], self.consts.before[:, :], self.to1[:, :], start=True, stop=True)
        nc.tensor.matmul(ps[:, 1, :], self.consts.ones[:, :], self.to1[:, :], start=True, stop=True).then_inc(self.counted, 1)

    def vector_slots(self, nc, dve, i, ps):
        N = 9
        n = [0]

        def link(ins):
            n[0] += 1
            ins.then_inc(self.step, 1)
            dve.wait_ge(self.step, N * i + n[0])

        dve.wait_ge(self.counted, i + 1)
        link(nc.vector.tensor_copy(self.total[:, :], ps[:, 1, :]))
        link(nc.vector.tensor_tensor_scan(self.upto[:, :], self.ones_n[:, :], self.total[:, :], self.carry[:, 0:1],
                                          ALU.mult, ALU.add))
        link(nc.vector.tensor_copy(self.carry[:, :], self.upto[:, NT - 1:NT]))
        link(nc.vector.tensor_tensor(self.upto[:, :], self.upto[:, :], self.total[:, :], ALU.subtract))
        link(nc.vector.tensor_tensor(self.upto[:, :], self.upto[:, :], ps[:, 0, :], ALU.add))
        link(nc.vector.tensor_tensor(self.upto[:, :], self.place[:, :], self.upto[:, :], ALU.subtract))
        link(nc.vector.tensor_scalar(self.back[:, :], self.place[:, :], -1.0, float(SLOTS - 1), ALU.mult, ALU.add))
        link(nc.vector.tensor_tensor(self.back[:, :], self.back[:, :], self.to1[:, :], ALU.mult))
        link(nc.vector.tensor_tensor(self.upto[:, :], self.upto[:, :], self.back[:, :], ALU.add))
        nc.vector.tensor_copy(self.row[:, :, 2 * D:2 * D + 1].rearrange("p t a -> p (t a)").bitcast(U32), self.place[:, :])
        nc.vector.tensor_copy(self.slot[:, :], self.upto[:, :]).then_inc(self.slots_done, 1)
        dve.wait_ge(self.slots_done, 2 * i + 1)
        nc.vector.tensor_scalar(self.place[:, :], self.place[:, :], float(S), None, ALU.add).then_inc(self.slots_done, 1)
        dve.wait_ge(self.slots_done, 2 * i + 2)

    def pool(self, nc, pool, i):
        pool.wait_ge(self.slots_done, 2 * i + 1)
        pool.sem_inc(self.held, 1)
        for t in range(NT):
            pool.indirect_dma_start(self.rows[:, :], bass.IndirectOffsetOnAxis(self.slot[:, t:t + 1], 0),
                                    self.row[:, t, :], None, bounds_check=SLOTS - 1,
                                    oob_is_err=False).then_inc(self.sent, 16)

    def vector_end(self, nc, dve, rounds):
        nc.vector.tensor_scalar(self.n0[:, :], self.carry[:, :], -1.0, float(T), ALU.mult, ALU.add).then_inc(self.finished, 1)
        dve.wait_ge(self.finished, 1)
        nc.vector.tensor_copy(self.n0_u[:, :], self.n0[:, :]).then_inc(self.finished, 1)

    def sync_end(self, nc, sp, rounds):
        sp.wait_ge(self.finished, 2)
        sp.wait_ge(self.sent, 16 * NT * rounds)
        sp.dma_start(self.count0, self.n0[0:1, 0:1]).then_inc(self.end_written, 16)
        first = sp.value_load(self.n0_u[0:1, 0:1], min_val=0, max_val=T)
        sp.dma_start(self.rows[bass.ds(first, TILE), :].rearrange("(s p) c -> p s c", p=P),
                     self.fill[:, :, :]).then_inc(self.end_written, 16)
        sp.wait_ge(self.end_written, 32)


def attention(nc, tag, consts, x, wq, wk, wv, wo, gate_w, rows, count0):
    with ExitStack() as ctx:
        m = Memory(nc, ctx, tag)
        x_in = m.sb("x_in", [P, NT, D])
        x_res = m.sb("x_res", [P, NT, D])
        xn = m.sb("xn", [P, NT, D])
        xt_hi = m.sb("xt_hi", [P, DH, S], F32R)
        xt_lo = m.sb("xt_lo", [P, DH, S], F32R)
        w_hi = m.sb("w_hi", [P, 4, DH, D], F32R)
        w_lo = m.sb("w_lo", [P, 4, DH, D], F32R)
        qp = m.sb("qp", [P, 2, HEADS, HW], F32R)
        kp = m.sb("kp", [P, HEADS, HW], F32R)
        qc = m.sb("qc", [P, 2, D], F32R)
        kc = m.sb("kc", [P, D], F32R)
        qht = m.sb("qht", [P, 2, 2, P], F32R)
        km = m.sb("km", [P, 2, 8, WIN], F32R)
        kz = m.sb("kz", [P, HEADS, WIN], F32R)
        qpt = m.sb("qpt", [P, PAIRS, S], F32R)
        va = m.sb("va", [P, KT, HEADS, OW])
        pt = m.sb("pt", [P, 4, 512])
        ot = m.sb("ot", [P, GROUPS, S])
        w_raw = ot[:, 0:DH, :]
        rden = m.sb("rden", [P, 2, HEADS])
        o_sb = m.sb("o_sb", [P, 2, D])
        o_hi = m.sb("o_hi", [P, 2, DH, P], F32R)
        o_lo = m.sb("o_lo", [P, 2, DH, P], F32R)
        bank = m.ps("bank", [P, 8, 512])
        ln = LayerNorm(m, "ln", consts, NT)
        route = Route(nc, m, consts, rows, count0)
        row = route.row

        names = """w_in w_hi_done w_lo_done zero_done x_loaded res_loaded xt_t xt_hi_done xt_lo_done
            kv_p kv_act kp_lo km_t km_done kz_t kz_done q_p q_act q_lo qh_t qh_done s_p s_max qp_t qp_done
            st_p exp_done pv_p ot_done on_t norm_r norm_done of_t of_hi of_lo out_p"""
        g = {n: m.sem(n) for n in names.split()}
        held = m.sem("held")
        HALVES = 2
        XT = DH * HALVES
        pairs_of = [2 if t % 2 == 0 else 4 for t in range(NT)]
        SP_N = sum(pairs_of)
        UNITS = 3
        U = HEADS * UNITS

        with nc.Block() as block:

            @block.sync
            def _(sp):
                def load(i):
                    sp.wait_ge(ln.done, NT * i)
                    sp.sem_inc(held, 1)
                    sp.dma_start(x_in[:, :, :], x[bass.ds(i * S, S), :].rearrange("(t p) c -> p t c", p=P)).then_inc(g["x_loaded"], 16)

                def load_res(i):
                    sp.wait_ge(route.x_done, NT * i)
                    sp.sem_inc(held, 1)
                    sp.dma_start(x_res[:, :, :], x[bass.ds(i * S, S), :].rearrange("(t p) c -> p t c", p=P)).then_inc(g["res_loaded"], 16)

                for n, w in enumerate((wq, wk, wv, wo)):
                    sp.dma_start(w_raw[:, :, n * D:(n + 1) * D], w.rearrange("(c p) n -> p c n", p=P)).then_inc(g["w_in"], 16)
                route.load(sp, gate_w)
                load(0)
                with sp.Fori(0, B - 1) as i:
                    load_res(i)
                    load(i + 1)
                load_res(B - 1)
                route.sync_end(nc, sp, B)

            @block.gpsimd
            def _(pool):
                route.prepare_pool(nc, pool)
                ln.power(nc, pool, 0)
                with pool.Fori(0, B - 1) as i:
                    ln.power(nc, pool, i + 1)
                    route.ln.power(nc, pool, i)
                    route.pool(nc, pool, i)
                route.ln.power(nc, pool, B - 1)
                route.pool(nc, pool, B - 1)
                pool.wait_ge(route.sent, 16 * NT * B)

            @block.tensor
            def _(pe):
                mm = nc.tensor.matmul

                def xt(i):
                    for c in range(XT):
                        half, d = divmod(c, DH)
                        if c == 0:
                            pe.wait_ge(ln.done, NT * i + NT)
                            pe.wait_ge(route.step, 9 * i)
                        if c >= 2:
                            pe.wait_ge(g["xt_lo_done"], XT * i + c - 1)
                        for t in range(4):
                            last = nc.tensor.transpose(bank[:, 4 + c % 2, t * P:(t + 1) * P],
                                                       xn[:, 4 * half + t, d * P:(d + 1) * P], consts.ident[:, :])
                        last.then_inc(g["xt_t"], 1)

                def project(out, t, w):
                    terms = [(a, b, d) for d in range(DH) for a, b in ((xt_hi, w_lo), (xt_lo, w_hi), (xt_hi, w_hi))]
                    for n, (a, b, d) in enumerate(terms):
                        last = mm(out, a[:, d, t * P:(t + 1) * P], b[:, w, d, :], start=n == 0, stop=n == len(terms) - 1)
                    return last

                def keys(i):
                    for kt in range(KT):
                        if kt == 0:
                            pe.wait_ge(g["xt_lo_done"], XT * i + DH)
                        project(bank[:, 2 * kt, 0:D], kt, 1)
                        project(bank[:, 2 * kt + 1, 0:D], kt, 2).then_inc(g["kv_p"], 1)
                    for kt in range(KT):
                        pe.wait_ge(g["kp_lo"], KT * i + kt + 1)
                        if kt:
                            pe.wait_ge(g["km_done"], 2 * KT * i + 2)
                        for e in range(2):
                            last = nc.tensor.transpose(bank[:, 7, e * P:(e + 1) * P], f32(kc[:, e * P:(e + 1) * P]), consts.ident[:, :])
                        last.then_inc(g["km_t"], 1)
                        for h in range(2):
                            if kt + h:
                                pe.wait_ge(g["kz_done"], 4 * KT * i + 4 * kt + 2 * h)
                            for p in range(4):
                                last = nc.tensor.transpose(bank[:, 6, p * P:(p + 1) * P],
                                                           f32(kp[:, 2 * (4 * h + p):2 * (4 * h + p) + 2, :].rearrange("p a b -> p (a b)")), consts.ident[:, :])
                            last.then_inc(g["kz_t"], 1)

                def q_project(i, t):
                    if t == 0:
                        pe.wait_ge(g["xt_lo_done"], XT * i + XT)
                    else:
                        pe.wait_ge(g["q_lo"], NT * i + t)
                    project(bank[:, 5, 0:D], t, 0).then_inc(g["q_p"], 1)

                def q_heads(i, t):
                    pe.wait_ge(g["q_act"], 2 * (NT * i + t) + 2)
                    if t:
                        pe.wait_ge(g["qh_done"], NT * i + t)
                    for e in range(2):
                        last = nc.tensor.transpose(bank[:, 4, e * P:(e + 1) * P], f32(qc[:, t % 2, e * P:(e + 1) * P]), consts.ident[:, :])
                    last.then_inc(g["qh_t"], 1)

                def scores(i, t):
                    pe.wait_ge(g["qh_done"], NT * i + t + 1)
                    if t == 0:
                        pe.wait_ge(g["km_done"], 2 * KT * i + 2 * KT)
                    nk = P * (1 + t % 2)
                    per = 512 // nk
                    for j in range(pairs_of[t]):
                        n = sum(pairs_of[:t]) + j
                        if n >= 2:
                            pe.wait_ge(g["s_max"], SP_N * i + n - 1)
                        for b in range(2):
                            h0 = (2 * j + b) * per
                            out = bank[:, 2 * (n % 2) + b, :]
                            mm(out, consts.ident_bf[:, :], consts.mask_q[:, t % 2, :], start=True, stop=False)
                            last = mm(out.rearrange("p (h k) -> p h k", k=nk), qht[:, t % 2, h0 // 8, :],
                                      km[:, h0 // 8, h0 % 8:h0 % 8 + per, 0:nk], start=False, stop=True)
                        last.then_inc(g["s_p"], 1)

                def q_packed(i, t):
                    for h in range(2):
                        if h == 0:
                            pe.wait_ge(g["s_max"], SP_N * i + sum(pairs_of[:t + 1]))
                            pe.wait_ge(g["q_lo"], NT * i + t + 1)
                        if t == 0:
                            pe.wait_ge(g["kz_done"], 4 * KT * (i + 1))
                            pe.wait_ge(g["km_done"], 2 * KT * (i + 1))
                        else:
                            pe.wait_ge(g["qp_done"], 2 * (NT * i + t) + h - 1)
                        for p in range(4):
                            last = nc.tensor.transpose(bank[:, 6 + h, p * P:(p + 1) * P],
                                                       f32(qp[:, t % 2, 2 * (4 * h + p):2 * (4 * h + p) + 2, :].rearrange("p a b -> p (a b)")), consts.ident[:, :])
                        last.then_inc(g["qp_t"], 1)

                qpt_v = qpt[:, :, :].rearrange("p a (w e c) -> p a w e c", e=2, c=P)

                def unit(i, n):
                    h, u = divmod(n, UNITS)
                    kt, odd, masked = ((0, 0, True), (0, 1, False), (1, 1, True))[u]
                    if n == 0:
                        pe.wait_ge(g["qp_done"], 2 * NT * (i + 1))
                    if n >= 4:
                        pe.wait_ge(g["exp_done"], U * i + n - 3)
                    out = bank[:, n % 4, :]
                    if masked:
                        mm(out, consts.ident_bf[:, :], consts.mask_k[:, :], start=True, stop=False)
                    mm(out.rearrange("p (w c) -> p w c", c=P), kz[:, h, kt * P:(kt + 1) * P], qpt_v[:, h // 2, :, odd, :],
                       start=not masked, stop=True).then_inc(g["st_p"], 1)

                def values(i, n):
                    h, u = divmod(n, UNITS)
                    q, r = divmod(h, 4)
                    if r == 0 and u == 0 and q >= 2:
                        pe.wait_ge(g["ot_done"], 2 * GROUPS * i + 2 * q - 2)
                    pe.wait_ge(g["exp_done"], U * i + n + 1)
                    odd = 1 if u else 0
                    mm(bank[OW * r:OW * r + OW, 4 + 2 * (q % 2) + odd, :], va[:, 1 if u == 2 else 0, h, :], pt[:, n % 4, :],
                       start=u < 2, stop=u != 1).then_inc(g["pv_p"], 1)

                ot_v = ot[:, :, :].rearrange("p g (e w c) -> p g e w c", e=2, c=P)

                def heads_out(i, t):
                    if t == 0:
                        pe.wait_ge(g["ot_done"], 2 * GROUPS * (i + 1))
                    if t >= 2:
                        pe.wait_ge(g["norm_done"], NT * i + t - 1)
                    for q in range(GROUPS):
                        last = nc.tensor.transpose(bank[:, t % 2, q * P:(q + 1) * P], ot_v[:, q, t % 2, t // 2, :], consts.ident[:, :])
                    last.then_inc(g["on_t"], 1)

                def attn_t(i, t):
                    pe.wait_ge(g["norm_done"], NT * i + t + 1)
                    if t >= 2:
                        pe.wait_ge(g["of_lo"], NT * i + t - 1)
                    for d in range(DH):
                        last = nc.tensor.transpose(bank[:, 2 + t % 2, d * P:(d + 1) * P], o_sb[:, t % 2, d * P:(d + 1) * P], consts.ident[:, :])
                    last.then_inc(g["of_t"], 1)

                def out_project(i, t):
                    pe.wait_ge(g["of_lo"], NT * i + t + 1)
                    if t >= 2:
                        pe.wait_ge(route.x_done, NT * i + t - 1)
                    terms = [(a, b, d) for d in range(DH) for a, b in ((o_hi, w_lo), (o_lo, w_hi), (o_hi, w_hi))]
                    for n, (a, b, d) in enumerate(terms):
                        last = mm(bank[:, 4 + t % 2, 0:D], a[:, t % 2, d, :], b[:, 3, d, :], start=n == 0, stop=n == len(terms) - 1)
                    last.then_inc(g["out_p"], 1)

                pe.wait_ge(g["w_lo_done"], 1)
                pe.wait_ge(g["zero_done"], 5)
                with pe.Fori(0, B) as i:
                    xt(i)
                    keys(i)
                    q_project(i, 0)
                    q_heads(i, 0)
                    for t in range(NT):
                        if t + 1 < NT:
                            q_project(i, t + 1)
                        scores(i, t)
                        if t:
                            q_packed(i, t - 1)
                        if t + 1 < NT:
                            q_heads(i, t + 1)
                    q_packed(i, NT - 1)
                    for n in range(U + 2):
                        if n < U:
                            unit(i, n)
                        if n >= 2:
                            values(i, n - 2)
                    for t in range(NT + 2):
                        if t < NT:
                            heads_out(i, t)
                        if 1 <= t <= NT:
                            attn_t(i, t - 1)
                        if t >= 2:
                            out_project(i, t - 2)
                    route.tensor(nc, pe, i, bank[:, 6, 0:2 * NT].rearrange("p (a t) -> p a t", a=2))

            @block.scalar
            def _(act):
                copy = lambda o, a: nc.scalar.activation(o, a, ACT.Copy)

                def xt(i):
                    for c in range(XT):
                        half, d = divmod(c, DH)
                        act.wait_ge(g["xt_t"], XT * i + c + 1)
                        copy(xt_hi[:, d, half * 512:half * 512 + 512], bank[:, 4 + c % 2, :]).then_inc(g["xt_hi_done"], 1)

                def keys(i):
                    for kt in range(KT):
                        act.wait_ge(g["kv_p"], KT * i + kt + 1)
                        if kt:
                            act.wait_ge(g["kz_t"], 2 * KT * i + 2)
                        kb = bank[:, 2 * kt, 0:D].rearrange("p (h c) -> p h c", c=HD)
                        copy(kp[:, :, :].rearrange("p h (a c) -> p h a c", a=2)[:, :, :, 0:HD],
                             kb.unsqueeze(2).broadcast_to([P, HEADS, 2, HD]))
                        copy(kc[:, :], bank[:, 2 * kt, 0:D])
                        copy(va[:, kt, :, 0:HD], bank[:, 2 * kt + 1, 0:D].rearrange("p (h c) -> p h c", c=HD)).then_inc(g["kv_act"], 1)
                        for h in range(2):
                            act.wait_ge(g["kz_t"], 2 * KT * i + 2 * kt + h + 1)
                            for r in range(2):
                                copy(kz[HW * r:HW * r + HW, 8 * h + r:8 * h + r + 7:2, kt * P:(kt + 1) * P],
                                     bank[HW * r:HW * r + HW, 6, :].rearrange("p (a k) -> p a k", k=P)).then_inc(g["kz_done"], 1)

                def q_copy(i, t):
                    act.wait_ge(g["q_p"], NT * i + t + 1)
                    if t >= 2:
                        act.wait_ge(g["qp_t"], 2 * (NT * i + t) - 2)
                    src = bank[:, 5, 0:D].rearrange("p (h c) -> p h c", c=HD)
                    copy(qp[:, t % 2, :, 0:2 * HD].rearrange("p h (a c) -> p h a c", a=2),
                         src.unsqueeze(2).broadcast_to([P, HEADS, 2, HD])).then_inc(g["q_act"], 1)
                    copy(qc[:, t % 2, :], bank[:, 5, 0:D]).then_inc(g["q_act"], 1)

                def q_heads(i, t):
                    act.wait_ge(g["qh_t"], NT * i + t + 1)
                    if t >= 2:
                        act.wait_ge(g["s_p"], SP_N * i + sum(pairs_of[:t - 1]))
                    copy(qht[:, t % 2, :, :], bank[:, 4, 0:2 * P].rearrange("p (e c) -> p e c", c=P)).then_inc(g["qh_done"], 1)

                def q_packed(i, t):
                    for h in range(2):
                        act.wait_ge(g["qp_t"], 2 * (NT * i + t) + h + 1)
                        copy(qpt[:, 4 * h:4 * h + 4, t * P:(t + 1) * P], bank[:, 6 + h, :].rearrange("p (a k) -> p a k", k=P)).then_inc(g["qp_done"], 1)

                act.wait_ge(g["w_lo_done"], 1)
                with act.Fori(0, B) as i:
                    xt(i)
                    keys(i)
                    q_copy(i, 0)
                    q_heads(i, 0)
                    for t in range(NT):
                        if t + 1 < NT:
                            q_copy(i, t + 1)
                            q_heads(i, t + 1)
                        if t:
                            q_packed(i, t - 1)
                    q_packed(i, NT - 1)
                    for n in range(U):
                        act.wait_ge(g["st_p"], U * i + n + 1)
                        if n >= 4:
                            act.wait_ge(g["pv_p"], U * i + n - 3)
                        nc.scalar.activation(pt[:, n % 4, :], bank[:, n % 4, :], ACT.Exp, scale=HD ** -0.5).then_inc(g["exp_done"], 1)
                    for t in range(NT):
                        act.wait_ge(g["of_t"], NT * i + t + 1)
                        if t >= 2:
                            act.wait_ge(g["out_p"], NT * i + t - 1)
                        copy(o_hi[:, t % 2, :, :], bank[:, 2 + t % 2, 0:D].rearrange("p (d c) -> p d c", c=P)).then_inc(g["of_hi"], 1)

            @block.vector
            def _(dve):
                tt = nc.vector.tensor_tensor

                def norm_in(i):
                    dve.wait_ge(g["x_loaded"], 16 * i + 16)
                    ln.stats(nc, dve, i, x_in)
                    dve.wait_ge(g["xt_t"], XT * i)
                    ln.apply(nc, dve, i, x_in, xn)

                dve.wait_ge(g["w_in"], 64)
                raw = w_raw.rearrange("p d (w n) -> p w d n", n=D)
                for w in range(4):
                    nc.vector.tensor_copy(w_hi[:, w, :, :], raw[:, w]).then_inc(g["w_hi_done"], 1)
                dve.wait_ge(g["w_hi_done"], 4)
                for w in range(4):
                    last = tt(w_lo[:, w, :, :], raw[:, w], f32(w_hi[:, w, :, :]), ALU.subtract)
                last.then_inc(g["w_lo_done"], 1)
                nc.vector.memset(f32(qp[:, :, :, :]), 0.0).then_inc(g["zero_done"], 1)
                nc.vector.memset(f32(kp[:, :, :]), 0.0).then_inc(g["zero_done"], 1)
                nc.vector.memset(f32(kz[:, :, :]), 0.0).then_inc(g["zero_done"], 1)
                nc.vector.memset(va[:, :, :, :], 0.0).then_inc(g["zero_done"], 1)
                dve.wait_ge(g["zero_done"], 4)
                nc.vector.memset(f32(kp[:, :, 3 * HD:3 * HD + 1]), 1.0)
                nc.vector.memset(va[:, :, :, HD:HD + 1], 1.0).then_inc(g["zero_done"], 1)
                route.prepare(nc, dve)
                norm_in(0)

                def sequence(i, more):
                    for c in range(XT):
                        half, d = divmod(c, DH)
                        dve.wait_ge(g["xt_hi_done"], XT * i + c + 1)
                        tt(xt_lo[:, d, half * 512:half * 512 + 512], bank[:, 4 + c % 2, :],
                           f32(xt_hi[:, d, half * 512:half * 512 + 512]), ALU.subtract).then_inc(g["xt_lo_done"], 1)
                    for kt in range(KT):
                        dve.wait_ge(g["kv_act"], KT * i + kt + 1)
                        tt(kp[:, :, HD:2 * HD], bank[:, 2 * kt, 0:D].rearrange("p (h c) -> p h c", c=HD),
                           f32(kp[:, :, 0:HD]), ALU.subtract).then_inc(g["kp_lo"], 1)
                        dve.wait_ge(g["km_t"], KT * i + kt + 1)
                        for e in range(2):
                            tt(km[:, e, :, kt * P:(kt + 1) * P],
                               bank[:, 7, e * P:(e + 1) * P].unsqueeze(1).broadcast_to([P, 8, P]),
                               consts.head_rows[:, :].unsqueeze(2).broadcast_to([P, 8, P]), ALU.mult).then_inc(g["km_done"], 1)

                    def q_low(t):
                        dve.wait_ge(g["q_act"], 2 * (NT * i + t) + 2)
                        tt(qp[:, t % 2, :, 2 * HD:3 * HD], bank[:, 5, 0:D].rearrange("p (h c) -> p h c", c=HD),
                           f32(qp[:, t % 2, :, 0:HD]), ALU.subtract).then_inc(g["q_lo"], 1)

                    q_low(0)
                    for t in range(NT):
                        nk = P * (1 + t % 2)
                        hp = 1024 // nk
                        for j in range(pairs_of[t]):
                            n = sum(pairs_of[:t]) + j
                            dve.wait_ge(g["s_p"], SP_N * i + n + 1)
                            if t >= 2 and j == 0:
                                dve.wait_ge(g["qp_t"], 2 * (NT * i + t) - 2)
                            nc.vector.tensor_reduce(
                                qp[:, t % 2, j * hp:(j + 1) * hp, 3 * HD:3 * HD + 1].rearrange("p h a -> p (h a)"),
                                bank[:, 2 * (n % 2):2 * (n % 2) + 2, :].rearrange("p b (h k) -> p (b h) k", k=nk),
                                AX.X, ALU.max, negate=True).then_inc(g["s_max"], 1)
                        if t + 1 < NT:
                            q_low(t + 1)
                    if more:
                        norm_in(i + 1)
                    for q in range(GROUPS):
                        for e in range(2):
                            dve.wait_ge(g["pv_p"], U * i + 4 * UNITS * (q + 1))
                            nc.vector.tensor_copy(ot[:, q, e * 512:e * 512 + 512], bank[:, 4 + 2 * (q % 2) + e, :]).then_inc(g["ot_done"], 1)

                    def norm_out(t):
                        dve.wait_ge(g["on_t"], NT * i + t + 1)
                        v = bank[:, t % 2, :].rearrange("p (h c) -> p h c", c=OW)
                        if t >= 2:
                            dve.wait_ge(g["norm_done"], NT * i + t - 1)
                        nc.vector.reciprocal(rden[:, t % 2, :].unsqueeze(2), v[:, :, HD:HD + 1]).then_inc(g["norm_r"], 1)
                        dve.wait_ge(g["norm_r"], NT * i + t + 1)
                        if t >= 2:
                            dve.wait_ge(g["of_t"], NT * i + t - 1)
                        tt(o_sb[:, t % 2, :].rearrange("p (h c) -> p h c", c=HD), v[:, :, 0:HD],
                           rden[:, t % 2, :].unsqueeze(2).broadcast_to([P, HEADS, HD]), ALU.mult).then_inc(g["norm_done"], 1)

                    def attn_low(t):
                        dve.wait_ge(g["of_hi"], NT * i + t + 1)
                        if t >= 2:
                            dve.wait_ge(g["out_p"], NT * i + t - 1)
                        tt(o_lo[:, t % 2, :, :], bank[:, 2 + t % 2, 0:D].rearrange("p (d c) -> p d c", c=P),
                           f32(o_hi[:, t % 2, :, :]), ALU.subtract).then_inc(g["of_lo"], 1)

                    def new_x(t):
                        dve.wait_ge(g["out_p"], NT * i + t + 1)
                        if t == 0:
                            dve.wait_ge(g["res_loaded"], 16 * i + 16)
                            dve.wait_ge(route.sent, 16 * NT * i)
                        tt(row[:, t, 0:D], bank[:, 4 + t % 2, 0:D], x_res[:, t, :], ALU.add).then_inc(route.x_done, 1)

                    for t in range(NT + 2):
                        if t < NT:
                            norm_out(t)
                        if 1 <= t <= NT:
                            attn_low(t - 1)
                        if t >= 2:
                            new_x(t - 2)
                    ps = bank[:, 6, 0:2 * NT].rearrange("p (a t) -> p a t", a=2)
                    route.vector_stats(nc, dve, i)
                    route.vector_choose(nc, dve, i)
                    route.vector_slots(nc, dve, i, ps)

                with dve.Fori(0, B - 1) as i:
                    sequence(i, True)
                sequence(B - 1, False)
                route.vector_end(nc, dve, B)


ORDER = 2
FREQS = 3
ENC = 2 * FREQS + 1
FO = 64
BLK = 32
NBLK = S // BLK
LAGS = S // P
PADB = 3
BW = NBLK + 4
SEQW = B * BW
FW = (P + BLK) * LAGS
CH = 4
CHUNKS = BLK // CH


def filters(nc, tag, times, phases, freqs, w1, b1, w2, b2, w3, b3, decay, arranged):
    TWO_PI = 6.283185
    ROUND = 1.5 * 2 ** 23
    with ExitStack() as ctx:
        m = Memory(nc, ctx, tag)
        t_row = m.sb("t_row", [P, S])
        ph = m.sb("ph", [ENC, 3])
        fr = m.sb("fr", [ENC, ORDER])
        turn = m.sb("turn", [ENC, S])
        near = m.sb("near", [ENC, S])
        enc = m.sb("enc", [ENC, S])
        w1_sb = m.sb("w1", [ENC, ORDER, FO])
        w2_sb = m.sb("w2", [FO, ORDER, FO])
        w3_sb = m.sb("w3", [FO, ORDER, D])
        b12 = m.sb("b12", [FO, 2, ORDER])
        b3_sb = m.sb("b3", [P, ORDER, DH])
        dec = m.sb("dec", [P, ORDER, DH])
        ndec = m.sb("ndec", [P, ORDER, DH])
        h1 = m.sb("h1", [FO, S])
        h2 = m.sb("h2", [FO, S])
        win = m.sb("win", [P, DH, S])
        flt = m.sb("flt", [P, DH, S + BLK])
        arr = m.sb("arr", [P, DH, P + BLK, LAGS])
        h_ps = m.ps("h_ps", [P, 2, 512])
        f_ps = m.ps("f_ps", [P, DH, 2, 512])
        loaded, fr_set, turned, enc_done, l1_p, l1_done, l2_p, l2_done, l3_p, win_done, flt_done, zeroed, arr_done, \
            stored, ndec_done = (m.sem(n) for n in ("loaded fr_set turned enc_done l1_p l1_done l2_p l2_done l3_p win_done "
                                                    "flt_done zeroed arr_done stored ndec_done").split())
        LOADS = 13

        with nc.Block() as block:

            @block.sync
            def _(sp):
                sp.dma_start(t_row[:, :], times.broadcast_to([P, S])).then_inc(loaded, 16)
                sp.dma_start(ph[:, :], phases).then_inc(loaded, 16)
                for k in range(2):
                    sp.dma_start(fr[FREQS * k:FREQS * k + FREQS, :], freqs).then_inc(loaded, 16)
                sp.dma_start(w1_sb[:, :, :], w1.rearrange("o k n -> k o n")).then_inc(loaded, 16)
                sp.dma_start(w2_sb[:, :, :], w2.rearrange("o k n -> k o n")).then_inc(loaded, 16)
                sp.dma_start(w3_sb[:, :, :], w3.rearrange("o k n -> k o n")).then_inc(loaded, 16)
                sp.dma_start(b12[:, 0, :], b1).then_inc(loaded, 16)
                sp.dma_start(b12[:, 1, :], b2).then_inc(loaded, 16)
                sp.dma_start(b3_sb[:, :, :], b3).then_inc(loaded, 16)
                sp.dma_start(dec[:, :, :], decay).then_inc(loaded, 16)
                sp.dma_start(fr[2 * FREQS:ENC, :], freqs[0:1, :]).then_inc(loaded, 16)
                sp.dma_start(win[:, 0, :], times.broadcast_to([P, S])).then_inc(loaded, 16)
                for o in range(ORDER):
                    for d in range(DH):
                        sp.wait_ge(arr_done, DH * o + d + 1)
                        for q in range(4):
                            sp.dma_start(arranged[o, d, :, q, :, :], arr[BLK * q:BLK * q + BLK, d, :, :].rearrange("p a b -> p (a b)")).then_inc(stored, 16)
                sp.wait_ge(stored, 64 * ORDER * DH)

            @block.vector
            def _(dve):
                dve.wait_ge(loaded, 16 * LOADS)
                nc.vector.tensor_scalar(fr[:, :], fr[:, :], ph[:, 2:3], None, ALU.mult).then_inc(fr_set, 1)
                dve.wait_ge(fr_set, 1)
                nc.vector.tensor_scalar(ndec[:, :, :], dec[:, :, :], -1.0, None, ALU.mult).then_inc(ndec_done, 1)
                nc.vector.memset(flt[:, :, S:S + BLK], 0.0).then_inc(zeroed, 1)
                dve.wait_ge(ndec_done, 1)
                nc.vector.tensor_tensor(ndec[:, :, :], ndec[:, :, :], dec[:, :, :], ALU.min).then_inc(ndec_done, 1)
                dve.wait_ge(ndec_done, 2)
                nc.vector.tensor_scalar(ndec[:, :, :], ndec[:, :, :], float(S), None, ALU.mult).then_inc(ndec_done, 1)
                for o in range(ORDER):
                    n = 5 * o
                    if o:
                        dve.wait_ge(l1_done, 2 * o)
                    nc.vector.tensor_scalar(turn[:, :], t_row[0:ENC, :], fr[:, o:o + 1], ph[:, 0:1], ALU.mult, ALU.add).then_inc(turned, 1)
                    dve.wait_ge(turned, n + 1)
                    nc.vector.tensor_scalar(near[:, :], turn[:, :], ROUND, None, ALU.add).then_inc(turned, 1)
                    dve.wait_ge(turned, n + 2)
                    nc.vector.tensor_scalar(near[:, :], near[:, :], -ROUND, None, ALU.add).then_inc(turned, 1)
                    dve.wait_ge(turned, n + 3)
                    nc.vector.tensor_tensor(turn[:, :], turn[:, :], near[:, :], ALU.subtract).then_inc(turned, 1)
                    dve.wait_ge(enc_done, 2 * o + 1)
                    dve.wait_ge(turned, n + 4)
                    nc.vector.tensor_scalar(turn[:, :], t_row[0:ENC, :], ph[:, 1:2], None, ALU.mult).then_inc(turned, 1)
                    dve.wait_ge(turned, n + 5)
                    nc.vector.tensor_tensor(enc[:, :], enc[:, :], turn[:, :], ALU.add).then_inc(enc_done, 1)
                    for d in range(DH):
                        dve.wait_ge(l3_p, DH * o + d + 1)
                        dve.wait_ge(win_done, DH * o + d + 1)
                        if o:
                            dve.wait_ge(arr_done, DH * (o - 1) + d + 1)
                        nc.vector.scalar_tensor_tensor(flt[:, d, 0:S], f_ps[:, d, :, :].rearrange("p a b -> p (a b)"),
                                                       b3_sb[:, o, d:d + 1], win[:, d, :], ALU.add, ALU.mult).then_inc(flt_done, 1)
                        dve.wait_ge(flt_done, DH * o + d + 1)
                        dve.wait_ge(zeroed, 1)
                        if o:
                            dve.wait_ge(stored, 64 * DH)
                        for k in range(LAGS):
                            last = nc.vector.tensor_copy(arr[:, d, :, k:k + 1].rearrange("p w a -> p (w a)"), flt[:, d, P * k:P * k + P + BLK])
                        last.then_inc(arr_done, 1)

            @block.scalar
            def _(act):
                act.wait_ge(loaded, 16 * LOADS)
                for o in range(ORDER):
                    act.wait_ge(turned, 5 * o + 4)
                    nc.scalar.activation(enc[:, :], turn[:, :], ACT.Sin, scale=TWO_PI).then_inc(enc_done, 1)
                    for h in range(2):
                        act.wait_ge(l1_p, 2 * o + h + 1)
                        nc.scalar.activation(h1[:, h * 512:h * 512 + 512], h_ps[0:FO, h, :], ACT.Gelu, bias=b12[:, 0, o:o + 1]).then_inc(l1_done, 1)
                    for h in range(2):
                        act.wait_ge(l2_p, 2 * o + h + 1)
                        nc.scalar.activation(h2[:, h * 512:h * 512 + 512], h_ps[0:FO, h, :], ACT.Gelu, bias=b12[:, 1, o:o + 1]).then_inc(l2_done, 1)
                    act.wait_ge(ndec_done, 3)
                    for d in range(DH):
                        if o:
                            act.wait_ge(flt_done, DH * (o - 1) + d + 1)
                        nc.scalar.activation(win[:, d, :], t_row[:, :], ACT.Exp, scale=ndec[:, o, d:d + 1]).then_inc(win_done, 1)

            @block.tensor
            def _(pe):
                mm = nc.tensor.matmul
                for o in range(ORDER):
                    pe.wait_ge(enc_done, 2 * o + 2)
                    if o:
                        pe.wait_ge(l2_done, 2 * o)
                    for h in range(2):
                        mm(h_ps[0:FO, h, :], w1_sb[:, o, :], enc[:, h * 512:h * 512 + 512], start=True, stop=True).then_inc(l1_p, 1)
                    for h in range(2):
                        pe.wait_ge(l1_done, 2 * o + 2)
                        mm(h_ps[0:FO, h, :], w2_sb[:, o, :], h1[:, h * 512:h * 512 + 512], start=True, stop=True).then_inc(l2_p, 1)
                    for d in range(DH):
                        pe.wait_ge(l2_done, 2 * o + 2)
                        if o:
                            pe.wait_ge(flt_done, DH * (o - 1) + d + 1)
                        for h in range(2):
                            last = mm(f_ps[:, d, h, :], w3_sb[:, o, d * P:(d + 1) * P], h2[:, h * 512:h * 512 + 512], start=True, stop=True)
                        last.then_inc(l3_p, 1)


def projections(nc, tag, consts, x, in_w, in_b, conv_w, conv_b, gate_w, gate_b, v_blocks, gates):
    MB = (ORDER + 1) * DH
    with ExitStack() as ctx:
        m = Memory(nc, ctx, tag)
        x_in = m.sb("x_in", [P, NT, D])
        xn = m.sb("xn", [P, NT, D])
        xt_hi = m.sb("xt_hi", [P, DH, S], F32R)
        xt_lo = m.sb("xt_lo", [P, DH, S], F32R)
        iw_hi = m.sb("iw_hi", [P, DH, 3 * D], F32R)
        iw_lo = m.sb("iw_lo", [P, DH, 3 * D], F32R)
        gw_hi = m.sb("gw_hi", [P, ORDER, DH, D], F32R)
        gw_lo = m.sb("gw_lo", [P, ORDER, DH, D], F32R)
        cols = m.sb("cols", [P, MB + ORDER * DH * 5])
        in_bc = cols[:, 0:MB]
        cw = cols[:, MB:MB + 12].rearrange("p (o d k) -> p o d k", o=ORDER, d=DH)
        cb = cols[:, MB + 12:MB + 16].rearrange("p (o d) -> p o d", o=ORDER)
        gb = cols[:, MB + 16:MB + 20].rearrange("p (o d) -> p o d", o=ORDER)
        vb = m.sb("vb", [P, DH, BLK, B, BW])
        vt = m.sb("vt", [P, 2, S])
        vs = m.sb("vs", [P, DH, NBLK, BLK])
        u = m.sb("u", [P, 2, S + 2])
        tap = m.sb("tap", [P, 2, S])
        xc = m.sb("xc", [P, 2, S])
        xc_hi = m.sb("xc_hi", [P, DH, S], F32R)
        xc_lo = m.sb("xc_lo", [P, DH, S], F32R)
        sg = tap
        w_raw = vt[:, :, :].rearrange("p d s -> p (d s)")
        w_raw2 = tap[:, :, :].rearrange("p d s -> p (d s)")
        bank = m.ps("bank", [P, 8, 512])
        ln = LayerNorm(m, "ln", consts, NT)
        names = """w_in c_in w_hi w_lo zeroed x_loaded xt_t xt_hi_done xt_lo_done v_p v_act v_blk u_p u_act tap0 tap1
            xc_done xc_hi_done xc_lo_done g_p sg_done g_done v_put v_stored"""
        g = {n: m.sem(n) for n in names.split()}
        held = m.sem("held")
        g_stored = [m.sem(f"g_stored{d}") for d in range(DH)]
        XT = 2 * DH

        with nc.Block() as block:

            @block.sync
            def _(sp):
                sp.dma_start(w_raw[:, 0:DH * 3 * D].rearrange("p (c n) -> p c n", c=DH),
                             in_w.rearrange("(c p) n -> p c n", p=P)).then_inc(g["w_in"], 16)
                for o in range(ORDER):
                    sp.dma_start(w_raw2[:, o * DH * D:(o + 1) * DH * D].rearrange("p (c n) -> p c n", c=DH),
                                 gate_w[o].rearrange("(c p) n -> p c n", p=P)).then_inc(g["w_in"], 16)
                for dst, src in ((in_bc, in_b), (cw, conv_w), (cb, conv_b), (gb, gate_b)):
                    sp.dma_start(dst, src).then_inc(g["c_in"], 16)

                def load(i):
                    sp.wait_ge(ln.done, NT * i)
                    sp.sem_inc(held, 1)
                    sp.dma_start(x_in[:, :, :], x[bass.ds(i * S, S), :].rearrange("(t p) c -> p t c", p=P)).then_inc(g["x_loaded"], 16)

                def store(i):
                    for n in range(ORDER * DH):
                        o, d = divmod(n, DH)
                        sp.wait_ge(g["g_done"], ORDER * DH * i + n + 1)
                        sp.sem_inc(held, 1)
                        sp.dma_start(gates[o, d, :, bass.ds(i * S, S)], tap[:, d, :]).then_inc(g_stored[d], 16)

                load(0)
                with sp.Fori(0, B - 1) as i:
                    load(i + 1)
                    store(i)
                store(B - 1)
                sp.wait_ge(g["v_put"], DH * B)
                for d in range(DH):
                    sp.dma_start(v_blocks[d], vb[:, d].rearrange("p c b k -> p (c b k)")).then_inc(g["v_stored"], 16)
                sp.wait_ge(g["v_stored"], 16 * DH)
                for d in range(DH):
                    sp.wait_ge(g_stored[d], 16 * ORDER * B)

            @block.gpsimd
            def _(pool):
                every = vb[:, :, :, :, :].rearrange("p a b c k -> p (a b c) k")
                pool.memset(every[:, :, 0:PADB], 0.0)
                pool.memset(every[:, :, PADB + NBLK:BW], 0.0).then_inc(g["zeroed"], 1)
                ln.power(nc, pool, 0)
                with pool.Fori(0, B - 1) as i:
                    ln.power(nc, pool, i + 1)

            @block.tensor
            def _(pe):
                mm = nc.tensor.matmul

                def xt(i):
                    for c in range(XT):
                        half, d = divmod(c, DH)
                        if c == 0:
                            pe.wait_ge(ln.done, NT * i + NT)
                        pe.wait_ge(g["xt_lo_done"], XT * i + c + 1)
                        for t in range(4):
                            last = nc.tensor.transpose(bank[:, 6 + c % 2, t * P:(t + 1) * P],
                                                       xn[:, 4 * half + t, d * P:(d + 1) * P], consts.ident[:, :])
                        last.then_inc(g["xt_t"], 1)

                def product(out, hi, lo, w_h, w_l, h, col):
                    terms = [(a, b, d) for d in range(DH) for a, b in ((w_h, lo), (w_l, hi), (w_h, hi))]
                    for n, (a, b, d) in enumerate(terms):
                        last = mm(out, a[:, d, col:col + P], b[:, d, h * 512:h * 512 + 512], start=n == 0, stop=n == len(terms) - 1)
                    return last

                pe.sem_inc(g["g_p"], 1)
                pe.wait_ge(g["w_lo"], 3)
                with pe.Fori(0, B) as i:
                    xt(i)
                    for d in range(DH):
                        pe.wait_ge(g["xt_lo_done"], XT * i + XT + 2)
                        if d == 0:
                            pe.wait_ge(g["sg_done"], 4 * i)
                        for h in range(2):
                            last = product(bank[:, 2 * d + h, :], xt_hi, xt_lo, iw_hi, iw_lo, h, d * P)
                        last.then_inc(g["v_p"], 1)
                    for o in range(ORDER):
                        for d in range(DH):
                            k = 2 * o + d
                            if d == 1:
                                pe.wait_ge(g["v_act"], DH * i + 1)
                            if k:
                                pe.wait_ge(g["u_act"], 4 * i + k)
                            if o and d == 1:
                                pe.wait_ge(g["sg_done"], 4 * i + 2)
                            for h in range(2):
                                last = product(bank[:, (4, 0)[d] + h, :], xt_hi, xt_lo, iw_hi, iw_lo, h, (1 + o) * D + d * P)
                            last.then_inc(g["u_p"], 1)
                        for d in range(DH):
                            if d == 0:
                                pe.wait_ge(g["xc_lo_done"], 4 * i + 2 * o + 2)
                                pe.wait_ge(g["v_act"], DH * i + 2)
                                if o:
                                    pe.wait_ge(g["sg_done"], 4 * i + 2)
                            else:
                                pe.wait_ge(g["u_act"], 4 * i + 2 * o + 2)
                            for h in range(2):
                                last = product(bank[:, (2, 0)[d] + h, :], xc_hi, xc_lo, gw_hi[:, o], gw_lo[:, o], h, d * P)
                            last.then_inc(g["g_p"], 1)

            @block.scalar
            def _(act):
                act.wait_ge(g["c_in"], 64)
                act.wait_ge(g["w_lo"], 3)
                act.wait_ge(g["zeroed"], 1)
                with act.Fori(0, B) as i:
                    for c in range(XT):
                        half, d = divmod(c, DH)
                        act.wait_ge(g["xt_t"], XT * i + c + 1)
                        nc.scalar.activation(xt_hi[:, d, half * 512:half * 512 + 512], bank[:, 6 + c % 2, :], ACT.Copy).then_inc(g["xt_hi_done"], 1)
                    for d in range(DH):
                        act.wait_ge(g["v_p"], DH * i + d + 1)
                        act.wait_ge(g["v_blk"], DH * i)
                        nc.scalar.activation(vt[:, d, :], bank[:, 2 * d:2 * d + 2, :].rearrange("p a b -> p (a b)"), ACT.Identity,
                                             bias=in_bc[:, d:d + 1]).then_inc(g["v_act"], 1)
                    for o in range(ORDER):
                        for d in range(DH):
                            k = 2 * o + d
                            act.wait_ge(g["u_p"], 4 * i + k + 1)
                            if o:
                                act.wait_ge(g["xc_done"], 4 * i + k - 1)
                            else:
                                act.wait_ge(g["xc_done"], 4 * i)
                            nc.scalar.activation(u[:, d, 1:S + 1], bank[:, (4, 0)[d]:(4, 0)[d] + 2, :].rearrange("p a b -> p (a b)"), ACT.Identity,
                                                 bias=in_bc[:, DH + k:DH + k + 1]).then_inc(g["u_act"], 1)
                            act.wait_ge(g["u_act"], 4 * i + k + 1)
                            act.wait_ge(g_stored[d], 32 * i + 16 * o)
                            nc.scalar.activation(tap[:, d, :], u[:, d, 0:S], ACT.Identity, bias=cb[:, o, d:d + 1],
                                                 scale=cw[:, o, d, 0:1]).then_inc(g["tap0"], 1)
                        for d in range(DH):
                            act.wait_ge(g["xc_done"], 4 * i + 2 * o + d + 1)
                            act.wait_ge(g["g_p"], 4 * i + 2 * o + 1)
                            nc.scalar.activation(xc_hi[:, d, :], xc[:, d, :], ACT.Copy).then_inc(g["xc_hi_done"], 1)
                        for d in range(DH):
                            act.wait_ge(g["g_p"], 4 * i + 2 * o + d + 2)
                            nc.scalar.activation(sg[:, d, :], bank[:, (2, 0)[d]:(2, 0)[d] + 2, :].rearrange("p a b -> p (a b)"), ACT.Sigmoid,
                                                 bias=gb[:, o, d:d + 1]).then_inc(g["sg_done"], 1)
                    for d in range(DH):
                        act.wait_ge(g["v_blk"], DH * i + d + 1)
                        nc.scalar.activation(vb[:, d, :, bass.ds(i, 1), PADB:PADB + NBLK].rearrange("p c b k -> p c (b k)"),
                                             vs[:, d, :, :].rearrange("p k c -> p c k"), ACT.Copy).then_inc(g["v_put"], 1)

            @block.vector
            def _(dve):
                tt = nc.vector.tensor_tensor
                stt = nc.vector.scalar_tensor_tensor
                dve.sem_inc(g["xt_lo_done"], 2)

                def norm_in(i):
                    dve.wait_ge(g["x_loaded"], 16 * i + 16)
                    ln.stats(nc, dve, i, x_in)
                    dve.wait_ge(g["xt_t"], XT * i)
                    ln.apply(nc, dve, i, x_in, xn)

                dve.wait_ge(g["w_in"], 48)
                raw_i = w_raw[:, 0:DH * 3 * D].rearrange("p (c n) -> p c n", c=DH)
                raw_g = w_raw2[:, 0:ORDER * DH * D].rearrange("p (o c n) -> p o c n", o=ORDER, c=DH)
                nc.vector.tensor_copy(iw_hi[:, :, :], raw_i).then_inc(g["w_hi"], 1)
                for o in range(ORDER):
                    nc.vector.tensor_copy(gw_hi[:, o], raw_g[:, o]).then_inc(g["w_hi"], 1)
                dve.wait_ge(g["w_hi"], 3)
                tt(iw_lo[:, :, :], raw_i, f32(iw_hi[:, :, :]), ALU.subtract).then_inc(g["w_lo"], 1)
                for o in range(ORDER):
                    tt(gw_lo[:, o], raw_g[:, o], f32(gw_hi[:, o]), ALU.subtract).then_inc(g["w_lo"], 1)
                nc.vector.memset(u[:, :, :], 0.0).then_inc(g["w_hi"], 1)
                norm_in(0)
                dve.wait_ge(g["w_hi"], 4)
                dve.wait_ge(g["w_lo"], 3)
                dve.wait_ge(g["zeroed"], 1)

                def sequence(i, more):
                    for c in range(XT):
                        half, d = divmod(c, DH)
                        dve.wait_ge(g["xt_hi_done"], XT * i + c + 1)
                        tt(xt_lo[:, d, half * 512:half * 512 + 512], bank[:, 6 + c % 2, :],
                           f32(xt_hi[:, d, half * 512:half * 512 + 512]), ALU.subtract).then_inc(g["xt_lo_done"], 1)
                    for d in range(DH):
                        dve.wait_ge(g["v_act"], DH * i + d + 1)
                        dve.wait_ge(g["v_put"], DH * i)
                        nc.vector.transpose(vs[:, d, :, :], vt[:, d, :].rearrange("p (k s) -> p k s", s=BLK)).then_inc(g["v_blk"], 1)
                    for o in range(ORDER):
                        for d in range(DH):
                            k = 4 * i + 2 * o + d
                            dve.wait_ge(g["tap0"], k + 1)
                            stt(xc[:, d, :], u[:, d, 1:S + 1], cw[:, o, d, 1:2], tap[:, d, :], ALU.mult, ALU.add).then_inc(g["tap1"], 1)
                            dve.wait_ge(g["tap1"], k + 1)
                            stt(xc[:, d, :], u[:, d, 2:S + 2], cw[:, o, d, 2:3], xc[:, d, :], ALU.mult, ALU.add).then_inc(g["xc_done"], 1)
                        for d in range(DH):
                            k = 4 * i + 2 * o + d
                            dve.wait_ge(g["xc_hi_done"], k + 1)
                            tt(xc_lo[:, d, :], xc[:, d, :], f32(xc_hi[:, d, :]), ALU.subtract).then_inc(g["xc_lo_done"], 1)
                        if o and more:
                            norm_in(i + 1)
                        for d in range(DH):
                            k = 4 * i + 2 * o + d
                            dve.wait_ge(g["sg_done"], k + 1)
                            tt(sg[:, d, :], sg[:, d, :], xc[:, d, :], ALU.mult).then_inc(g["g_done"], 1)

                with dve.Fori(0, B - 1) as i:
                    sequence(i, True)
                sequence(B - 1, False)


def convolutions(nc, tag, arranged, v_blocks, gates, v_mid, v_out):
    ROUNDS = ORDER * DH
    PER = CHUNKS
    with ExitStack() as ctx:
        m = Memory(nc, ctx, tag)
        tp = m.sb("tp", [P, 2, 4, CH, BLK * LAGS])
        vi = m.sb("vi", [P, 2, 4, CH * SEQW])
        yc = m.sb("yc", [P, BLK, B * NBLK])
        yt = m.sb("yt", [P, 2, S])
        gt = m.sb("gt", [P, 2, S])
        vn = m.sb("vn", [P, 2, S])
        vb = m.sb("vb", [P, BLK, B, BW])
        y_ps = m.ps("y_ps", [P, 4, 2, B * NBLK])
        t_loaded = [m.sem(f"t_loaded{n}") for n in range(2)]
        v_loaded = [m.sem(f"v_loaded{n}") for n in range(2)]
        y_p, y_act, yt_done, vn_done, vb_done, mid_stored, zeroed, held = (
            m.sem(n) for n in "y_p y_act yt_done vn_done vb_done mid_stored zeroed held".split())
        g_loaded = [m.sem(f"g_loaded{n}") for n in range(2)]
        out_stored = [m.sem(f"out_stored{n}") for n in range(2)]

        with nc.Block() as block:

            @block.sync
            def _(sp):
                def chunk(r, c, k):
                    o, d = divmod(r, DH)
                    n = r * PER + c
                    if isinstance(c, int) and n < 2:
                        pass
                    else:
                        sp.wait_ge(y_p, n - 1)
                        sp.sem_inc(held, 1)
                    src = bass.AP(arranged.tensor, r * P * FW + c * (4 * CH * FW),
                                  [[LAGS, P], [FW, 4 * CH], [1, BLK * LAGS]])
                    sp.dma_start(tp[:, k].rearrange("p q c n -> p (q c) n"), src).then_inc(t_loaded[k], 16)
                    vsrc = v_blocks if o == 0 else v_mid
                    for a in range(4):
                        src = bass.AP(vsrc.tensor, d * P * BLK * SEQW + c * (CH * SEQW) + a,
                                      [[BLK * SEQW, BLK], [BLK * BLK * SEQW, 4], [1, CH * SEQW - a]])
                        sp.dma_start(vi[BLK * a:BLK * a + BLK, k, :, 0:CH * SEQW - a], src).then_inc(v_loaded[k], 16)

                for r in range(ROUNDS):
                    if r >= DH:
                        sp.wait_ge(mid_stored, 16 * (r - DH + 1))
                    for k in range(2):
                        chunk(r, k, k)
                    with sp.Fori(1, PER // 2) as i:
                        for k in range(2):
                            chunk(r, i * 2 + k, k)

            @block.tensor
            def _(pe):
                for r in range(ROUNDS):
                    def pair(i, r=r):
                        for k in range(2):
                            n = r * PER + i * 2 + k
                            pe.wait_ge(t_loaded[k], 16 * (r * PER // 2) + i * 16 + 16)
                            pe.wait_ge(v_loaded[k], 64 * (r * PER // 2) + i * 64 + 64)
                            pe.wait_ge(y_act, n * 2 + 2)
                            for c in range(CH):
                                bk, at = 2 * k + c // 2, c % 2
                                for j in range(LAGS):
                                    w = NBLK - 4 * j
                                    for q in range(4):
                                        out = y_ps[BLK * q:BLK * q + BLK, bk, at, :].rearrange("p (b i) -> p b i", b=B)[:, :, 4 * j:NBLK]
                                        lhs = tp[:, k, q, c, :].rearrange("p (w l) -> p w l", l=LAGS)[:, :, LAGS - 1 - j]
                                        rhs = vi[:, k, q, c * SEQW:(c + 1) * SEQW].rearrange("p (b i) -> p b i", b=B)[:, :, 0:w]
                                        last = nc.tensor.matmul(out, lhs, rhs, start=j == 0, stop=j == LAGS - 1, skip_group_check=True)
                            last.then_inc(y_p, 1)
                    with pe.Fori(0, PER // 2) as i:
                        pair(i)

            @block.scalar
            def _(act):
                act.sem_inc(y_act, 4)
                for r in range(ROUNDS):
                    if r:
                        act.wait_ge(yt_done, B * r)
                    with act.Fori(0, PER // 2) as i:
                        for k in range(2):
                            act.wait_ge(y_p, i * 2 + (r * PER + k + 1))
                            for h in range(2):
                                nc.scalar.activation(yc[:, bass.ds(i * (2 * CH) + (k * CH + 2 * h), 2), :],
                                                     y_ps[:, 2 * k + h, :, :], ACT.Copy).then_inc(y_act, 1)

            @block.gpsimd
            def _(pool):
                every = vb[:, :, :, :].rearrange("p a b k -> p (a b) k")
                pool.memset(every[:, :, 0:PADB], 0.0)
                pool.memset(every[:, :, PADB + NBLK:BW], 0.0).then_inc(zeroed, 1)
                for r in range(ROUNDS):
                    o, d = divmod(r, DH)

                    def load(b, k, r=r, o=o, d=d):
                        pool.wait_ge(vn_done, B * r + b + 1)
                        pool.sem_inc(held, 1)
                        pool.dma_start(gt[:, k, :], gates[o, d, :, bass.ds(b * S, S)]).then_inc(g_loaded[k], 16)

                    def store(b, k, r=r, d=d):
                        pool.wait_ge(vn_done, B * r + b + 3)
                        pool.sem_inc(held, 1)
                        pool.dma_start(v_out[d, :, bass.ds(b * S, S)], vn[:, k, :]).then_inc(out_stored[k], 16)

                    with pool.Fori(0, B // 2) as i:
                        for k in range(2):
                            load(i * 2 + k, k)
                        for k in range(2):
                            if o:
                                store(i * 2 + k, k)
                    if o == 0:
                        pool.wait_ge(vb_done, B * (r + 1))
                        pool.dma_start(v_mid[d], vb[:, :, :, :].rearrange("p a b c -> p (a b c)")).then_inc(mid_stored, 16)
                for k in range(2):
                    pool.wait_ge(out_stored[k], 16 * (B // 2) * DH)
                pool.wait_ge(mid_stored, 16 * DH)

            @block.vector
            def _(dve):
                dve.sem_inc(vn_done, 2)
                dve.wait_ge(zeroed, 1)
                for r in range(ROUNDS):
                    o, d = divmod(r, DH)
                    dve.wait_ge(y_act, 4 + 2 * PER * (r + 1))
                    if o == 0 and r:
                        dve.wait_ge(mid_stored, 16 * r)

                    def one(b, k, r=r, o=o, d=d):
                        n = B * r + b
                        dve.wait_ge(vn_done, n + 1)
                        nc.vector.transpose(yt[:, k, :].rearrange("p (i c) -> p i c", c=BLK),
                                            yc[:, :, b * NBLK:(b + 1) * NBLK].rearrange("p c i -> p i c")).then_inc(yt_done, 1)
                        dve.wait_ge(yt_done, n + 1)
                        dve.wait_ge(g_loaded[k], 16 * (B // 2) * r + (b - k) * 8 + 16)
                        if o:
                            dve.wait_ge(out_stored[k], 16 * (B // 2) * (r - DH) + (b - k) * 8)
                        else:
                            dve.wait_ge(vb_done, n)
                        nc.vector.tensor_tensor(vn[:, k, :].rearrange("p (i s) -> p i s", s=BLK),
                                                yt[:, k, :].rearrange("p (i s) -> p i s", s=BLK)[:, :, ::-1],
                                                gt[:, k, :].rearrange("p (i s) -> p i s", s=BLK), ALU.mult).then_inc(vn_done, 1)
                        if o == 0:
                            dve.wait_ge(vn_done, n + 3)
                            nc.vector.transpose(vb[:, :, b, PADB:PADB + NBLK].rearrange("p c k -> p k c"),
                                                vn[:, k, :].rearrange("p (k s) -> p k s", s=BLK)).then_inc(vb_done, 1)

                    for b in range(B):
                        one(b, b % 2)


def hyena_out(nc, tag, consts, x, v, out_w, out_b, gate_w, rows, count0):
    with ExitStack() as ctx:
        m = Memory(nc, ctx, tag)
        x_res = m.sb("x_res", [P, 2, NT, D])
        vt = m.sb("vt", [P, 2, DH, S])
        v_hi = m.sb("v_hi", [P, 2, DH, S], F32R)
        v_lo = m.sb("v_lo", [P, 2, DH, S], F32R)
        w_hi = m.sb("w_hi", [P, DH, D], F32R)
        w_lo = m.sb("w_lo", [P, DH, D], F32R)
        w_raw = m.sb("w_raw", [P, DH, D])
        brow = m.sb("brow", [P, D])
        bank = m.ps("bank", [P, 6, 512])
        route_ps = m.ps("route_ps", [P, 512])
        route = Route(nc, m, consts, rows, count0)
        w_in, w_hi_done, w_lo_done, v_hi_done, v_lo_done, res_done, out_p, held = (
            m.sem(n) for n in "w_in w_hi_done w_lo_done v_hi_done v_lo_done res_done out_p held".split())
        x_loaded = [m.sem(f"x_loaded{k}") for k in range(2)]
        v_loaded = [m.sem(f"v_loaded{k}") for k in range(2)]

        with nc.Block() as block:

            @block.sync
            def _(sp):
                sp.dma_start(w_raw[:, :, :], out_w.rearrange("(c p) n -> p c n", p=P)).then_inc(w_in, 16)
                sp.dma_start(brow[:, :], out_b.rearrange("(a n) -> a n", a=1).broadcast_to([P, D])).then_inc(w_in, 16)
                route.load(sp, gate_w)
                with sp.Fori(0, B // 2) as i:
                    for k in range(2):
                        b = i * 2 + k
                        sp.wait_ge(v_lo_done, b + 1)
                        sp.wait_ge(v_hi_done, b + 1)
                        sp.sem_inc(held, 1)
                        sp.dma_start(vt[:, k], v[:, :, bass.ds(b * S, S)].rearrange("d p s -> p d s")).then_inc(v_loaded[k], 16)
                        sp.wait_ge(v_lo_done, b + 2)
                        sp.sem_inc(held, 1)
                        sp.dma_start(x_res[:, k], x[bass.ds(b * S, S), :].rearrange("(t p) c -> p t c", p=P)).then_inc(x_loaded[k], 16)
                route.sync_end(nc, sp, B)

            @block.gpsimd
            def _(pool):
                route.prepare_pool(nc, pool)
                with pool.Fori(0, B) as i:
                    route.ln.power(nc, pool, i)
                    route.pool(nc, pool, i)
                pool.wait_ge(route.sent, 16 * NT * B)

            @block.tensor
            def _(pe):
                pe.sem_inc(out_p, NT)
                pe.wait_ge(w_lo_done, 1)
                with pe.Fori(0, B // 2) as i:
                    for k in range(2):
                        b = i * 2 + k
                        pe.wait_ge(v_lo_done, b + 3)
                        for t in range(NT):
                            pe.wait_ge(route.x_done, b * NT + max(t - 3, 0))
                            terms = [(a, c, d) for d in range(DH) for a, c in ((v_hi, w_lo), (v_lo, w_hi), (v_hi, w_hi))]
                            for n, (a, c, d) in enumerate(terms):
                                last = nc.tensor.matmul(bank[:, (NT * k + t) % 4, 0:D], a[:, k, d, t * P:(t + 1) * P], c[:, d, :],
                                                        start=n == 0, stop=n == len(terms) - 1)
                            last.then_inc(out_p, 1)
                        route.tensor(nc, pe, b, route_ps[:, 0:2 * NT].rearrange("p (a t) -> p a t", a=2))

            @block.scalar
            def _(act):
                act.sem_inc(v_hi_done, 2)
                with act.Fori(0, B // 2) as i:
                    for k in range(2):
                        act.wait_ge(v_loaded[k], i * 16 + 16)
                        act.wait_ge(out_p, i * (2 * NT) + NT * k)
                        nc.scalar.activation(v_hi[:, k], vt[:, k], ACT.Copy).then_inc(v_hi_done, 1)

            @block.vector
            def _(dve):
                tt = nc.vector.tensor_tensor
                dve.sem_inc(v_lo_done, 2)
                dve.wait_ge(w_in, 32)
                nc.vector.tensor_copy(w_hi[:, :, :], w_raw[:, :, :]).then_inc(w_hi_done, 1)
                dve.wait_ge(w_hi_done, 1)
                tt(w_lo[:, :, :], w_raw[:, :, :], f32(w_hi[:, :, :]), ALU.subtract).then_inc(w_lo_done, 1)
                route.prepare(nc, dve)
                with dve.Fori(0, B // 2) as i:
                    for k in range(2):
                        b = i * 2 + k
                        dve.wait_ge(v_hi_done, b + 3)
                        tt(v_lo[:, k], vt[:, k], f32(v_hi[:, k]), ALU.subtract).then_inc(v_lo_done, 1)
                        dve.wait_ge(x_loaded[k], i * 16 + 16)
                        for t in range(NT):
                            tt(x_res[:, k, t, :], x_res[:, k, t, :], brow[:, :], ALU.add).then_inc(res_done, 1)
                        dve.wait_ge(route.sent, 16 * NT * b)
                        for t in range(NT):
                            dve.wait_ge(out_p, NT * b + t + 1 + NT)
                            dve.wait_ge(res_done, NT * b + t + 1)
                            tt(route.row[:, t, 0:D], bank[:, (NT * k + t) % 4, 0:D], x_res[:, k, t, :], ALU.add).then_inc(route.x_done, 1)
                        route.vector_stats(nc, dve, b)
                        route.vector_choose(nc, dve, b)
                        route.vector_slots(nc, dve, b, route_ps[:, 0:2 * NT].rearrange("p (a t) -> p a t", a=2))
                route.vector_end(nc, dve, B)


def hybrid_block(nc, x, wq, wk, wv, wo, times, phases, freqs, mlp_w1, mlp_b1, mlp_w2, mlp_b2, mlp_w3, mlp_b3, decay,
                 in_w, in_b, conv_w, conv_b, hy_gate_w, hy_gate_b, hy_out_w, hy_out_b,
                 gate_w, w1, b1, w2, b2, sw1, sb1, sw2, sb2, out):
    def scratch(name, shape):
        return nc.dram_tensor(name, shape, F32).ap()
    arranged = scratch("arranged", [ORDER, DH, CHUNKS, 4, CH, FW])
    v_blocks = scratch("v_blocks", [DH, P, BLK * SEQW])
    v_mid = scratch("v_mid", [DH, P, BLK * SEQW])
    v_out = scratch("v_out", [DH, P, T])
    gates = scratch("gates", [ORDER, DH, P, T])
    rows_a, rows_b = scratch("rows_a", [SLOTS, ROW]), scratch("rows_b", [SLOTS, ROW])
    count_a, count_b = scratch("count_a", [1, 1]), scratch("count_b", [1, 1])
    x_mid = scratch("x_mid", [T, D])
    with ExitStack() as ctx:
        consts = Constants(nc, ctx)
        consts.make(nc)
        filters(nc, "flt", times, phases, freqs, mlp_w1, mlp_b1, mlp_w2, mlp_b2, mlp_w3, mlp_b3, decay, arranged)
        attention(nc, "att", consts, x, wq, wk, wv, wo, gate_w, rows_a, count_a)
        feed_forward(nc, "ffa", consts, rows_a, count_a, w1, b1, w2, b2, sw1, sb1, sw2, sb2, x_mid)
        projections(nc, "prj", consts, x_mid, in_w, in_b, conv_w, conv_b, hy_gate_w, hy_gate_b, v_blocks, gates)
        convolutions(nc, "cnv", arranged, v_blocks, gates, v_mid, v_out)
        hyena_out(nc, "hyo", consts, x_mid, v_out, hy_out_w, hy_out_b, gate_w, rows_b, count_b)
        feed_forward(nc, "ffb", consts, rows_b, count_b, w1, b1, w2, b2, sw1, sb1, sw2, sb2, out)


def kernel(**inputs):
    import concourse.bacc as bacc
    from concourse.bass_utils import run_bass_kernel_spmd

    a = {name.split("_", 1)[1]: np.asarray(v) for name, v in inputs.items()}

    def columns(v):
        return np.moveaxis(v.reshape(v.shape[:-1] + (-1, P)), -1, 0)
    phases = np.zeros((ENC, 3), np.float32)
    phases[FREQS:2 * FREQS, 0] = 0.25
    phases[2 * FREQS, 1] = 1
    phases[:2 * FREQS, 2] = 1
    args = {
        "x": a["attn_a_hidden_states"].reshape(T, D),
        "wq": a["attn_a_Wq"].T, "wk": a["attn_a_Wk"].T, "wv": a["attn_a_Wv"].T, "wo": a["attn_a_Wo"].T,
        "times": np.linspace(0, 1, S, dtype=np.float32)[::-1][None], "phases": phases,
        "freqs": a["attn_b_freqs"].T,
        "mlp_w1": a["attn_b_mlp_w1"], "mlp_b1": a["attn_b_mlp_b1"].T,
        "mlp_w2": a["attn_b_mlp_w2"], "mlp_b2": a["attn_b_mlp_b2"].T,
        "mlp_w3": a["attn_b_mlp_w3"], "mlp_b3": columns(a["attn_b_mlp_b3"]), "decay": columns(a["attn_b_decay"]),
        "in_w": a["attn_b_in_proj_w"], "in_b": columns(a["attn_b_in_proj_b"]),
        "conv_w": columns(a["attn_b_conv_w"][:, :, 0]).transpose(0, 1, 3, 2), "conv_b": columns(a["attn_b_conv_b"]),
        "hy_gate_w": a["attn_b_gate_w"], "hy_gate_b": columns(a["attn_b_gate_b"]),
        "hy_out_w": a["attn_b_out_proj_w"], "hy_out_b": a["attn_b_out_proj_b"],
        "gate_w": a["ffn_gate_w"], "w1": a["ffn_w1"], "b1": a["ffn_b1"].reshape(2, HB, P).transpose(0, 2, 1),
        "w2": a["ffn_w2"], "b2": a["ffn_b2"],
        "sw1": a["ffn_sw1"], "sb1": a["ffn_sb1"].reshape(HB, P).T, "sw2": a["ffn_sw2"], "sb2": a["ffn_sb2"],
    }
    nc = bacc.Bacc("TRN2", target_bir_lowering=False, num_devices=1)
    arrays, aps = {}, []
    for name, v in args.items():
        arrays[f"in_{name}"] = np.ascontiguousarray(v)
        aps.append(nc.dram_tensor(f"in_{name}", v.shape, mybir.dt.from_np(v.dtype), kind="ExternalInput").ap())
    aps.append(nc.dram_tensor("out", [T, D], F32, kind="ExternalOutput").ap())
    hybrid_block(nc, *aps)
    r = run_bass_kernel_spmd(nc, [arrays], core_ids=[0])
    return r.results[0]["out"].reshape(B, S, D)
```

```python
import numpy as np
import concourse.bass as bass
from concourse import mybir
from contextlib import ExitStack

F32 = mybir.dt.float32
F32R = mybir.dt.float32r
BF16 = mybir.dt.bfloat16
U32 = mybir.dt.uint32
I32 = mybir.dt.int32
ALU = mybir.AluOpType
ACT = mybir.ActivationFunctionType
AX = mybir.AxisListType

P = 128
B, S, D = 8, 1024, 256
T = B * S
HID = 1024
DH = D // P
TILE = 512
SUB = TILE // P
SLOTS = T + TILE
NTILES = SLOTS // TILE
ROW = 2 * D + 8
HB = HID // P
EPS = 1e-5
MASKED = -1e37


def f32(ap):
    return ap.bitcast(F32)


class Memory:

    def __init__(self, nc, ctx, tag):
        self.nc, self.ctx, self.tag = nc, ctx, tag
        self.sems = []
        ctx.callback(self.clear)

    def sb(self, name, shape, dt=F32):
        return self.ctx.enter_context(self.nc.sbuf_tensor(f"{self.tag}_{name}", shape, dt))

    def ps(self, name, shape, dt=F32):
        return self.ctx.enter_context(self.nc.psum_tensor(f"{self.tag}_{name}", shape, dt))

    def sem(self, name):
        self.sems.append(self.nc.alloc_semaphore(name=f"{self.tag}_{name}"))
        return self.sems[-1]

    def clear(self):
        self.nc.clear_and_free_semaphores(self.sems)
        self.nc.all_engine_barrier()


def feed_forward(nc, tag, consts, rows, count0, w1, b1, w2, b2, sw1, sb1, sw2, sb2, out):
    NETS = 3
    STEPS = 2 * HB
    RING = 4
    LAG = 2
    up_w = [sw1, w1[0], w1[1]]
    down_w = [sw2, w2[0], w2[1]]
    with ExitStack() as ctx:
        m = Memory(nc, ctx, tag)
        w_raw = m.sb("w_raw", [P, 2, DH * HID])
        up_hi = m.sb("up_hi", [P, NETS, DH, HID], F32R)
        up_lo = m.sb("up_lo", [P, NETS, DH, HID], F32R)
        dn_hi = m.sb("dn_hi", [P, NETS, HB, D], F32R)
        dn_lo = m.sb("dn_lo", [P, NETS, HB, D], F32R)
        xn = m.sb("xn", [P, SUB, D])
        res = m.sb("res", [P, SUB, ROW])
        xt_hi = m.sb("xt_hi", [P, DH, TILE], F32R)
        xt_lo = m.sb("xt_lo", [P, DH, TILE], F32R)
        h_f = m.sb("h_f", [P, RING, TILE])
        h_hi = m.sb("h_hi", [P, RING, TILE], F32R)
        h_lo = m.sb("h_lo", [P, RING, TILE], F32R)
        y_sb = m.sb("y_sb", [P, SUB, D])
        token = m.sb("token", [P, SUB], U32)
        b_up = m.sb("b_up", [P, NETS, HB])
        b_tile = m.sb("b_tile", [P, NTILES, HB])
        c_hid = m.sb("c_hid", [P, 2, HB])
        c_wide = m.sb("c_wide", [P, 2, HB, P])
        row_b = m.sb("row_b", [P, NETS, D])
        konst = m.sb("konst", [P, 2, D])
        k_tile = m.sb("k_tile", [P, D])
        flag = m.sb("flag", [P, NTILES])
        nflag = m.sb("nflag", [P, NTILES])
        flag_u = m.sb("flag_u", [P, NTILES], U32)
        start = m.sb("start", [P, NTILES])
        n0 = m.sb("n0", [P, 1])
        up_ps = m.ps("up_ps", [P, RING, TILE])
        t_ps = m.ps("t_ps", [P, DH, TILE])
        y_ps = m.ps("y_ps", [P, SUB, D])

        w_loaded = [m.sem(f"w_loaded{n}") for n in range(2)]
        w_hi = m.sem("w_hi")
        w_lo = m.sem("w_lo")
        b_loaded = m.sem("b_loaded")
        tiles_known = m.sem("tiles_known")
        starts_made = m.sem("starts_made")
        const_hid = m.sem("const_hid")
        const_y = m.sem("const_y")
        const_done = m.sem("const_done")
        xn_loaded = m.sem("xn_loaded")
        res_loaded = m.sem("res_loaded")
        transposed = m.sem("transposed")
        xt_hi_done = m.sem("xt_hi_done")
        xt_lo_done = m.sem("xt_lo_done")
        up_done = m.sem("up_done")
        h_act = m.sem("h_act")
        h_hi_done = m.sem("h_hi_done")
        h_lo_done = m.sem("h_lo_done")
        down_done = m.sem("down_done")
        y_done = m.sem("y_done")
        base_done = m.sem("base_done")
        base_step = m.sem("base_step")
        y_stored = m.sem("y_stored")
        held = m.sem("held")

        tile_rows = rows.rearrange("(t s p) c -> t p s c", p=P, s=SUB)

        with nc.Block() as block:

            @block.sync
            def _(sp):
                for n in range(2 * NETS):
                    net, down = divmod(n, 2)
                    if n >= 2:
                        sp.wait_ge(w_lo, n - 1)
                    src = (down_w if down else up_w)[net].rearrange("(c p) n -> p c n", p=P)
                    dst = w_raw[:, n % 2, :].rearrange("p (c n) -> p c n", c=HB if down else DH)
                    sp.dma_start(dst, src).then_inc(w_loaded[n % 2], 16)
                    if n == 0:
                        sp.dma_start(xn[:, :, :], tile_rows[0, :, :, D:2 * D]).then_inc(xn_loaded, 16)
                        sp.dma_start(res[:, :, :], tile_rows[0]).then_inc(res_loaded, 16)

                def load(i):
                    sp.wait_ge(transposed, DH * i)
                    sp.sem_inc(held, 1)
                    sp.dma_start(xn[:, :, :], rows[bass.ds(i * TILE, TILE), D:2 * D]
                                 .rearrange("(s p) c -> p s c", p=P)).then_inc(xn_loaded, 16)
                    sp.wait_ge(y_done, 1 + i)
                    sp.sem_inc(held, 1)
                    sp.dma_start(res[:, :, :], rows[bass.ds(i * TILE, TILE), :]
                                 .rearrange("(s p) c -> p s c", p=P)).then_inc(res_loaded, 16)

                with sp.Fori(1, NTILES) as i:
                    load(i)

            @block.gpsimd
            def _(pool):
                pool.dma_start(b_up[:, 0, :], sb1).then_inc(b_loaded, 16)
                for e in range(2):
                    pool.dma_start(b_up[:, 1 + e, :], b1[e]).then_inc(b_loaded, 16)
                pool.dma_start(row_b[:, 0, :], sb2.rearrange("(a n) -> a n", a=1).broadcast_to([P, D])).then_inc(b_loaded, 16)
                for e in range(2):
                    pool.dma_start(row_b[:, 1 + e, :], b2[e:e + 1, :].broadcast_to([P, D])).then_inc(b_loaded, 16)
                pool.dma_start(n0[:, :], count0.broadcast_to([P, 1])).then_inc(b_loaded, 16)
                pool.iota(start[:, :], pattern=[[TILE, NTILES]], base=0, channel_multiplier=0,
                          allow_small_or_imprecise_dtypes=True).then_inc(starts_made, 1)

                def scatter(i):
                    for s in range(SUB):
                        if s == 0:
                            pool.wait_ge(y_done, i + 2)
                            pool.sem_inc(held, 1)
                        pool.indirect_dma_start(out, bass.IndirectOffsetOnAxis(token[:, s:s + 1], 0),
                                                y_sb[:, s, :], None, bounds_check=T - 1,
                                                oob_is_err=False).then_inc(y_stored, 16)

                with pool.Fori(0, NTILES) as i:
                    scatter(i)
                pool.wait_ge(y_stored, 16 * SUB * NTILES)

            @block.tensor
            def _(pe):
                pe.sem_inc(down_done, RING)
                pe.sem_inc(up_done, 1)

                def transposes(i):
                    pe.wait_ge(xn_loaded, 16 * i + 16)
                    pe.wait_ge(xt_lo_done, DH * i + 1)
                    for d in range(DH):
                        for s in range(SUB):
                            last = nc.tensor.transpose(t_ps[:, d, s * P:(s + 1) * P],
                                                       xn[:, s, d * P:(d + 1) * P], consts.ident[:, :])
                        last.then_inc(transposed, 1)

                def up(i, s, net):
                    g = i * STEPS + s
                    j = s % HB
                    if s == 0:
                        pe.wait_ge(xt_lo_done, DH * i + DH + 1)
                    pe.wait_ge(h_act, g + 1)
                    terms = [(a, b, d) for d in range(DH) for a, b in
                             ((up_hi, xt_lo), (up_lo, xt_hi), (up_hi, xt_hi))]
                    for n, (a, b, d) in enumerate(terms):
                        last = nc.tensor.matmul(up_ps[:, s % RING, :], a[:, net, d, j * P:(j + 1) * P],
                                                b[:, d, :], start=n == 0, stop=n == len(terms) - 1)
                    last.then_inc(up_done, 1)

                def down(i, s, net):
                    g = i * STEPS + s
                    j = s % HB
                    if s == 0:
                        pe.wait_ge(y_done, i + 1)
                    pe.wait_ge(h_lo_done, g + RING + 1)
                    for t in range(SUB):
                        for n, (a, b) in enumerate(((h_hi, dn_lo), (h_lo, dn_hi), (h_hi, dn_hi))):
                            last = nc.tensor.matmul(y_ps[:, t, :], a[:, s % RING, t * P:(t + 1) * P],
                                                    b[:, net, j, :],
                                                    start=s == 0 and n == 0 and t % 2 == 0,
                                                    stop=s == STEPS - 1 and n == 2, skip_group_check=True)
                    last.then_inc(down_done, 1)

                def steps(i, of, net, more):
                    for s in of:
                        if s < STEPS:
                            up(i, s, net if s >= HB else 0)
                        if s == STEPS - 1 and more:
                            transposes(i + 1)
                        if s >= LAG:
                            down(i, s - LAG, net if s - LAG >= HB else 0)

                expert = pe.alloc_register(f"{tag}_expert")

                def tile(i, more):
                    steps(i, range(HB), 0, more)
                    pe.reg_load(expert, flag_u[0:1, bass.ds(i, 1)])
                    with pe.If_lt(expert, 1):
                        steps(i, range(HB, STEPS + LAG), 1, more)
                    with pe.Else():
                        steps(i, range(HB, STEPS + LAG), 2, more)

                pe.wait_ge(xn_loaded, 16)
                transposes(0)
                for e in range(2):
                    pe.wait_ge(w_lo, 2 * e + 4)
                    pe.wait_ge(const_hid, e + 1)
                    terms = [(j, w) for j in range(HB) for w in (dn_hi, dn_lo)]
                    for n, (j, w) in enumerate(terms):
                        last = nc.tensor.matmul(up_ps[:, e, 0:D], c_wide[:, e, j, :],
                                                f32(w[:, 1 + e, j, :]), start=n == 0, stop=n == len(terms) - 1)
                    last.then_inc(const_y, 1)
                pe.wait_ge(tiles_known, 4)
                pe.wait_ge(const_done, 3)
                with pe.Fori(0, NTILES - 1) as i:
                    tile(i, True)
                tile(NTILES - 1, False)

            @block.scalar
            def _(act):
                act.sem_inc(h_act, RING)

                def split(i):
                    for d in range(DH):
                        act.wait_ge(transposed, DH * i + d + 1)
                        if d == 0:
                            act.wait_ge(up_done, STEPS * i + 1)
                        nc.scalar.activation(xt_hi[:, d, :], t_ps[:, d, :], ACT.Copy).then_inc(xt_hi_done, 1)

                def hidden(i, s):
                    g = i * STEPS + s
                    act.wait_ge(up_done, g + 2)
                    act.wait_ge(h_lo_done, g + 1)
                    bias = b_up[:, 0, s:s + 1] if s < HB else b_tile[:, i, s - HB:s - HB + 1] if isinstance(i, int) \
                        else b_tile[:, bass.ds(i, 1), s - HB:s - HB + 1].rearrange("p a b -> p (a b)")
                    nc.scalar.activation(h_f[:, s % RING, :], up_ps[:, s % RING, :], ACT.Relu,
                                         bias=bias).then_inc(h_act, 1)

                act.wait_ge(b_loaded, 16 * 7)
                split(0)
                act.wait_ge(tiles_known, 4)
                with act.Fori(0, NTILES - 1) as i:
                    for s in range(STEPS):
                        hidden(i, s)
                    split(i + 1)
                for s in range(STEPS):
                    hidden(NTILES - 1, s)

            @block.vector
            def _(dve):
                dve.sem_inc(h_lo_done, RING)
                dve.sem_inc(y_done, 1)
                dve.sem_inc(xt_lo_done, 1)
                for n in range(2 * NETS):
                    net, down = divmod(n, 2)
                    hi, lo = (dn_hi, dn_lo) if down else (up_hi, up_lo)
                    raw = w_raw[:, n % 2, :].rearrange("p (c n) -> p c n", c=HB if down else DH)
                    dve.wait_ge(w_loaded[n % 2], 16 * (n // 2 + 1))
                    nc.vector.tensor_copy(hi[:, net, :, :], raw).then_inc(w_hi, 1)
                    dve.wait_ge(w_hi, n + 1)
                    nc.vector.tensor_tensor(lo[:, net, :, :], raw, f32(hi[:, net, :, :]), ALU.subtract).then_inc(w_lo, 1)
                    if n == 0:
                        dve.wait_ge(b_loaded, 16 * 7)
                        dve.wait_ge(starts_made, 1)
                        nc.vector.tensor_scalar(flag[:, :], start[:, :], n0[:, 0:1], None, ALU.is_ge).then_inc(tiles_known, 1)
                        dve.wait_ge(tiles_known, 1)
                        nc.vector.tensor_copy(flag_u[:, :], flag[:, :])
                        nc.vector.tensor_scalar(nflag[:, :], flag[:, :], -1.0, 1.0, ALU.mult, ALU.add).then_inc(tiles_known, 1)
                        dve.wait_ge(tiles_known, 2)
                        wide = [P, NTILES, HB]
                        nc.vector.tensor_tensor(b_tile[:, :, :], b_up[:, 1:2, :].broadcast_to(wide),
                                                nflag[:, :].unsqueeze(2).broadcast_to(wide), ALU.mult)
                        nc.vector.tensor_tensor(c_wide[:, 0, :, :].rearrange("p a b -> p (a b)")[:, 0:NTILES * HB].rearrange("p (a b) -> p a b", b=HB),
                                                b_up[:, 2:3, :].broadcast_to(wide),
                                                flag[:, :].unsqueeze(2).broadcast_to(wide), ALU.mult).then_inc(tiles_known, 1)
                        dve.wait_ge(tiles_known, 3)
                        nc.vector.tensor_tensor(b_tile[:, :, :], b_tile[:, :, :],
                                                c_wide[:, 0, :, :].rearrange("p a b -> p (a b)")[:, 0:NTILES * HB].rearrange("p (a b) -> p a b", b=HB),
                                                ALU.add).then_inc(tiles_known, 1)
                        dve.wait_ge(tiles_known, 4)
                        nc.vector.tensor_relu(c_hid[:, :, :], b_up[:, 1:3, :]).then_inc(h_hi_done, 1)
                        dve.wait_ge(h_hi_done, 1)
                        for e in range(2):
                            nc.vector.tensor_copy(c_wide[:, e, :, :],
                                                  c_hid[:, e, :].unsqueeze(2).broadcast_to([P, HB, P])).then_inc(const_hid, 1)

                def split(i):
                    for d in range(DH):
                        dve.wait_ge(xt_hi_done, DH * i + d + 1)
                        nc.vector.tensor_tensor(xt_lo[:, d, :], t_ps[:, d, :], f32(xt_hi[:, d, :]),
                                                ALU.subtract).then_inc(xt_lo_done, 1)

                def base(i):
                    at = slice(i, i + 1) if isinstance(i, int) else bass.ds(i, 1)
                    dve.wait_ge(base_step, 3 * i + 1)
                    nc.vector.tensor_scalar(k_tile[:, :], konst[:, 0, :], nflag[:, at], None, ALU.mult).then_inc(base_step, 1)
                    dve.wait_ge(base_step, 3 * i + 2)
                    nc.vector.scalar_tensor_tensor(k_tile[:, :], konst[:, 1, :], flag[:, at], k_tile[:, :],
                                                   ALU.mult, ALU.add).then_inc(base_step, 1)
                    dve.wait_ge(res_loaded, 16 * i + 16)
                    dve.wait_ge(base_step, 3 * i + 3)
                    nc.vector.tensor_tensor(res[:, :, 0:D], res[:, :, 0:D],
                                            k_tile[:, :].unsqueeze(1).broadcast_to([P, SUB, D]), ALU.add).then_inc(base_step, 1)

                def hidden(i, s):
                    g = i * STEPS + s
                    dve.wait_ge(h_act, g + RING + 1)
                    dve.wait_ge(down_done, g + 1)
                    nc.vector.tensor_copy(h_hi[:, s % RING, :], h_f[:, s % RING, :]).then_inc(h_hi_done, 1)
                    dve.wait_ge(h_hi_done, g + 2)
                    nc.vector.tensor_tensor(h_lo[:, s % RING, :], h_f[:, s % RING, :], f32(h_hi[:, s % RING, :]),
                                            ALU.subtract).then_inc(h_lo_done, 1)

                def finish(i):
                    dve.wait_ge(down_done, STEPS * i + STEPS + RING)
                    dve.wait_ge(base_step, 3 * i + 4)
                    dve.wait_ge(y_stored, 16 * SUB * i)
                    nc.vector.tensor_copy(token[:, :], res[:, :, 2 * D:2 * D + 1].rearrange("p s c -> p (s c)").bitcast(U32))
                    nc.vector.tensor_tensor(y_sb[:, :, :], y_ps[:, :, :], res[:, :, 0:D], ALU.add).then_inc(y_done, 1)

                split(0)
                for e in range(2):
                    dve.wait_ge(const_y, 2)
                    if e == 0:
                        nc.vector.tensor_tensor(row_b[:, 1, :], row_b[:, 1, :], row_b[:, 2, :], ALU.add).then_inc(const_done, 1)
                    dve.wait_ge(const_done, 1 + e)
                    nc.vector.scalar_tensor_tensor(konst[:, e, :], up_ps[:, 1 - e, 0:D], 1.0, row_b[:, 1, :],
                                                   ALU.mult, ALU.add).then_inc(const_done, 1)
                dve.wait_ge(const_done, 3)
                nc.vector.tensor_tensor(konst[:, :, :], konst[:, :, :], row_b[:, 0:1, :].broadcast_to([P, 2, D]),
                                        ALU.add).then_inc(base_step, 1)
                def blocks(i):
                    for s in range(STEPS):
                        hidden(i, s)
                        if s == HB - 1:
                            base(i)

                with dve.Fori(0, NTILES - 1) as i:
                    blocks(i)
                    split(i + 1)
                    finish(i)
                blocks(NTILES - 1)
                finish(NTILES - 1)


class Constants:

    def __init__(self, nc, ctx):
        m = Memory(nc, ctx, "c")
        self.ident = m.sb("ident", [P, P])
        self.ident_bf = m.sb("ident_bf", [P, P], BF16)
        self.before = m.sb("before", [P, P])
        self.ones = m.sb("ones", [P, P])
        self.minus_half = m.sb("minus_half", [P, 16])
        self.head_rows = m.sb("head_rows", [P, 8])
        self.mask_q = m.sb("mask_q", [P, 2, 512], BF16)
        self.mask_k = m.sb("mask_k", [P, 512], BF16)
        self.made = m.sem("made")
        self.zeroed = m.sem("zeroed")

    def make(self, nc):
        with nc.Block() as block:
            @block.gpsimd
            def _(pool):
                pool.memset(self.ident[:, :], 0.0).then_inc(self.zeroed, 1)
                pool.memset(self.ones[:, :], 1.0).then_inc(self.zeroed, 1)
                pool.wait_ge(self.zeroed, 2)
                pool.affine_select(out=self.ident[:, :], in_=self.ident[:, :], compare_op=ALU.not_equal, fill=1.0,
                                   base=0, pattern=[[-1, P]], channel_multiplier=1).then_inc(self.made, 1)
                pool.affine_select(out=self.before[:, :], in_=self.ones[:, :], compare_op=ALU.is_gt, fill=0.0,
                                   base=0, pattern=[[1, P]], channel_multiplier=-1).then_inc(self.made, 1)
                pool.wait_ge(self.made, 2)
                pool.tensor_copy(self.ident_bf[:, :], self.ident[:, :]).then_inc(self.made, 1)
                pool.memset(self.minus_half[:, :], -0.5).then_inc(self.made, 1)
                pool.affine_select(out=self.head_rows[:, :], in_=self.ones[:, 0:8], compare_op=ALU.is_ge, fill=0.0,
                                   base=0, pattern=[[-16, 8]], channel_multiplier=1).then_inc(self.made, 1)
                pool.wait_ge(self.made, 5)
                pool.affine_select(out=self.head_rows[:, :], in_=self.head_rows[:, :], compare_op=ALU.is_ge, fill=0.0,
                                   base=15, pattern=[[16, 8]], channel_multiplier=-1).then_inc(self.made, 1)
                pool.memset(self.mask_q[:, :, :], 0.0).then_inc(self.zeroed, 1)
                pool.memset(self.mask_k[:, :], 0.0).then_inc(self.zeroed, 1)
                pool.wait_ge(self.zeroed, 4)
                pool.affine_select(out=self.mask_q[:, 0, :], in_=self.mask_q[:, 0, :], compare_op=ALU.is_ge, fill=MASKED,
                                   base=0, pattern=[[0, 4], [-1, P]], channel_multiplier=1).then_inc(self.made, 1)
                pool.affine_select(out=self.mask_q[:, 1, :], in_=self.mask_q[:, 1, :], compare_op=ALU.is_ge, fill=MASKED,
                                   base=P, pattern=[[0, 2], [-1, 2 * P]], channel_multiplier=1).then_inc(self.made, 1)
                pool.affine_select(out=self.mask_k[:, :], in_=self.mask_k[:, :], compare_op=ALU.is_ge, fill=MASKED,
                                   base=0, pattern=[[0, 4], [1, P]], channel_multiplier=-1).then_inc(self.made, 1)
                pool.wait_ge(self.made, 9)


NT = S // P
HEADS = 16
HD = D // HEADS
WIN = 256
KT = WIN // P
HW = 64
PAIRS = HEADS // 2
OW = 32
GROUPS = HEADS // 4


class LayerNorm:

    def __init__(self, m, name, consts, n):
        self.n, self.consts = n, consts
        self.stat = m.sb(f"{name}_stat", [P, n, 6])
        self.mv = m.sb(f"{name}_mv", [P, n, 2])
        self.rstd = m.sb(f"{name}_rstd", [P, n])
        self.stats_done = m.sem(f"{name}_stats")
        self.aggr_done = m.sem(f"{name}_aggr")
        self.eps_added = m.sem(f"{name}_eps")
        self.rstd_done = m.sem(f"{name}_rstd")
        self.done = m.sem(f"{name}_done")
        self.held = m.sem(f"{name}_held")

    def stats(self, nc, dve, i, x):
        for t in range(self.n):
            nc.vector.bn_stats(self.stat[:, t, :], x[:, t, :]).then_inc(self.stats_done, 1)
        dve.wait_ge(self.stats_done, self.n * i + self.n)
        dve.sem_inc(self.held, 1)
        for t in range(self.n):
            nc.vector.bn_aggr(self.mv[:, t, :], self.stat[:, t, :]).then_inc(self.aggr_done, 1)

    def power(self, nc, pool, i):
        pool.wait_ge(self.aggr_done, self.n * i + self.n)
        pool.sem_inc(self.held, 1)
        nc.gpsimd.tensor_scalar(self.rstd[:, :], self.mv[:, :, 1:2].rearrange("p n a -> p (n a)"), EPS, None,
                                ALU.add).then_inc(self.eps_added, 1)
        pool.wait_ge(self.eps_added, i + 1)
        nc.gpsimd.tensor_tensor(self.rstd[:, :], self.rstd[:, :], self.consts.minus_half[:, 0:self.n],
                                ALU.pow).then_inc(self.rstd_done, 1)

    def apply(self, nc, dve, i, x, out):
        dve.wait_ge(self.rstd_done, i + 1)
        for t in range(self.n):
            nc.vector.tensor_scalar(out[:, t, :], x[:, t, :], self.mv[:, t, 0:1], self.rstd[:, t:t + 1],
                                    ALU.subtract, ALU.mult).then_inc(self.done, 1)


class Route:

    def __init__(self, nc, m, consts, rows, count0, buffers=1):
        self.consts, self.rows, self.count0 = consts, rows, count0
        self.ln = LayerNorm(m, "route", consts, NT)
        self.row = m.sb("row", [P, buffers, NT, ROW])
        self.gate = m.sb("gate", [P, 2, D])
        self.gate_d = m.sb("gate_d", [P, D])
        self.prod = m.sb("prod", [P, D])
        self.score = m.sb("score", [P, NT])
        self.to1 = m.sb("to1", [P, NT])
        self.total = m.sb("total", [P, NT])
        self.upto = m.sb("upto", [P, NT])
        self.carry = m.sb("carry", [P, 1])
        self.place = m.sb("place", [P, NT])
        self.back = m.sb("back", [P, NT])
        self.ones_n = m.sb("ones_n", [P, NT])
        self.slot = m.sb("slot", [P, NT], U32)
        self.fill = m.sb("fill", [P, SUB, ROW])
        self.n0 = m.sb("n0", [P, 1])
        self.n0_u = m.sb("n0_u", [P, 1], U32)
        self.gate_loaded = m.sem("gate_loaded")
        self.gate_done = m.sem("gate_done")
        self.x_done = m.sem("x_done")
        self.scored = m.sem("scored")
        self.chosen = m.sem("chosen")
        self.counted = m.sem("counted")
        self.step = m.sem("slot_step")
        self.slots_done = m.sem("slots_done")
        self.sent = m.sem("sent")
        self.held = m.sem("slots_held")
        self.numbered = m.sem("numbered")
        self.finished = m.sem("finished")
        self.end_written = m.sem("end_written")

    def load(self, eng, gate_w):
        for e in range(2):
            eng.dma_start(self.gate[:, e, :], gate_w[e:e + 1, :].broadcast_to([P, D])).then_inc(self.gate_loaded, 16)

    def prepare_pool(self, nc, pool):
        nc.gpsimd.iota(self.place[:, :], pattern=[[P, NT]], base=0, channel_multiplier=1,
                       allow_small_or_imprecise_dtypes=True).then_inc(self.numbered, 1)

    def prepare(self, nc, dve):
        dve.wait_ge(self.gate_loaded, 32)
        nc.vector.tensor_tensor(self.gate_d[:, :], self.gate[:, 1, :], self.gate[:, 0, :], ALU.subtract).then_inc(self.gate_done, 1)
        nc.vector.memset(self.carry[:, :], 0.0).then_inc(self.gate_done, 1)
        nc.vector.memset(self.ones_n[:, :], 1.0).then_inc(self.gate_done, 1)
        nc.vector.memset(self.row[:, :, :, 2 * D:ROW], 0.0).then_inc(self.gate_done, 1)
        nc.vector.memset(self.fill[:, :, :], 0.0).then_inc(self.gate_done, 1)
        dve.wait_ge(self.gate_done, 5)
        nc.vector.memset(self.fill[:, :, 2 * D:2 * D + 1].bitcast(U32), 2 * T).then_inc(self.gate_done, 1)
        dve.wait_ge(self.gate_done, 6)
        dve.wait_ge(self.numbered, 1)

    def vector_stats(self, nc, dve, i, k=0):
        dve.wait_ge(self.x_done, NT * i + NT)
        self.ln.stats(nc, dve, i, self.row[:, k, :, 0:D])

    def vector_norm(self, nc, dve, i, k=0):
        self.ln.apply(nc, dve, i, self.row[:, k, :, 0:D], self.row[:, k, :, D:2 * D])

    def vector_choose(self, nc, dve, i, k=0):
        row, ln = self.row[:, k], self.ln
        for t in range(NT):
            dve.wait_ge(ln.done, NT * i + t + 1)
            dve.wait_ge(self.scored, NT * i + t)
            nc.vector.tensor_tensor_reduce(self.prod[:, :], row[:, t, D:2 * D], self.gate_d[:, :], 1.0, 0.0,
                                           ALU.mult, ALU.add, self.score[:, t:t + 1]).then_inc(self.scored, 1)
        dve.wait_ge(self.scored, NT * i + NT)
        nc.vector.tensor_scalar(self.to1[:, :], self.score[:, :], 0.0, None, ALU.is_gt).then_inc(self.chosen, 1)

    def tensor(self, nc, pe, i, ps):
        pe.wait_ge(self.chosen, i + 1)
        nc.tensor.matmul(ps[:, 0, :], self.consts.before[:, :], self.to1[:, :], start=True, stop=True)
        nc.tensor.matmul(ps[:, 1, :], self.consts.ones[:, :], self.to1[:, :], start=True, stop=True).then_inc(self.counted, 1)

    def vector_slots(self, nc, dve, i, ps, k=0):
        N = 9
        n = [0]

        def link(ins):
            n[0] += 1
            ins.then_inc(self.step, 1)
            dve.wait_ge(self.step, N * i + n[0])

        dve.wait_ge(self.counted, i + 1)
        link(nc.vector.tensor_copy(self.total[:, :], ps[:, 1, :]))
        link(nc.vector.tensor_tensor_scan(self.upto[:, :], self.ones_n[:, :], self.total[:, :], self.carry[:, 0:1],
                                          ALU.mult, ALU.add))
        link(nc.vector.tensor_copy(self.carry[:, :], self.upto[:, NT - 1:NT]))
        link(nc.vector.tensor_tensor(self.upto[:, :], self.upto[:, :], self.total[:, :], ALU.subtract))
        link(nc.vector.tensor_tensor(self.upto[:, :], self.upto[:, :], ps[:, 0, :], ALU.add))
        link(nc.vector.tensor_tensor(self.upto[:, :], self.place[:, :], self.upto[:, :], ALU.subtract))
        link(nc.vector.tensor_scalar(self.back[:, :], self.place[:, :], -1.0, float(SLOTS - 1), ALU.mult, ALU.add))
        link(nc.vector.tensor_tensor(self.back[:, :], self.back[:, :], self.to1[:, :], ALU.mult))
        link(nc.vector.tensor_tensor(self.upto[:, :], self.upto[:, :], self.back[:, :], ALU.add))
        nc.vector.tensor_copy(self.row[:, k, :, 2 * D:2 * D + 1].rearrange("p t a -> p (t a)").bitcast(U32), self.place[:, :])
        nc.vector.tensor_copy(self.slot[:, :], self.upto[:, :]).then_inc(self.slots_done, 1)
        dve.wait_ge(self.slots_done, 2 * i + 1)
        nc.vector.tensor_scalar(self.place[:, :], self.place[:, :], float(S), None, ALU.add).then_inc(self.slots_done, 1)
        dve.wait_ge(self.slots_done, 2 * i + 2)

    def pool(self, nc, pool, i, k=0):
        pool.wait_ge(self.slots_done, 2 * i + 1)
        pool.sem_inc(self.held, 1)
        for t in range(NT):
            pool.indirect_dma_start(self.rows[:, :], bass.IndirectOffsetOnAxis(self.slot[:, t:t + 1], 0),
                                    self.row[:, k, t, :], None, bounds_check=SLOTS - 1,
                                    oob_is_err=False).then_inc(self.sent, 16)

    def vector_end(self, nc, dve, rounds):
        nc.vector.tensor_scalar(self.n0[:, :], self.carry[:, :], -1.0, float(T), ALU.mult, ALU.add).then_inc(self.finished, 1)
        dve.wait_ge(self.finished, 1)
        nc.vector.tensor_copy(self.n0_u[:, :], self.n0[:, :]).then_inc(self.finished, 1)

    def sync_end(self, nc, sp, rounds):
        sp.wait_ge(self.finished, 2)
        sp.wait_ge(self.sent, 16 * NT * rounds)
        sp.dma_start(self.count0, self.n0[0:1, 0:1]).then_inc(self.end_written, 16)
        first = sp.value_load(self.n0_u[0:1, 0:1], min_val=0, max_val=T)
        sp.dma_start(self.rows[bass.ds(first, TILE), :].rearrange("(s p) c -> p s c", p=P),
                     self.fill[:, :, :]).then_inc(self.end_written, 16)
        sp.wait_ge(self.end_written, 32)


def attention(nc, tag, consts, x, wq, wk, wv, wo, gate_w, rows, count0):
    with ExitStack() as ctx:
        m = Memory(nc, ctx, tag)
        x_in = m.sb("x_in", [P, NT, D])
        x_res = m.sb("x_res", [P, NT, D])
        xn = m.sb("xn", [P, NT, D])
        xt_hi = m.sb("xt_hi", [P, DH, S], F32R)
        xt_lo = m.sb("xt_lo", [P, DH, S], F32R)
        w_hi = m.sb("w_hi", [P, 4, DH, D], F32R)
        w_lo = m.sb("w_lo", [P, 4, DH, D], F32R)
        qp = m.sb("qp", [P, 2, HEADS, HW], F32R)
        kp = m.sb("kp", [P, HEADS, HW], F32R)
        qc = m.sb("qc", [P, 2, D], F32R)
        kc = m.sb("kc", [P, D], F32R)
        qht = m.sb("qht", [P, 2, 2, P], F32R)
        km = m.sb("km", [P, 2, 8, WIN], F32R)
        kz = m.sb("kz", [P, HEADS, WIN], F32R)
        qpt = m.sb("qpt", [P, PAIRS, S], F32R)
        va = m.sb("va", [P, KT, HEADS, OW])
        pt = m.sb("pt", [P, 4, 512])
        ot = m.sb("ot", [P, GROUPS, S])
        w_raw = ot[:, 0:DH, :]
        rden = m.sb("rden", [P, 2, HEADS])
        o_sb = m.sb("o_sb", [P, 2, D])
        o_hi = m.sb("o_hi", [P, 2, DH, P], F32R)
        o_lo = m.sb("o_lo", [P, 2, DH, P], F32R)
        bank = m.ps("bank", [P, 8, 512])
        ln = LayerNorm(m, "ln", consts, NT)
        route = Route(nc, m, consts, rows, count0)
        row = route.row[:, 0]

        names = """w_in w_hi_done w_lo_done zero_done x_loaded res_loaded xt_t xt_hi_done xt_lo_done
            kv_p kv_act kp_lo km_t km_done kz_t kz_done q_p q_act q_lo qh_t qh_done s_p s_max qp_t qp_done
            st_p exp_done pv_p ot_done on_t norm_r norm_done of_t of_hi of_lo out_p"""
        g = {n: m.sem(n) for n in names.split()}
        held = m.sem("held")
        HALVES = 2
        XT = DH * HALVES
        pairs_of = [2 if t % 2 == 0 else 4 for t in range(NT)]
        SP_N = sum(pairs_of)
        UNITS = 3
        U = HEADS * UNITS
        count_ps = bank[:, 5, 0:2 * NT].rearrange("p (a t) -> p a t", a=2)

        with nc.Block() as block:

            @block.sync
            def _(sp):
                def load(i):
                    sp.wait_ge(ln.done, NT * i)
                    sp.sem_inc(held, 1)
                    sp.dma_start(x_in[:, :, :], x[bass.ds(i * S, S), :].rearrange("(t p) c -> p t c", p=P)).then_inc(g["x_loaded"], 16)

                def load_res(i):
                    sp.wait_ge(route.x_done, NT * i)
                    sp.sem_inc(held, 1)
                    sp.dma_start(x_res[:, :, :], x[bass.ds(i * S, S), :].rearrange("(t p) c -> p t c", p=P)).then_inc(g["res_loaded"], 16)

                for n, w in enumerate((wq, wk, wv, wo)):
                    sp.dma_start(w_raw[:, :, n * D:(n + 1) * D], w.rearrange("(c p) n -> p c n", p=P)).then_inc(g["w_in"], 16)
                route.load(sp, gate_w)
                load(0)
                with sp.Fori(0, B - 1) as i:
                    load_res(i)
                    load(i + 1)
                load_res(B - 1)
                route.sync_end(nc, sp, B)

            @block.gpsimd
            def _(pool):
                route.prepare_pool(nc, pool)
                ln.power(nc, pool, 0)
                with pool.Fori(0, B - 1) as i:
                    ln.power(nc, pool, i + 1)
                    route.ln.power(nc, pool, i)
                    route.pool(nc, pool, i)
                route.ln.power(nc, pool, B - 1)
                route.pool(nc, pool, B - 1)
                pool.wait_ge(route.sent, 16 * NT * B)

            @block.tensor
            def _(pe):
                mm = nc.tensor.matmul

                def xt(i, chunks=range(XT)):
                    for c in chunks:
                        half, d = divmod(c, DH)
                        if c == 0:
                            pe.wait_ge(ln.done, NT * i + NT)
                        if c >= 2:
                            pe.wait_ge(g["xt_lo_done"], XT * i + c - 1)
                        for t in range(4):
                            last = nc.tensor.transpose(bank[:, 6 + c % 2, t * P:(t + 1) * P],
                                                       xn[:, 4 * half + t, d * P:(d + 1) * P], consts.ident[:, :])
                        last.then_inc(g["xt_t"], 1)

                def project(out, t, w):
                    terms = [(a, b, d) for d in range(DH) for a, b in ((xt_hi, w_lo), (xt_lo, w_hi), (xt_hi, w_hi))]
                    for n, (a, b, d) in enumerate(terms):
                        last = mm(out, a[:, d, t * P:(t + 1) * P], b[:, w, d, :], start=n == 0, stop=n == len(terms) - 1)
                    return last

                def keys(i):
                    for kt in range(KT):
                        if kt == 0:
                            pe.wait_ge(g["xt_lo_done"], XT * i + DH)
                        project(bank[:, 2 * kt, 0:D], kt, 1)
                        project(bank[:, 2 * kt + 1, 0:D], kt, 2).then_inc(g["kv_p"], 1)
                    for kt in range(KT):
                        pe.wait_ge(g["kp_lo"], KT * i + kt + 1)
                        if kt:
                            pe.wait_ge(g["km_done"], 2 * KT * i + 2)
                        for e in range(2):
                            last = nc.tensor.transpose(bank[:, 7, e * P:(e + 1) * P], f32(kc[:, e * P:(e + 1) * P]), consts.ident[:, :])
                        last.then_inc(g["km_t"], 1)
                        for h in range(2):
                            if kt + h:
                                pe.wait_ge(g["kz_done"], 4 * KT * i + 4 * kt + 2 * h)
                            for p in range(4):
                                last = nc.tensor.transpose(bank[:, 6, p * P:(p + 1) * P],
                                                           f32(kp[:, 2 * (4 * h + p):2 * (4 * h + p) + 2, :].rearrange("p a b -> p (a b)")), consts.ident[:, :])
                            last.then_inc(g["kz_t"], 1)

                def q_project(i, t):
                    if t == 0:
                        pe.wait_ge(g["xt_lo_done"], XT * i + XT)
                        pe.wait_ge(route.x_done, NT * i)
                    else:
                        pe.wait_ge(g["q_lo"], NT * i + t)
                        if t == 2:
                            pe.wait_ge(route.step, 9 * i)
                    project(bank[:, 5, 0:D], t, 0).then_inc(g["q_p"], 1)

                def q_heads(i, t):
                    pe.wait_ge(g["q_act"], 2 * (NT * i + t) + 2)
                    if t:
                        pe.wait_ge(g["qh_done"], NT * i + t)
                    for e in range(2):
                        last = nc.tensor.transpose(bank[:, 4, e * P:(e + 1) * P], f32(qc[:, t % 2, e * P:(e + 1) * P]), consts.ident[:, :])
                    last.then_inc(g["qh_t"], 1)

                def scores(i, t):
                    pe.wait_ge(g["qh_done"], NT * i + t + 1)
                    if t == 0:
                        pe.wait_ge(g["km_done"], 2 * KT * i + 2 * KT)
                    nk = P * (1 + t % 2)
                    per = 512 // nk
                    for j in range(pairs_of[t]):
                        n = sum(pairs_of[:t]) + j
                        if n >= 2:
                            pe.wait_ge(g["s_max"], SP_N * i + n - 1)
                        for b in range(2):
                            h0 = (2 * j + b) * per
                            out = bank[:, 2 * (n % 2) + b, :]
                            mm(out, consts.ident_bf[:, :], consts.mask_q[:, t % 2, :], start=True, stop=False)
                            last = mm(out.rearrange("p (h k) -> p h k", k=nk), qht[:, t % 2, h0 // 8, :],
                                      km[:, h0 // 8, h0 % 8:h0 % 8 + per, 0:nk], start=False, stop=True)
                        last.then_inc(g["s_p"], 1)

                def q_packed(i, t):
                    for h in range(2):
                        if h == 0:
                            pe.wait_ge(g["s_max"], SP_N * i + sum(pairs_of[:t + 1]))
                            pe.wait_ge(g["q_lo"], NT * i + t + 1)
                        if t == 0:
                            pe.wait_ge(g["kz_done"], 4 * KT * (i + 1))
                            pe.wait_ge(g["km_done"], 2 * KT * (i + 1))
                        else:
                            pe.wait_ge(g["qp_done"], 2 * (NT * i + t) + h - 1)
                        for p in range(4):
                            last = nc.tensor.transpose(bank[:, 6 + h, p * P:(p + 1) * P],
                                                       f32(qp[:, t % 2, 2 * (4 * h + p):2 * (4 * h + p) + 2, :].rearrange("p a b -> p (a b)")), consts.ident[:, :])
                        last.then_inc(g["qp_t"], 1)

                qpt_v = qpt[:, :, :].rearrange("p a (w e c) -> p a w e c", e=2, c=P)

                def unit(i, n):
                    h, u = divmod(n, UNITS)
                    kt, odd, masked = ((0, 0, True), (0, 1, False), (1, 1, True))[u]
                    if n == 0:
                        pe.wait_ge(g["qp_done"], 2 * NT * (i + 1))
                    if n >= 4:
                        pe.wait_ge(g["exp_done"], U * i + n - 3)
                    out = bank[:, n % 4, :]
                    if masked:
                        mm(out, consts.ident_bf[:, :], consts.mask_k[:, :], start=True, stop=False)
                    mm(out.rearrange("p (w c) -> p w c", c=P), kz[:, h, kt * P:(kt + 1) * P], qpt_v[:, h // 2, :, odd, :],
                       start=not masked, stop=True).then_inc(g["st_p"], 1)

                def values(i, n):
                    h, u = divmod(n, UNITS)
                    q, r = divmod(h, 4)
                    if r == 0 and u == 0 and q >= 2:
                        pe.wait_ge(g["ot_done"], 2 * GROUPS * i + 2 * q - 2)
                    pe.wait_ge(g["exp_done"], U * i + n + 1)
                    odd = 1 if u else 0
                    mm(bank[OW * r:OW * r + OW, 4 + 2 * (q % 2) + odd, :], va[:, 1 if u == 2 else 0, h, :], pt[:, n % 4, :],
                       start=u < 2, stop=u != 1).then_inc(g["pv_p"], 1)

                ot_v = ot[:, :, :].rearrange("p g (e w c) -> p g e w c", e=2, c=P)

                def heads_out(i, t):
                    if t == 0:
                        pe.wait_ge(g["ot_done"], 2 * GROUPS * (i + 1))
                    if t >= 2:
                        pe.wait_ge(g["norm_done"], NT * i + t - 1)
                    for q in range(GROUPS):
                        last = nc.tensor.transpose(bank[:, t % 2, q * P:(q + 1) * P], ot_v[:, q, t % 2, t // 2, :], consts.ident[:, :])
                    last.then_inc(g["on_t"], 1)

                def attn_t(i, t):
                    pe.wait_ge(g["norm_done"], NT * i + t + 1)
                    if t >= 2:
                        pe.wait_ge(g["of_lo"], NT * i + t - 1)
                    for d in range(DH):
                        last = nc.tensor.transpose(bank[:, 2 + t % 2, d * P:(d + 1) * P], o_sb[:, t % 2, d * P:(d + 1) * P], consts.ident[:, :])
                    last.then_inc(g["of_t"], 1)

                def out_project(i, t):
                    pe.wait_ge(g["of_lo"], NT * i + t + 1)
                    if t >= 2:
                        pe.wait_ge(route.x_done, NT * i + t - 1)
                    terms = [(a, b, d) for d in range(DH) for a, b in ((o_hi, w_lo), (o_lo, w_hi), (o_hi, w_hi))]
                    for n, (a, b, d) in enumerate(terms):
                        last = mm(bank[:, 4 + t % 2, 0:D], a[:, t % 2, d, :], b[:, 3, d, :], start=n == 0, stop=n == len(terms) - 1)
                    last.then_inc(g["out_p"], 1)

                pe.wait_ge(g["w_lo_done"], 1)
                pe.wait_ge(g["zero_done"], 5)
                def begin(i):
                    keys(i)
                    q_project(i, 0)
                    q_heads(i, 0)
                    q_project(i, 1)
                    scores(i, 0)
                    q_heads(i, 1)

                def count(i):
                    pe.wait_ge(g["q_lo"], NT * i + NT + 2)
                    route.tensor(nc, pe, i, count_ps)

                def rest(i, more):
                    for t in range(1, NT):
                        if t + 1 < NT:
                            q_project(i, t + 1)
                        scores(i, t)
                        q_packed(i, t - 1)
                        if t + 1 < NT:
                            q_heads(i, t + 1)
                    q_packed(i, NT - 1)
                    for n in range(U + 2):
                        if n < U:
                            unit(i, n)
                        if n >= 2:
                            values(i, n - 2)
                    for t in range(NT + 2):
                        if t < NT:
                            heads_out(i, t)
                        if 1 <= t <= NT:
                            attn_t(i, t - 1)
                        if t >= 2:
                            out_project(i, t - 2)
                        if more and t % 2 == 1 and t < 2 * XT:
                            xt(i + 1, [t // 2])

                xt(0)
                begin(0)
                with pe.Fori(0, B - 1) as i:
                    rest(i, True)
                    begin(i + 1)
                    count(i)
                rest(B - 1, False)
                route.tensor(nc, pe, B - 1, count_ps)

            @block.scalar
            def _(act):
                copy = lambda o, a: nc.scalar.activation(o, a, ACT.Copy)

                def xt(i, chunks=range(XT)):
                    for c in chunks:
                        half, d = divmod(c, DH)
                        act.wait_ge(g["xt_t"], XT * i + c + 1)
                        copy(xt_hi[:, d, half * 512:half * 512 + 512], bank[:, 6 + c % 2, :]).then_inc(g["xt_hi_done"], 1)

                def keys(i):
                    for kt in range(KT):
                        act.wait_ge(g["kv_p"], KT * i + kt + 1)
                        if kt:
                            act.wait_ge(g["kz_t"], 2 * KT * i + 2)
                        kb = bank[:, 2 * kt, 0:D].rearrange("p (h c) -> p h c", c=HD)
                        copy(kp[:, :, :].rearrange("p h (a c) -> p h a c", a=2)[:, :, :, 0:HD],
                             kb.unsqueeze(2).broadcast_to([P, HEADS, 2, HD]))
                        copy(kc[:, :], bank[:, 2 * kt, 0:D])
                        copy(va[:, kt, :, 0:HD], bank[:, 2 * kt + 1, 0:D].rearrange("p (h c) -> p h c", c=HD)).then_inc(g["kv_act"], 1)
                        for h in range(2):
                            act.wait_ge(g["kz_t"], 2 * KT * i + 2 * kt + h + 1)
                            for r in range(2):
                                copy(kz[HW * r:HW * r + HW, 8 * h + r:8 * h + r + 7:2, kt * P:(kt + 1) * P],
                                     bank[HW * r:HW * r + HW, 6, :].rearrange("p (a k) -> p a k", k=P)).then_inc(g["kz_done"], 1)

                def q_copy(i, t):
                    act.wait_ge(g["q_p"], NT * i + t + 1)
                    if t >= 2:
                        act.wait_ge(g["qp_t"], 2 * (NT * i + t) - 2)
                    src = bank[:, 5, 0:D].rearrange("p (h c) -> p h c", c=HD)
                    copy(qp[:, t % 2, :, 0:2 * HD].rearrange("p h (a c) -> p h a c", a=2),
                         src.unsqueeze(2).broadcast_to([P, HEADS, 2, HD])).then_inc(g["q_act"], 1)
                    copy(qc[:, t % 2, :], bank[:, 5, 0:D]).then_inc(g["q_act"], 1)

                def q_heads(i, t):
                    act.wait_ge(g["qh_t"], NT * i + t + 1)
                    if t >= 2:
                        act.wait_ge(g["s_p"], SP_N * i + sum(pairs_of[:t - 1]))
                    copy(qht[:, t % 2, :, :], bank[:, 4, 0:2 * P].rearrange("p (e c) -> p e c", c=P)).then_inc(g["qh_done"], 1)

                def q_packed(i, t):
                    for h in range(2):
                        act.wait_ge(g["qp_t"], 2 * (NT * i + t) + h + 1)
                        copy(qpt[:, 4 * h:4 * h + 4, t * P:(t + 1) * P], bank[:, 6 + h, :].rearrange("p (a k) -> p a k", k=P)).then_inc(g["qp_done"], 1)

                act.wait_ge(g["w_lo_done"], 1)
                def begin(i):
                    keys(i)
                    for t in range(2):
                        q_copy(i, t)
                        q_heads(i, t)

                def rest(i, more):
                    for t in range(1, NT):
                        if t + 1 < NT:
                            q_copy(i, t + 1)
                            q_heads(i, t + 1)
                        q_packed(i, t - 1)
                    q_packed(i, NT - 1)
                    for n in range(U):
                        act.wait_ge(g["st_p"], U * i + n + 1)
                        if n >= 4:
                            act.wait_ge(g["pv_p"], U * i + n - 3)
                        nc.scalar.activation(pt[:, n % 4, :], bank[:, n % 4, :], ACT.Exp, scale=HD ** -0.5).then_inc(g["exp_done"], 1)
                    for t in range(NT):
                        act.wait_ge(g["of_t"], NT * i + t + 1)
                        if t >= 2:
                            act.wait_ge(g["out_p"], NT * i + t - 1)
                        copy(o_hi[:, t % 2, :, :], bank[:, 2 + t % 2, 0:D].rearrange("p (d c) -> p d c", c=P)).then_inc(g["of_hi"], 1)
                        if more and t % 2 == 0:
                            xt(i + 1, [t // 2])

                xt(0)
                begin(0)
                with act.Fori(0, B - 1) as i:
                    rest(i, True)
                    begin(i + 1)
                rest(B - 1, False)

            @block.vector
            def _(dve):
                tt = nc.vector.tensor_tensor

                def norm_in(i):
                    dve.wait_ge(g["x_loaded"], 16 * i + 16)
                    ln.stats(nc, dve, i, x_in)
                    dve.wait_ge(g["xt_t"], XT * i)
                    ln.apply(nc, dve, i, x_in, xn)

                dve.wait_ge(g["w_in"], 64)
                raw = w_raw.rearrange("p d (w n) -> p w d n", n=D)
                for w in range(4):
                    nc.vector.tensor_copy(w_hi[:, w, :, :], raw[:, w]).then_inc(g["w_hi_done"], 1)
                dve.wait_ge(g["w_hi_done"], 4)
                for w in range(4):
                    last = tt(w_lo[:, w, :, :], raw[:, w], f32(w_hi[:, w, :, :]), ALU.subtract)
                last.then_inc(g["w_lo_done"], 1)
                nc.vector.memset(f32(qp[:, :, :, :]), 0.0).then_inc(g["zero_done"], 1)
                nc.vector.memset(f32(kp[:, :, :]), 0.0).then_inc(g["zero_done"], 1)
                nc.vector.memset(f32(kz[:, :, :]), 0.0).then_inc(g["zero_done"], 1)
                nc.vector.memset(va[:, :, :, :], 0.0).then_inc(g["zero_done"], 1)
                dve.wait_ge(g["zero_done"], 4)
                nc.vector.memset(f32(kp[:, :, 3 * HD:3 * HD + 1]), 1.0)
                nc.vector.memset(va[:, :, :, HD:HD + 1], 1.0).then_inc(g["zero_done"], 1)
                route.prepare(nc, dve)
                norm_in(0)

                def xt(i, chunks=range(XT)):
                    for c in chunks:
                        half, d = divmod(c, DH)
                        dve.wait_ge(g["xt_hi_done"], XT * i + c + 1)
                        tt(xt_lo[:, d, half * 512:half * 512 + 512], bank[:, 6 + c % 2, :],
                           f32(xt_hi[:, d, half * 512:half * 512 + 512]), ALU.subtract).then_inc(g["xt_lo_done"], 1)

                def keys(i):
                    for kt in range(KT):
                        dve.wait_ge(g["kv_act"], KT * i + kt + 1)
                        tt(kp[:, :, HD:2 * HD], bank[:, 2 * kt, 0:D].rearrange("p (h c) -> p h c", c=HD),
                           f32(kp[:, :, 0:HD]), ALU.subtract).then_inc(g["kp_lo"], 1)
                        dve.wait_ge(g["km_t"], KT * i + kt + 1)
                        for e in range(2):
                            tt(km[:, e, :, kt * P:(kt + 1) * P],
                               bank[:, 7, e * P:(e + 1) * P].unsqueeze(1).broadcast_to([P, 8, P]),
                               consts.head_rows[:, :].unsqueeze(2).broadcast_to([P, 8, P]), ALU.mult).then_inc(g["km_done"], 1)

                def q_low(i, t):
                    dve.wait_ge(g["q_act"], 2 * (NT * i + t) + 2)
                    tt(qp[:, t % 2, :, 2 * HD:3 * HD], bank[:, 5, 0:D].rearrange("p (h c) -> p h c", c=HD),
                       f32(qp[:, t % 2, :, 0:HD]), ALU.subtract).then_inc(g["q_lo"], 1)

                def greatest(i, t):
                    nk = P * (1 + t % 2)
                    hp = 1024 // nk
                    for j in range(pairs_of[t]):
                        n = sum(pairs_of[:t]) + j
                        dve.wait_ge(g["s_p"], SP_N * i + n + 1)
                        if t >= 2 and j == 0:
                            dve.wait_ge(g["qp_t"], 2 * (NT * i + t) - 2)
                        nc.vector.tensor_reduce(
                            qp[:, t % 2, j * hp:(j + 1) * hp, 3 * HD:3 * HD + 1].rearrange("p h a -> p (h a)"),
                            bank[:, 2 * (n % 2):2 * (n % 2) + 2, :].rearrange("p b (h k) -> p (b h) k", k=nk),
                            AX.X, ALU.max, negate=True).then_inc(g["s_max"], 1)

                def rest(i, more):
                    for t in range(1, NT):
                        greatest(i, t)
                        if t + 1 < NT:
                            q_low(i, t + 1)
                    if more:
                        norm_in(i + 1)
                    for q in range(GROUPS):
                        for e in range(2):
                            dve.wait_ge(g["pv_p"], U * i + 4 * UNITS * (q + 1))
                            nc.vector.tensor_copy(ot[:, q, e * 512:e * 512 + 512], bank[:, 4 + 2 * (q % 2) + e, :]).then_inc(g["ot_done"], 1)

                    def norm_out(t):
                        dve.wait_ge(g["on_t"], NT * i + t + 1)
                        v = bank[:, t % 2, :].rearrange("p (h c) -> p h c", c=OW)
                        if t >= 2:
                            dve.wait_ge(g["norm_done"], NT * i + t - 1)
                        nc.vector.reciprocal(rden[:, t % 2, :].unsqueeze(2), v[:, :, HD:HD + 1]).then_inc(g["norm_r"], 1)
                        dve.wait_ge(g["norm_r"], NT * i + t + 1)
                        if t >= 2:
                            dve.wait_ge(g["of_t"], NT * i + t - 1)
                        tt(o_sb[:, t % 2, :].rearrange("p (h c) -> p h c", c=HD), v[:, :, 0:HD],
                           rden[:, t % 2, :].unsqueeze(2).broadcast_to([P, HEADS, HD]), ALU.mult).then_inc(g["norm_done"], 1)

                    def attn_low(t):
                        dve.wait_ge(g["of_hi"], NT * i + t + 1)
                        if t >= 2:
                            dve.wait_ge(g["out_p"], NT * i + t - 1)
                        tt(o_lo[:, t % 2, :, :], bank[:, 2 + t % 2, 0:D].rearrange("p (d c) -> p d c", c=P),
                           f32(o_hi[:, t % 2, :, :]), ALU.subtract).then_inc(g["of_lo"], 1)

                    def new_x(t):
                        dve.wait_ge(g["out_p"], NT * i + t + 1)
                        if t == 0:
                            dve.wait_ge(g["res_loaded"], 16 * i + 16)
                            dve.wait_ge(route.sent, 16 * NT * i)
                        tt(row[:, t, 0:D], bank[:, 4 + t % 2, 0:D], x_res[:, t, :], ALU.add).then_inc(route.x_done, 1)

                    for t in range(NT + 2):
                        if t < NT:
                            norm_out(t)
                        if 1 <= t <= NT:
                            attn_low(t - 1)
                        if t >= 2:
                            new_x(t - 2)
                        if more and t % 2 == 1 and t < 2 * XT:
                            xt(i + 1, [t // 2])
                    route.vector_stats(nc, dve, i)

                def begin(i, route_of):
                    keys(i)
                    q_low(i, 0)
                    if route_of is not None:
                        route.vector_norm(nc, dve, route_of)
                    greatest(i, 0)
                    q_low(i, 1)
                    if route_of is not None:
                        route.vector_choose(nc, dve, route_of)
                        route.vector_slots(nc, dve, route_of, count_ps)

                xt(0)
                begin(0, None)
                with dve.Fori(0, B - 1) as i:
                    rest(i, True)
                    begin(i + 1, i)
                rest(B - 1, False)
                route.vector_norm(nc, dve, B - 1)
                route.vector_choose(nc, dve, B - 1)
                route.vector_slots(nc, dve, B - 1, count_ps)
                route.vector_end(nc, dve, B)


ORDER = 2
FREQS = 3
ENC = 2 * FREQS + 1
FO = 64
BLK = 32
NBLK = S // BLK
LAGS = S // P
PADB = 3
BW = NBLK + 4
SEQW = B * BW
FW = (P + BLK) * LAGS
CH = 4
CHUNKS = BLK // CH


def filters(nc, tag, times, phases, freqs, w1, b1, w2, b2, w3, b3, decay, arranged):
    TWO_PI = 6.283185
    ROUND = 1.5 * 2 ** 23
    with ExitStack() as ctx:
        m = Memory(nc, ctx, tag)
        t_row = m.sb("t_row", [P, S])
        ph = m.sb("ph", [ENC, 3])
        fr = m.sb("fr", [ENC, ORDER])
        turn = m.sb("turn", [ENC, S])
        near = m.sb("near", [ENC, S])
        enc = m.sb("enc", [ENC, S])
        w1_sb = m.sb("w1", [ENC, ORDER, FO])
        w2_sb = m.sb("w2", [FO, ORDER, FO])
        w3_sb = m.sb("w3", [FO, ORDER, D])
        b12 = m.sb("b12", [FO, 2, ORDER])
        b3_sb = m.sb("b3", [P, ORDER, DH])
        dec = m.sb("dec", [P, ORDER, DH])
        ndec = m.sb("ndec", [P, ORDER, DH])
        h1 = m.sb("h1", [FO, S])
        h2 = m.sb("h2", [FO, S])
        win = m.sb("win", [P, DH, S])
        flt = m.sb("flt", [P, DH, S + BLK])
        arr = m.sb("arr", [P, DH, P + BLK, LAGS])
        h_ps = m.ps("h_ps", [P, 2, 512])
        f_ps = m.ps("f_ps", [P, DH, 2, 512])
        loaded, fr_set, turned, enc_done, l1_p, l1_done, l2_p, l2_done, l3_p, win_done, flt_done, zeroed, arr_done, \
            stored, ndec_done = (m.sem(n) for n in ("loaded fr_set turned enc_done l1_p l1_done l2_p l2_done l3_p win_done "
                                                    "flt_done zeroed arr_done stored ndec_done").split())
        LOADS = 13

        with nc.Block() as block:

            @block.sync
            def _(sp):
                sp.dma_start(t_row[:, :], times.broadcast_to([P, S])).then_inc(loaded, 16)
                sp.dma_start(ph[:, :], phases).then_inc(loaded, 16)
                for k in range(2):
                    sp.dma_start(fr[FREQS * k:FREQS * k + FREQS, :], freqs).then_inc(loaded, 16)
                sp.dma_start(w1_sb[:, :, :], w1.rearrange("o k n -> k o n")).then_inc(loaded, 16)
                sp.dma_start(w2_sb[:, :, :], w2.rearrange("o k n -> k o n")).then_inc(loaded, 16)
                sp.dma_start(w3_sb[:, :, :], w3.rearrange("o k n -> k o n")).then_inc(loaded, 16)
                sp.dma_start(b12[:, 0, :], b1).then_inc(loaded, 16)
                sp.dma_start(b12[:, 1, :], b2).then_inc(loaded, 16)
                sp.dma_start(b3_sb[:, :, :], b3).then_inc(loaded, 16)
                sp.dma_start(dec[:, :, :], decay).then_inc(loaded, 16)
                sp.dma_start(fr[2 * FREQS:ENC, :], freqs[0:1, :]).then_inc(loaded, 16)
                sp.dma_start(win[:, 0, :], times.broadcast_to([P, S])).then_inc(loaded, 16)
                for o in range(ORDER):
                    for d in range(DH):
                        sp.wait_ge(arr_done, DH * o + d + 1)
                        for q in range(4):
                            sp.dma_start(arranged[o, d, :, q, :, :], arr[BLK * q:BLK * q + BLK, d, :, :].rearrange("p a b -> p (a b)")).then_inc(stored, 16)
                sp.wait_ge(stored, 64 * ORDER * DH)

            @block.vector
            def _(dve):
                dve.wait_ge(loaded, 16 * LOADS)
                nc.vector.tensor_scalar(fr[:, :], fr[:, :], ph[:, 2:3], None, ALU.mult).then_inc(fr_set, 1)
                dve.wait_ge(fr_set, 1)
                nc.vector.tensor_scalar(ndec[:, :, :], dec[:, :, :], -1.0, None, ALU.mult).then_inc(ndec_done, 1)
                nc.vector.memset(flt[:, :, S:S + BLK], 0.0).then_inc(zeroed, 1)
                dve.wait_ge(ndec_done, 1)
                nc.vector.tensor_tensor(ndec[:, :, :], ndec[:, :, :], dec[:, :, :], ALU.min).then_inc(ndec_done, 1)
                dve.wait_ge(ndec_done, 2)
                nc.vector.tensor_scalar(ndec[:, :, :], ndec[:, :, :], float(S), None, ALU.mult).then_inc(ndec_done, 1)
                for o in range(ORDER):
                    n = 5 * o
                    if o:
                        dve.wait_ge(l1_done, 2 * o)
                    nc.vector.tensor_scalar(turn[:, :], t_row[0:ENC, :], fr[:, o:o + 1], ph[:, 0:1], ALU.mult, ALU.add).then_inc(turned, 1)
                    dve.wait_ge(turned, n + 1)
                    nc.vector.tensor_scalar(near[:, :], turn[:, :], ROUND, None, ALU.add).then_inc(turned, 1)
                    dve.wait_ge(turned, n + 2)
                    nc.vector.tensor_scalar(near[:, :], near[:, :], -ROUND, None, ALU.add).then_inc(turned, 1)
                    dve.wait_ge(turned, n + 3)
                    nc.vector.tensor_tensor(turn[:, :], turn[:, :], near[:, :], ALU.subtract).then_inc(turned, 1)
                    dve.wait_ge(enc_done, 2 * o + 1)
                    dve.wait_ge(turned, n + 4)
                    nc.vector.tensor_scalar(turn[:, :], t_row[0:ENC, :], ph[:, 1:2], None, ALU.mult).then_inc(turned, 1)
                    dve.wait_ge(turned, n + 5)
                    nc.vector.tensor_tensor(enc[:, :], enc[:, :], turn[:, :], ALU.add).then_inc(enc_done, 1)
                    for d in range(DH):
                        dve.wait_ge(l3_p, DH * o + d + 1)
                        dve.wait_ge(win_done, DH * o + d + 1)
                        if o:
                            dve.wait_ge(arr_done, DH * (o - 1) + d + 1)
                        nc.vector.scalar_tensor_tensor(flt[:, d, 0:S], f_ps[:, d, :, :].rearrange("p a b -> p (a b)"),
                                                       b3_sb[:, o, d:d + 1], win[:, d, :], ALU.add, ALU.mult).then_inc(flt_done, 1)
                        dve.wait_ge(flt_done, DH * o + d + 1)
                        dve.wait_ge(zeroed, 1)
                        if o:
                            dve.wait_ge(stored, 64 * DH)
                        for k in range(LAGS):
                            last = nc.vector.tensor_copy(arr[:, d, :, k:k + 1].rearrange("p w a -> p (w a)"), flt[:, d, P * k:P * k + P + BLK])
                        last.then_inc(arr_done, 1)

            @block.scalar
            def _(act):
                act.wait_ge(loaded, 16 * LOADS)
                for o in range(ORDER):
                    act.wait_ge(turned, 5 * o + 4)
                    nc.scalar.activation(enc[:, :], turn[:, :], ACT.Sin, scale=TWO_PI).then_inc(enc_done, 1)
                    for h in range(2):
                        act.wait_ge(l1_p, 2 * o + h + 1)
                        nc.scalar.activation(h1[:, h * 512:h * 512 + 512], h_ps[0:FO, h, :], ACT.Gelu, bias=b12[:, 0, o:o + 1]).then_inc(l1_done, 1)
                    for h in range(2):
                        act.wait_ge(l2_p, 2 * o + h + 1)
                        nc.scalar.activation(h2[:, h * 512:h * 512 + 512], h_ps[0:FO, h, :], ACT.Gelu, bias=b12[:, 1, o:o + 1]).then_inc(l2_done, 1)
                    act.wait_ge(ndec_done, 3)
                    for d in range(DH):
                        if o:
                            act.wait_ge(flt_done, DH * (o - 1) + d + 1)
                        nc.scalar.activation(win[:, d, :], t_row[:, :], ACT.Exp, scale=ndec[:, o, d:d + 1]).then_inc(win_done, 1)

            @block.tensor
            def _(pe):
                mm = nc.tensor.matmul
                for o in range(ORDER):
                    pe.wait_ge(enc_done, 2 * o + 2)
                    if o:
                        pe.wait_ge(l2_done, 2 * o)
                    for h in range(2):
                        mm(h_ps[0:FO, h, :], w1_sb[:, o, :], enc[:, h * 512:h * 512 + 512], start=True, stop=True).then_inc(l1_p, 1)
                    for h in range(2):
                        pe.wait_ge(l1_done, 2 * o + 2)
                        mm(h_ps[0:FO, h, :], w2_sb[:, o, :], h1[:, h * 512:h * 512 + 512], start=True, stop=True).then_inc(l2_p, 1)
                    for d in range(DH):
                        pe.wait_ge(l2_done, 2 * o + 2)
                        if o:
                            pe.wait_ge(flt_done, DH * (o - 1) + d + 1)
                        for h in range(2):
                            last = mm(f_ps[:, d, h, :], w3_sb[:, o, d * P:(d + 1) * P], h2[:, h * 512:h * 512 + 512], start=True, stop=True)
                        last.then_inc(l3_p, 1)


def projections(nc, tag, consts, x, in_w, in_b, conv_w, conv_b, gate_w, gate_b, v_blocks, gates):
    MB = (ORDER + 1) * DH
    with ExitStack() as ctx:
        m = Memory(nc, ctx, tag)
        x_in = m.sb("x_in", [P, NT, D])
        xt_hi = m.sb("xt_hi", [P, DH, S], F32R)
        xt_lo = m.sb("xt_lo", [P, DH, S], F32R)
        iw_hi = m.sb("iw_hi", [P, DH, 3 * D], F32R)
        iw_lo = m.sb("iw_lo", [P, DH, 3 * D], F32R)
        gw_hi = m.sb("gw_hi", [P, ORDER, DH, D], F32R)
        gw_lo = m.sb("gw_lo", [P, ORDER, DH, D], F32R)
        cols = m.sb("cols", [P, MB + ORDER * DH * 5])
        in_bc = cols[:, 0:MB]
        cw = cols[:, MB:MB + 12].rearrange("p (o d k) -> p o d k", o=ORDER, d=DH)
        cb = cols[:, MB + 12:MB + 16].rearrange("p (o d) -> p o d", o=ORDER)
        gb = cols[:, MB + 16:MB + 20].rearrange("p (o d) -> p o d", o=ORDER)
        vb = m.sb("vb", [P, DH, BLK, B, BW])
        vt = m.sb("vt", [P, S])
        vs = m.sb("vs", [P, DH, NBLK, BLK])
        u = m.sb("u", [P, 2, S + 2])
        tap = m.sb("tap", [P, 2, S])
        xc = m.sb("xc", [P, ORDER, DH, S])
        xc_hi = m.sb("xc_hi", [P, ORDER, DH, S], F32R)
        xc_lo = m.sb("xc_lo", [P, ORDER, DH, S], F32R)
        sg = m.sb("sg", [P, 2, S])
        gate = (tap, sg)
        w_raw = xc[:, 0].rearrange("p d s -> p (d s)")
        w_raw2 = xc[:, 1].rearrange("p d s -> p (d s)")
        bank = m.ps("bank", [P, 8, 512])
        ln = LayerNorm(m, "ln", consts, NT)
        names = """w_in c_in w_hi w_lo zeroed x_loaded xt_t xt_hi_done xt_lo_done v_p v_act v_blk u_p u_act tap0 tap1
            xc_done xc_hi_done xc_lo_done g_p sg_done g_done v_put v_stored"""
        g = {n: m.sem(n) for n in names.split()}
        held = m.sem("held")
        g_stored = [[m.sem(f"g_stored{o}{d}") for d in range(DH)] for o in range(ORDER)]
        XT = 2 * DH

        with nc.Block() as block:

            @block.sync
            def _(sp):
                sp.dma_start(w_raw[:, 0:DH * 3 * D].rearrange("p (c n) -> p c n", c=DH),
                             in_w.rearrange("(c p) n -> p c n", p=P)).then_inc(g["w_in"], 16)
                for o in range(ORDER):
                    sp.dma_start(w_raw2[:, o * DH * D:(o + 1) * DH * D].rearrange("p (c n) -> p c n", c=DH),
                                 gate_w[o].rearrange("(c p) n -> p c n", p=P)).then_inc(g["w_in"], 16)
                for dst, src in ((in_bc, in_b), (cw, conv_w), (cb, conv_b), (gb, gate_b)):
                    sp.dma_start(dst, src).then_inc(g["c_in"], 16)

                def load(i):
                    if not isinstance(i, int):
                        sp.wait_ge(g["xt_t"], XT * i)
                        sp.sem_inc(held, 1)
                    sp.dma_start(x_in[:, :, :], x[bass.ds(i * S, S), :].rearrange("(t p) c -> p t c", p=P)).then_inc(g["x_loaded"], 16)

                def store(i):
                    for n in range(ORDER * DH):
                        o, d = divmod(n, DH)
                        sp.wait_ge(g["g_done"], ORDER * DH * i + n + 1)
                        sp.sem_inc(held, 1)
                        sp.dma_start(gates[o, d, :, bass.ds(i * S, S)], gate[o][:, d, :]).then_inc(g_stored[o][d], 16)

                load(0)
                with sp.Fori(0, B - 1) as i:
                    load(i + 1)
                    store(i)
                store(B - 1)
                sp.wait_ge(g["v_put"], DH * B)
                for d in range(DH):
                    sp.dma_start(v_blocks[d], vb[:, d].rearrange("p c b k -> p (c b k)")).then_inc(g["v_stored"], 16)
                sp.wait_ge(g["v_stored"], 16 * DH)
                for o in range(ORDER):
                    for d in range(DH):
                        sp.wait_ge(g_stored[o][d], 16 * B)

            @block.gpsimd
            def _(pool):
                every = vb[:, :, :, :, :].rearrange("p a b c k -> p (a b c) k")
                pool.memset(every[:, :, 0:PADB], 0.0)
                pool.memset(every[:, :, PADB + NBLK:BW], 0.0).then_inc(g["zeroed"], 1)
                ln.power(nc, pool, 0)
                with pool.Fori(0, B - 1) as i:
                    ln.power(nc, pool, i + 1)

            @block.tensor
            def _(pe):
                mm = nc.tensor.matmul

                def xt(i):
                    for c in range(XT):
                        half, d = divmod(c, DH)
                        if c == 0:
                            pe.wait_ge(ln.done, NT * i + NT)
                        pe.wait_ge(g["xt_lo_done"], XT * i + c + 1)
                        for t in range(4):
                            last = nc.tensor.transpose(bank[:, 6 + c % 2, t * P:(t + 1) * P],
                                                       x_in[:, 4 * half + t, d * P:(d + 1) * P], consts.ident[:, :])
                        last.then_inc(g["xt_t"], 1)

                def product(out, hi, lo, w_h, w_l, h, col):
                    terms = [(a, b, d) for d in range(DH) for a, b in ((w_h, lo), (w_l, hi), (w_h, hi))]
                    for n, (a, b, d) in enumerate(terms):
                        last = mm(out, a[:, d, col:col + P], b[:, d, h * 512:h * 512 + 512], start=n == 0, stop=n == len(terms) - 1)
                    return last

                def control(i, o, d, at):
                    for h in range(2):
                        last = product(bank[:, at + h, :], xt_hi, xt_lo, iw_hi, iw_lo, h, (1 + o) * D + d * P)
                    last.then_inc(g["u_p"], 1)

                def value(i, d, at):
                    for h in range(2):
                        last = product(bank[:, at + h, :], xt_hi, xt_lo, iw_hi, iw_lo, h, d * P)
                    last.then_inc(g["v_p"], 1)

                def gates_of(i, o, d, at):
                    if d == 0:
                        pe.wait_ge(g["xc_lo_done"], 4 * i + 2 * o + 2)
                    for h in range(2):
                        last = product(bank[:, at + h, :], xc_hi[:, o], xc_lo[:, o], gw_hi[:, o], gw_lo[:, o], h, d * P)
                    last.then_inc(g["g_p"], 1)

                def sequence(i, more):
                    pe.wait_ge(g["xt_lo_done"], XT * i + XT + 2)
                    pe.wait_ge(g["sg_done"], 4 * i + 1)
                    control(i, 0, 0, 0)
                    pe.wait_ge(g["sg_done"], 4 * i + 4)
                    control(i, 0, 1, 2)
                    pe.wait_ge(g["sg_done"], 4 * i + 3)
                    value(i, 0, 4)
                    pe.wait_ge(g["u_act"], 4 * i + 1)
                    value(i, 1, 0)
                    pe.wait_ge(g["u_act"], 4 * i + 2)
                    control(i, 1, 0, 2)
                    pe.wait_ge(g["v_act"], DH * i + 1)
                    control(i, 1, 1, 4)
                    pe.wait_ge(g["v_act"], DH * i + 2)
                    gates_of(i, 0, 0, 0)
                    pe.wait_ge(g["u_act"], 4 * i + 3)
                    gates_of(i, 0, 1, 2)
                    if more:
                        xt(i + 1)
                    pe.wait_ge(g["u_act"], 4 * i + 4)
                    gates_of(i, 1, 0, 4)
                    pe.wait_ge(g["sg_done"], 4 * i + 6)
                    gates_of(i, 1, 1, 2)

                pe.sem_inc(g["g_p"], 4)
                pe.wait_ge(g["w_lo"], 3)
                xt(0)
                with pe.Fori(0, B - 1) as i:
                    sequence(i, True)
                sequence(B - 1, False)

            @block.scalar
            def _(act):
                act.wait_ge(g["c_in"], 64)
                act.wait_ge(g["w_lo"], 3)
                act.wait_ge(g["zeroed"], 1)
                act.sem_inc(g["sg_done"], 4)
                both = lambda at: bank[:, at:at + 2, :].rearrange("p a b -> p (a b)")

                def xt(i):
                    for c in range(XT):
                        half, d = divmod(c, DH)
                        act.wait_ge(g["xt_t"], XT * i + c + 1)
                        nc.scalar.activation(xt_hi[:, d, half * 512:half * 512 + 512], bank[:, 6 + c % 2, :], ACT.Copy).then_inc(g["xt_hi_done"], 1)

                def control(i, o, d, at):
                    k = 2 * o + d
                    act.wait_ge(g["u_p"], 4 * i + k + 1)
                    act.wait_ge(g["xc_done"], 4 * i + o * (d + 1))
                    nc.scalar.activation(u[:, d, 1:S + 1], both(at), ACT.Identity,
                                         bias=in_bc[:, DH + k:DH + k + 1]).then_inc(g["u_act"], 1)
                    act.wait_ge(g["u_act"], 4 * i + k + 1)
                    if o == 0:
                        act.wait_ge(g_stored[0][d], 16 * i)
                    nc.scalar.activation(tap[:, d, :], u[:, d, 0:S], ACT.Identity, bias=cb[:, o, d:d + 1],
                                         scale=cw[:, o, d, 0:1]).then_inc(g["tap0"], 1)

                def value(i, d, at):
                    act.wait_ge(g["v_p"], DH * i + d + 1)
                    act.wait_ge(g["v_blk"], DH * i + d)
                    nc.scalar.activation(vt[:, :], both(at), ACT.Identity, bias=in_bc[:, d:d + 1]).then_inc(g["v_act"], 1)

                def high(i, o, d):
                    act.wait_ge(g["xc_done"], 4 * i + 2 * o + d + 1)
                    act.wait_ge(g["g_p"], 4 * i + 2 * o + 2)
                    nc.scalar.activation(xc_hi[:, o, d, :], xc[:, o, d, :], ACT.Copy).then_inc(g["xc_hi_done"], 1)

                def gates_of(i, o, d, at):
                    act.wait_ge(g["g_p"], 4 * i + 2 * o + d + 5)
                    if o == 0:
                        act.wait_ge(g["xc_done"], 4 * i + d + 3)
                    else:
                        act.wait_ge(g_stored[1][d], 16 * i)
                    nc.scalar.activation(gate[o][:, d, :], both(at), ACT.Sigmoid, bias=gb[:, o, d:d + 1]).then_inc(g["sg_done"], 1)

                def sequence(i, more):
                    control(i, 0, 0, 0)
                    control(i, 0, 1, 2)
                    high(i, 0, 0)
                    value(i, 0, 4)
                    high(i, 0, 1)
                    value(i, 1, 0)
                    control(i, 1, 0, 2)
                    control(i, 1, 1, 4)
                    high(i, 1, 0)
                    high(i, 1, 1)
                    gates_of(i, 0, 0, 0)
                    gates_of(i, 0, 1, 2)
                    if more:
                        xt(i + 1)
                    for d in range(DH):
                        act.wait_ge(g["v_blk"], DH * i + d + 1)
                        at = slice(i, i + 1) if isinstance(i, int) else bass.ds(i, 1)
                        nc.scalar.activation(vb[:, d, :, at, PADB:PADB + NBLK].rearrange("p c b k -> p c (b k)"),
                                             vs[:, d, :, :].rearrange("p k c -> p c k"), ACT.Copy).then_inc(g["v_put"], 1)
                    gates_of(i, 1, 0, 4)
                    gates_of(i, 1, 1, 2)

                xt(0)
                with act.Fori(0, B - 1) as i:
                    sequence(i, True)
                sequence(B - 1, False)

            @block.vector
            def _(dve):
                tt = nc.vector.tensor_tensor
                stt = nc.vector.scalar_tensor_tensor
                dve.sem_inc(g["xt_lo_done"], 2)

                def stats(i):
                    dve.wait_ge(g["x_loaded"], 16 * i + 16)
                    ln.stats(nc, dve, i, x_in)

                dve.wait_ge(g["w_in"], 48)
                raw_i = w_raw[:, 0:DH * 3 * D].rearrange("p (c n) -> p c n", c=DH)
                raw_g = w_raw2[:, 0:ORDER * DH * D].rearrange("p (o c n) -> p o c n", o=ORDER, c=DH)
                nc.vector.tensor_copy(iw_hi[:, :, :], raw_i).then_inc(g["w_hi"], 1)
                for o in range(ORDER):
                    nc.vector.tensor_copy(gw_hi[:, o], raw_g[:, o]).then_inc(g["w_hi"], 1)
                dve.wait_ge(g["w_hi"], 3)
                tt(iw_lo[:, :, :], raw_i, f32(iw_hi[:, :, :]), ALU.subtract).then_inc(g["w_lo"], 1)
                for o in range(ORDER):
                    tt(gw_lo[:, o], raw_g[:, o], f32(gw_hi[:, o]), ALU.subtract).then_inc(g["w_lo"], 1)
                nc.vector.memset(u[:, :, :], 0.0).then_inc(g["w_hi"], 1)
                stats(0)
                ln.apply(nc, dve, 0, x_in, x_in)
                dve.wait_ge(g["w_hi"], 4)
                dve.wait_ge(g["w_lo"], 3)
                dve.wait_ge(g["zeroed"], 1)

                def xt(i):
                    for c in range(XT):
                        half, d = divmod(c, DH)
                        dve.wait_ge(g["xt_hi_done"], XT * i + c + 1)
                        tt(xt_lo[:, d, half * 512:half * 512 + 512], bank[:, 6 + c % 2, :],
                           f32(xt_hi[:, d, half * 512:half * 512 + 512]), ALU.subtract).then_inc(g["xt_lo_done"], 1)

                def control(i, o, d):
                    k = 4 * i + 2 * o + d
                    dve.wait_ge(g["tap0"], k + 1)
                    stt(xc[:, o, d, :], u[:, d, 1:S + 1], cw[:, o, d, 1:2], tap[:, d, :], ALU.mult, ALU.add).then_inc(g["tap1"], 1)
                    dve.wait_ge(g["tap1"], k + 1)
                    stt(xc[:, o, d, :], u[:, d, 2:S + 2], cw[:, o, d, 2:3], xc[:, o, d, :], ALU.mult, ALU.add).then_inc(g["xc_done"], 1)

                def low(i, o, d):
                    dve.wait_ge(g["xc_hi_done"], 4 * i + 2 * o + d + 1)
                    tt(xc_lo[:, o, d, :], xc[:, o, d, :], f32(xc_hi[:, o, d, :]), ALU.subtract).then_inc(g["xc_lo_done"], 1)

                def blocks(i, d):
                    dve.wait_ge(g["v_act"], DH * i + d + 1)
                    dve.wait_ge(g["v_put"], DH * i)
                    nc.vector.transpose(vs[:, d, :, :], vt[:, :].rearrange("p (k s) -> p k s", s=BLK)).then_inc(g["v_blk"], 1)

                def gated(i, o, d):
                    dve.wait_ge(g["sg_done"], 4 * i + 2 * o + d + 5)
                    tt(gate[o][:, d, :], gate[o][:, d, :], xc[:, o, d, :], ALU.mult).then_inc(g["g_done"], 1)

                def sequence(i, more):
                    dve.wait_ge(g["g_done"], 4 * i)
                    control(i, 0, 0)
                    control(i, 0, 1)
                    low(i, 0, 0)
                    blocks(i, 0)
                    low(i, 0, 1)
                    blocks(i, 1)
                    control(i, 1, 0)
                    control(i, 1, 1)
                    if more:
                        stats(i + 1)
                    low(i, 1, 0)
                    low(i, 1, 1)
                    if more:
                        ln.apply(nc, dve, i + 1, x_in, x_in)
                    gated(i, 0, 0)
                    gated(i, 0, 1)
                    if more:
                        xt(i + 1)
                    gated(i, 1, 0)
                    gated(i, 1, 1)

                xt(0)
                with dve.Fori(0, B - 1) as i:
                    sequence(i, True)
                sequence(B - 1, False)


def convolutions(nc, tag, arranged, v_blocks, gates, v_mid, v_out):
    ROUNDS = ORDER * DH
    PER = CHUNKS
    with ExitStack() as ctx:
        m = Memory(nc, ctx, tag)
        tp = m.sb("tp", [P, 2, 4, CH, BLK * LAGS])
        vi = m.sb("vi", [P, 2, 4, CH * SEQW])
        yc = m.sb("yc", [P, 2, BLK, B * NBLK])
        yt = m.sb("yt", [P, 2, S])
        gt = m.sb("gt", [P, 2, S])
        vn = m.sb("vn", [P, 2, S])
        vb = m.sb("vb", [P, BLK, B, BW])
        y_ps = m.ps("y_ps", [P, 4, 2, B * NBLK])
        t_loaded = [m.sem(f"t_loaded{n}") for n in range(2)]
        v_loaded = [m.sem(f"v_loaded{n}") for n in range(2)]
        y_p, y_act, yt_done, vn_done, vb_done, mid_stored, zeroed, held = (
            m.sem(n) for n in "y_p y_act yt_done vn_done vb_done mid_stored zeroed held".split())
        act_moved, dve_moved = m.sem("act_moved"), m.sem("dve_moved")
        g_loaded = [m.sem(f"g_loaded{n}") for n in range(2)]
        out_stored = [m.sem(f"out_stored{n}") for n in range(2)]

        with nc.Block() as block:

            @block.sync
            def _(sp):
                def chunk(r, c, k):
                    o, d = divmod(r, DH)
                    n = r * PER + c
                    if isinstance(c, int) and n < 2:
                        pass
                    else:
                        sp.wait_ge(y_p, n - 1)
                        sp.sem_inc(held, 1)
                    def windows():
                        src = bass.AP(arranged.tensor, r * P * FW + c * (4 * CH * FW),
                                      [[LAGS, P], [FW, 4 * CH], [1, BLK * LAGS]])
                        sp.dma_start(tp[:, k].rearrange("p q c n -> p (q c) n"), src).then_inc(t_loaded[k], 16)

                    def inputs():
                        src = bass.AP((v_mid if o else v_blocks).tensor, d * P * BLK * SEQW + c * (CH * SEQW),
                                      [[BLK * SEQW, BLK], [BLK * BLK * SEQW, 4], [1, CH * SEQW]])
                        sp.dma_start(vi[0:BLK, k], src).then_inc(v_loaded[k], 16)

                    if o and isinstance(c, int) and c == 0:
                        windows()
                        sp.wait_ge(mid_stored, 16 * (r - DH + 1))
                        inputs()
                    else:
                        inputs()
                        windows()

                for r in range(ROUNDS):
                    for k in range(2):
                        chunk(r, k, k)
                    with sp.Fori(1, PER // 2) as i:
                        for k in range(2):
                            chunk(r, i * 2 + k, k)

            @block.tensor
            def _(pe):
                for r in range(ROUNDS):
                    def pair(i, r=r):
                        for k in range(2):
                            n = r * PER + i * 2 + k
                            pe.wait_ge(t_loaded[k], 16 * (r * PER // 2) + i * 16 + 16)
                            pe.wait_ge(v_loaded[k], 16 * (r * PER // 2) + i * 16 + 16)
                            pe.wait_ge(act_moved, 2 * n + 2)
                            pe.wait_ge(dve_moved, 2 * n + 2)
                            pe.wait_ge(y_act, n * 2 + 2)
                            for c in range(CH):
                                bk, at = 2 * k + c // 2, c % 2
                                for j in range(LAGS):
                                    w = NBLK - 4 * j
                                    for q in range(4):
                                        out = y_ps[BLK * q:BLK * q + BLK, bk, at, :].rearrange("p (b i) -> p b i", b=B)[:, :, 4 * j:NBLK]
                                        lhs = tp[:, k, q, c, :].rearrange("p (w l) -> p w l", l=LAGS)[:, :, LAGS - 1 - j]
                                        rhs = vi[:, k, q, c * SEQW:(c + 1) * SEQW].rearrange("p (b i) -> p b i", b=B)[:, :, 0:w]
                                        last = nc.tensor.matmul(out, lhs, rhs, start=j == 0, stop=j == LAGS - 1, skip_group_check=True)
                            last.then_inc(y_p, 1)
                    with pe.Fori(0, PER // 2) as i:
                        pair(i)

            @block.scalar
            def _(act):
                def move(r, c, k):
                    act.wait_ge(v_loaded[k], (c - k) * 8 + (16 * (r * PER // 2) + 16))
                    for a, qs in ((1, 4), (2, 2)):
                        nc.scalar.activation(vi[BLK * a:BLK * a + BLK, k, 0:qs, 0:CH * SEQW - a],
                                             vi[0:BLK, k, 0:qs, a:CH * SEQW], ACT.Copy).then_inc(act_moved, 1)

                def sums(r, c, k):
                    act.wait_ge(y_p, c + (r * PER + 1))
                    for h in range(2):
                        at = c * CH + 2 * h
                        at = slice(at, at + 2) if isinstance(c, int) else bass.ds(at, 2)
                        nc.scalar.activation(yc[:, r % 2, at, :], y_ps[:, 2 * k + h, :, :], ACT.Copy).then_inc(y_act, 1)

                act.sem_inc(y_act, 4)
                move(0, 0, 0)
                for r in range(ROUNDS):
                    if r >= 2:
                        act.wait_ge(yt_done, B * (r - 1))
                    with act.Fori(0, PER // 2 - 1) as i:
                        for k in range(2):
                            move(r, i * 2 + (k + 1), 1 - k)
                            sums(r, i * 2 + k, k)
                    move(r, PER - 1, 1)
                    sums(r, PER - 2, 0)
                    if r + 1 < ROUNDS:
                        move(r + 1, 0, 0)
                    sums(r, PER - 1, 1)

            @block.gpsimd
            def _(pool):
                every = vb[:, :, :, :].rearrange("p a b k -> p (a b) k")
                pool.memset(every[:, :, 0:PADB], 0.0)
                pool.memset(every[:, :, PADB + NBLK:BW], 0.0).then_inc(zeroed, 1)
                for r in range(ROUNDS):
                    o, d = divmod(r, DH)

                    def load(b, k, r=r, o=o, d=d):
                        pool.wait_ge(vn_done, B * r + b + 1)
                        pool.sem_inc(held, 1)
                        pool.dma_start(gt[:, k, :], gates[o, d, :, bass.ds(b * S, S)]).then_inc(g_loaded[k], 16)

                    def store(b, k, r=r, d=d):
                        pool.wait_ge(vn_done, B * r + b + 3)
                        pool.sem_inc(held, 1)
                        pool.dma_start(v_out[d, :, bass.ds(b * S, S)], vn[:, k, :]).then_inc(out_stored[k], 16)

                    with pool.Fori(0, B // 2) as i:
                        for k in range(2):
                            load(i * 2 + k, k)
                        for k in range(2):
                            if o:
                                store(i * 2 + k, k)
                    if o == 0:
                        pool.wait_ge(vb_done, B * (r + 1))
                        pool.dma_start(v_mid[d], vb[:, :, :, :].rearrange("p a b c -> p (a b c)")).then_inc(mid_stored, 16)
                for k in range(2):
                    pool.wait_ge(out_stored[k], 16 * (B // 2) * DH)
                pool.wait_ge(mid_stored, 16 * DH)

            @block.vector
            def _(dve):
                dve.sem_inc(vn_done, 2)
                dve.wait_ge(zeroed, 1)

                def move(n):
                    k = n % 2
                    dve.wait_ge(v_loaded[k], 16 * (n // 2) + 16)
                    for a, qs in ((3, 0), (2, 2)):
                        nc.vector.tensor_copy(vi[BLK * a:BLK * a + BLK, k, qs:4, 0:CH * SEQW - a],
                                              vi[0:BLK, k, qs:4, a:CH * SEQW]).then_inc(dve_moved, 1)

                def sequence(r, b):
                    o, d = divmod(r, DH)
                    k = b % 2
                    n = B * r + b
                    if b == 0:
                        dve.wait_ge(y_act, 4 + 2 * PER * (r + 1))
                        if o == 0 and r:
                            dve.wait_ge(mid_stored, 16 * r)
                    dve.wait_ge(vn_done, n + 1)
                    nc.vector.transpose(yt[:, k, :].rearrange("p (i c) -> p i c", c=BLK),
                                        yc[:, r % 2, :, b * NBLK:(b + 1) * NBLK].rearrange("p c i -> p i c")).then_inc(yt_done, 1)
                    dve.wait_ge(yt_done, n + 1)
                    dve.wait_ge(g_loaded[k], 16 * (B // 2) * r + (b - k) * 8 + 16)
                    if o:
                        dve.wait_ge(out_stored[k], 16 * (B // 2) * (r - DH) + (b - k) * 8)
                    else:
                        dve.wait_ge(vb_done, n)
                    nc.vector.tensor_tensor(vn[:, k, :].rearrange("p (i s) -> p i s", s=BLK),
                                            yt[:, k, :].rearrange("p (i s) -> p i s", s=BLK)[:, :, ::-1],
                                            gt[:, k, :].rearrange("p (i s) -> p i s", s=BLK), ALU.mult).then_inc(vn_done, 1)
                    if o == 0:
                        dve.wait_ge(vn_done, n + 3)
                        nc.vector.transpose(vb[:, :, b, PADB:PADB + NBLK].rearrange("p c k -> p k c"),
                                            vn[:, k, :].rearrange("p (k s) -> p k s", s=BLK)).then_inc(vb_done, 1)

                after = (1, 1, 2, 1, 2, 1, 0, 0)
                move(0)
                for r in range(ROUNDS):
                    for c in range(PER):
                        if r * PER + c + 1 < ROUNDS * PER:
                            move(r * PER + c + 1)
                        if r:
                            for b in range(sum(after[:c]), sum(after[:c + 1])):
                                sequence(r - 1, b)
                for b in range(B):
                    sequence(ROUNDS - 1, b)


def hyena_out(nc, tag, consts, x, v, out_w, out_b, gate_w, rows, count0):
    with ExitStack() as ctx:
        m = Memory(nc, ctx, tag)
        x_res = m.sb("x_res", [P, 2, NT, D])
        vt = m.sb("vt", [P, 2, DH, S])
        v_hi = m.sb("v_hi", [P, 2, DH, S], F32R)
        v_lo = m.sb("v_lo", [P, 2, DH, S], F32R)
        w_hi = m.sb("w_hi", [P, DH, D], F32R)
        w_lo = m.sb("w_lo", [P, DH, D], F32R)
        w_raw = m.sb("w_raw", [P, DH, D])
        brow = m.sb("brow", [P, D])
        bank = m.ps("bank", [P, NT // 2, 2, D])
        route_ps = m.ps("route_ps", [P, 512])
        route = Route(nc, m, consts, rows, count0, buffers=2)
        w_in, w_hi_done, w_lo_done, v_hi_done, v_lo_done, res_done, out_p, held = (
            m.sem(n) for n in "w_in w_hi_done w_lo_done v_hi_done v_lo_done res_done out_p held".split())
        x_loaded = [m.sem(f"x_loaded{k}") for k in range(2)]
        v_loaded = [m.sem(f"v_loaded{k}") for k in range(2)]

        count_ps = route_ps[:, 0:2 * NT].rearrange("p (a t) -> p a t", a=2)

        def sequences(engine, step):
            with engine.Fori(0, (B - 2) // 2) as i:
                for k in range(2):
                    step(i * 2 + (1 + k), (1 + k) % 2)

        with nc.Block() as block:

            @block.sync
            def _(sp):
                sp.dma_start(w_raw[:, :, :], out_w.rearrange("(c p) n -> p c n", p=P)).then_inc(w_in, 16)
                sp.dma_start(brow[:, :], out_b.rearrange("(a n) -> a n", a=1).broadcast_to([P, D])).then_inc(w_in, 16)
                route.load(sp, gate_w)

                def load_v(b, k):
                    sp.dma_start(vt[:, k], v[:, :, bass.ds(b * S, S)].rearrange("d p s -> p d s")).then_inc(v_loaded[k], 16)

                def load_x(b, k):
                    sp.dma_start(x_res[:, k], x[bass.ds(b * S, S), :].rearrange("(t p) c -> p t c", p=P)).then_inc(x_loaded[k], 16)

                for k in range(2):
                    load_v(k, k)
                    load_x(k, k)
                with sp.Fori(1, B // 2) as i:
                    for k in range(2):
                        b = i * 2 + k
                        sp.wait_ge(v_lo_done, b - 1)
                        sp.sem_inc(held, 1)
                        load_v(b, k)
                        sp.wait_ge(route.x_done, NT * b - NT)
                        sp.sem_inc(held, 1)
                        load_x(b, k)
                route.sync_end(nc, sp, B)

            @block.gpsimd
            def _(pool):
                route.prepare_pool(nc, pool)
                route.ln.power(nc, pool, 0)

                def step(i, k):
                    route.ln.power(nc, pool, i)
                    route.pool(nc, pool, i - 1, 1 - k)
                sequences(pool, step)
                step(B - 1, (B - 1) % 2)
                route.pool(nc, pool, B - 1, (B - 1) % 2)
                pool.wait_ge(route.sent, 16 * NT * B)

            @block.tensor
            def _(pe):
                def products(i, k):
                    pe.wait_ge(v_lo_done, i + 1)
                    terms = [(a, c, d) for d in range(DH) for a, c in ((v_hi, w_lo), (v_lo, w_hi), (v_hi, w_hi))]
                    for t in range(NT):
                        if t % 2 == 0 and not (isinstance(i, int) and i == 0):
                            pe.wait_ge(route.x_done, NT * i - NT + t + 2)
                        for n, (a, c, d) in enumerate(terms):
                            last = nc.tensor.matmul(bank[:, t // 2, t % 2, :], a[:, k, d, t * P:(t + 1) * P], c[:, d, :],
                                                    start=n == 0 and t % 2 == 0, stop=n == len(terms) - 1, skip_group_check=True)
                        last.then_inc(out_p, 1)

                def step(i, k):
                    products(i, k)
                    route.tensor(nc, pe, i - 1, count_ps)

                pe.wait_ge(w_lo_done, 1)
                products(0, 0)
                sequences(pe, step)
                step(B - 1, (B - 1) % 2)
                route.tensor(nc, pe, B - 1, count_ps)

            @block.scalar
            def _(act):
                def high(i, k):
                    act.wait_ge(v_loaded[k], (i - k) * 8 + 16)
                    if not isinstance(i, int):
                        act.wait_ge(out_p, NT * i - NT)
                    nc.scalar.activation(v_hi[:, k], vt[:, k], ACT.Copy).then_inc(v_hi_done, 1)

                for k in range(2):
                    high(k, k)
                with act.Fori(1, B // 2) as i:
                    for k in range(2):
                        high(i * 2 + k, k)

            @block.vector
            def _(dve):
                tt = nc.vector.tensor_tensor
                dve.wait_ge(w_in, 32)
                nc.vector.tensor_copy(w_hi[:, :, :], w_raw[:, :, :]).then_inc(w_hi_done, 1)
                dve.wait_ge(w_hi_done, 1)
                tt(w_lo[:, :, :], w_raw[:, :, :], f32(w_hi[:, :, :]), ALU.subtract).then_inc(w_lo_done, 1)

                def low(i, k):
                    dve.wait_ge(v_hi_done, i + 1)
                    tt(v_lo[:, k], vt[:, k], f32(v_hi[:, k]), ALU.subtract).then_inc(v_lo_done, 1)

                    dve.wait_ge(x_loaded[k], (i - k) * 8 + 16)
                    tt(x_res[:, k], x_res[:, k], brow[:, :].unsqueeze(1).broadcast_to([P, NT, D]), ALU.add).then_inc(res_done, 1)

                def sums(i, k):
                    if not isinstance(i, int) or i:
                        dve.wait_ge(route.sent, 16 * NT * i - 16 * NT)
                    for t in range(0, NT, 2):
                        dve.wait_ge(out_p, NT * i + t + 2)
                        dve.wait_ge(res_done, i + 1)
                        tt(route.row[:, k, t:t + 2, 0:D], bank[:, t // 2, :, :], x_res[:, k, t:t + 2, :], ALU.add).then_inc(route.x_done, 2)
                    route.vector_stats(nc, dve, i, k)

                def choose(i, k):
                    route.vector_norm(nc, dve, i, k)
                    route.vector_choose(nc, dve, i, k)

                def step(i, k, more=True):
                    if more:
                        low(i + 1, 1 - k)
                    sums(i, k)
                    route.vector_slots(nc, dve, i - 1, count_ps, 1 - k)
                    choose(i, k)

                low(0, 0)
                route.prepare(nc, dve)
                low(1, 1)
                sums(0, 0)
                choose(0, 0)
                sequences(dve, step)
                step(B - 1, (B - 1) % 2, False)
                dve.wait_ge(route.sent, 16 * NT * (B - 1))
                route.vector_slots(nc, dve, B - 1, count_ps, (B - 1) % 2)
                route.vector_end(nc, dve, B)


def hybrid_block(nc, x, wq, wk, wv, wo, times, phases, freqs, mlp_w1, mlp_b1, mlp_w2, mlp_b2, mlp_w3, mlp_b3, decay,
                 in_w, in_b, conv_w, conv_b, hy_gate_w, hy_gate_b, hy_out_w, hy_out_b,
                 gate_w, w1, b1, w2, b2, sw1, sb1, sw2, sb2, out):
    def scratch(name, shape):
        return nc.dram_tensor(name, shape, F32).ap()
    arranged = scratch("arranged", [ORDER, DH, CHUNKS, 4, CH, FW])
    v_blocks = scratch("v_blocks", [DH, P, BLK * SEQW])
    v_mid = scratch("v_mid", [DH, P, BLK * SEQW])
    v_out = scratch("v_out", [DH, P, T])
    gates = scratch("gates", [ORDER, DH, P, T])
    rows_a, rows_b = scratch("rows_a", [SLOTS, ROW]), scratch("rows_b", [SLOTS, ROW])
    count_a, count_b = scratch("count_a", [1, 1]), scratch("count_b", [1, 1])
    x_mid = scratch("x_mid", [T, D])
    with ExitStack() as ctx:
        consts = Constants(nc, ctx)
        consts.make(nc)
        filters(nc, "flt", times, phases, freqs, mlp_w1, mlp_b1, mlp_w2, mlp_b2, mlp_w3, mlp_b3, decay, arranged)
        attention(nc, "att", consts, x, wq, wk, wv, wo, gate_w, rows_a, count_a)
        feed_forward(nc, "ffa", consts, rows_a, count_a, w1, b1, w2, b2, sw1, sb1, sw2, sb2, x_mid)
        projections(nc, "prj", consts, x_mid, in_w, in_b, conv_w, conv_b, hy_gate_w, hy_gate_b, v_blocks, gates)
        convolutions(nc, "cnv", arranged, v_blocks, gates, v_mid, v_out)
        hyena_out(nc, "hyo", consts, x_mid, v_out, hy_out_w, hy_out_b, gate_w, rows_b, count_b)
        feed_forward(nc, "ffb", consts, rows_b, count_b, w1, b1, w2, b2, sw1, sb1, sw2, sb2, out)


def kernel(**inputs):
    import concourse.bacc as bacc
    from concourse.bass_utils import run_bass_kernel_spmd

    a = {name.split("_", 1)[1]: np.asarray(v) for name, v in inputs.items()}

    def columns(v):
        return np.moveaxis(v.reshape(v.shape[:-1] + (-1, P)), -1, 0)
    phases = np.zeros((ENC, 3), np.float32)
    phases[FREQS:2 * FREQS, 0] = 0.25
    phases[2 * FREQS, 1] = 1
    phases[:2 * FREQS, 2] = 1
    args = {
        "x": a["attn_a_hidden_states"].reshape(T, D),
        "wq": a["attn_a_Wq"].T, "wk": a["attn_a_Wk"].T, "wv": a["attn_a_Wv"].T, "wo": a["attn_a_Wo"].T,
        "times": np.linspace(0, 1, S, dtype=np.float32)[::-1][None], "phases": phases,
        "freqs": a["attn_b_freqs"].T,
        "mlp_w1": a["attn_b_mlp_w1"], "mlp_b1": a["attn_b_mlp_b1"].T,
        "mlp_w2": a["attn_b_mlp_w2"], "mlp_b2": a["attn_b_mlp_b2"].T,
        "mlp_w3": a["attn_b_mlp_w3"], "mlp_b3": columns(a["attn_b_mlp_b3"]), "decay": columns(a["attn_b_decay"]),
        "in_w": a["attn_b_in_proj_w"], "in_b": columns(a["attn_b_in_proj_b"]),
        "conv_w": columns(a["attn_b_conv_w"][:, :, 0]).transpose(0, 1, 3, 2), "conv_b": columns(a["attn_b_conv_b"]),
        "hy_gate_w": a["attn_b_gate_w"], "hy_gate_b": columns(a["attn_b_gate_b"]),
        "hy_out_w": a["attn_b_out_proj_w"], "hy_out_b": a["attn_b_out_proj_b"],
        "gate_w": a["ffn_gate_w"], "w1": a["ffn_w1"], "b1": a["ffn_b1"].reshape(2, HB, P).transpose(0, 2, 1),
        "w2": a["ffn_w2"], "b2": a["ffn_b2"],
        "sw1": a["ffn_sw1"], "sb1": a["ffn_sb1"].reshape(HB, P).T, "sw2": a["ffn_sw2"], "sb2": a["ffn_sb2"],
    }
    nc = bacc.Bacc("TRN2", target_bir_lowering=False, num_devices=1)
    arrays, aps = {}, []
    for name, v in args.items():
        arrays[f"in_{name}"] = np.ascontiguousarray(v)
        aps.append(nc.dram_tensor(f"in_{name}", v.shape, mybir.dt.from_np(v.dtype), kind="ExternalInput").ap())
    aps.append(nc.dram_tensor("out", [T, D], F32, kind="ExternalOutput").ap())
    hybrid_block(nc, *aps)
    r = run_bass_kernel_spmd(nc, [arrays], core_ids=[0])
    return r.results[0]["out"].reshape(B, S, D)
```

```python
import numpy as np
import concourse.bass as bass
from concourse import mybir
from contextlib import ExitStack

F32 = mybir.dt.float32
F32R = mybir.dt.float32r
BF16 = mybir.dt.bfloat16
U32 = mybir.dt.uint32
I32 = mybir.dt.int32
ALU = mybir.AluOpType
ACT = mybir.ActivationFunctionType
AX = mybir.AxisListType

P = 128
B, S, D = 8, 1024, 256
T = B * S
HID = 1024
DH = D // P
TILE = 512
SUB = TILE // P
SLOTS = T + TILE
NTILES = SLOTS // TILE
ROW = 2 * D + 8
HB = HID // P
EPS = 1e-5
MASKED = -1e37


def f32(ap):
    return ap.bitcast(F32)


class Memory:

    def __init__(self, nc, ctx, tag):
        self.nc, self.ctx, self.tag = nc, ctx, tag
        self.sems = []
        ctx.callback(self.clear)

    def sb(self, name, shape, dt=F32):
        return self.ctx.enter_context(self.nc.sbuf_tensor(f"{self.tag}_{name}", shape, dt))

    def ps(self, name, shape, dt=F32):
        return self.ctx.enter_context(self.nc.psum_tensor(f"{self.tag}_{name}", shape, dt))

    def sem(self, name):
        self.sems.append(self.nc.alloc_semaphore(name=f"{self.tag}_{name}"))
        return self.sems[-1]

    def clear(self):
        self.nc.clear_and_free_semaphores(self.sems)
        self.nc.all_engine_barrier()


def feed_forward(nc, tag, consts, rows, count0, w1, b1, w2, b2, sw1, sb1, sw2, sb2, out):
    NETS = 3
    STEPS = 2 * HB
    RING = 4
    LAG = 2
    up_w = [sw1, w1[0], w1[1]]
    down_w = [sw2, w2[0], w2[1]]
    with ExitStack() as ctx:
        m = Memory(nc, ctx, tag)
        w_raw = m.sb("w_raw", [P, 2, DH * HID])
        up_hi = m.sb("up_hi", [P, NETS, DH, HID], F32R)
        up_lo = m.sb("up_lo", [P, NETS, DH, HID], F32R)
        dn_hi = m.sb("dn_hi", [P, NETS, HB, D], F32R)
        dn_lo = m.sb("dn_lo", [P, NETS, HB, D], F32R)
        xn = m.sb("xn", [P, SUB, D])
        res = m.sb("res", [P, SUB, ROW])
        xt_hi = m.sb("xt_hi", [P, DH, TILE], F32R)
        xt_lo = m.sb("xt_lo", [P, DH, TILE], F32R)
        h_f = m.sb("h_f", [P, RING, TILE])
        h_hi = m.sb("h_hi", [P, RING, TILE], F32R)
        h_lo = m.sb("h_lo", [P, RING, TILE], F32R)
        y_sb = m.sb("y_sb", [P, SUB, D])
        token = m.sb("token", [P, SUB], U32)
        b_up = m.sb("b_up", [P, NETS, HB])
        b_tile = m.sb("b_tile", [P, NTILES, HB])
        c_hid = m.sb("c_hid", [P, 2, HB])
        c_wide = m.sb("c_wide", [P, 2, HB, P])
        row_b = m.sb("row_b", [P, NETS, D])
        konst = m.sb("konst", [P, 2, D])
        k_tile = m.sb("k_tile", [P, D])
        flag = m.sb("flag", [P, NTILES])
        nflag = m.sb("nflag", [P, NTILES])
        flag_u = m.sb("flag_u", [P, NTILES], U32)
        start = m.sb("start", [P, NTILES])
        n0 = m.sb("n0", [P, 1])
        up_ps = m.ps("up_ps", [P, RING, TILE])
        t_ps = m.ps("t_ps", [P, DH, TILE])
        y_ps = m.ps("y_ps", [P, SUB, D])

        w_loaded = [m.sem(f"w_loaded{n}") for n in range(2)]
        w_hi = m.sem("w_hi")
        w_lo = m.sem("w_lo")
        b_loaded = m.sem("b_loaded")
        tiles_known = m.sem("tiles_known")
        starts_made = m.sem("starts_made")
        const_hid = m.sem("const_hid")
        const_y = m.sem("const_y")
        const_done = m.sem("const_done")
        xn_loaded = m.sem("xn_loaded")
        res_loaded = m.sem("res_loaded")
        transposed = m.sem("transposed")
        xt_hi_done = m.sem("xt_hi_done")
        xt_lo_done = m.sem("xt_lo_done")
        up_done = m.sem("up_done")
        h_act = m.sem("h_act")
        h_hi_done = m.sem("h_hi_done")
        c_hid_done = m.sem("c_hid_done")
        h_lo_done = m.sem("h_lo_done")
        down_done = m.sem("down_done")
        y_done = m.sem("y_done")
        base_done = m.sem("base_done")
        base_step = m.sem("base_step")
        y_stored = m.sem("y_stored")
        held = m.sem("held")

        tile_rows = rows.rearrange("(t s p) c -> t p s c", p=P, s=SUB)

        with nc.Block() as block:

            @block.sync
            def _(sp):
                sp.dma_start(xn[:, :, :], tile_rows[0, :, :, D:2 * D]).then_inc(xn_loaded, 16)
                for n in range(2 * NETS):
                    net, down = divmod(n, 2)
                    if n >= 2:
                        sp.wait_ge(w_lo, n - 1)
                    src = (down_w if down else up_w)[net].rearrange("(c p) n -> p c n", p=P)
                    dst = w_raw[:, n % 2, :].rearrange("p (c n) -> p c n", c=HB if down else DH)
                    sp.dma_start(dst, src).then_inc(w_loaded[n % 2], 16)
                    if n == 1:
                        sp.dma_start(res[:, :, :], tile_rows[0]).then_inc(res_loaded, 16)

                def load(i):
                    sp.wait_ge(transposed, DH * i)
                    sp.sem_inc(held, 1)
                    sp.dma_start(xn[:, :, :], rows[bass.ds(i * TILE, TILE), D:2 * D]
                                 .rearrange("(s p) c -> p s c", p=P)).then_inc(xn_loaded, 16)
                    sp.wait_ge(y_done, 1 + i)
                    sp.sem_inc(held, 1)
                    sp.dma_start(res[:, :, :], rows[bass.ds(i * TILE, TILE), :]
                                 .rearrange("(s p) c -> p s c", p=P)).then_inc(res_loaded, 16)

                with sp.Fori(1, NTILES) as i:
                    load(i)

            @block.gpsimd
            def _(pool):
                pool.dma_start(b_up[:, 0, :], sb1).then_inc(b_loaded, 16)
                for e in range(2):
                    pool.dma_start(b_up[:, 1 + e, :], b1[e]).then_inc(b_loaded, 16)
                pool.dma_start(row_b[:, 0, :], sb2.rearrange("(a n) -> a n", a=1).broadcast_to([P, D])).then_inc(b_loaded, 16)
                for e in range(2):
                    pool.dma_start(row_b[:, 1 + e, :], b2[e:e + 1, :].broadcast_to([P, D])).then_inc(b_loaded, 16)
                pool.dma_start(n0[:, :], count0.broadcast_to([P, 1])).then_inc(b_loaded, 16)
                pool.iota(start[:, :], pattern=[[TILE, NTILES]], base=0, channel_multiplier=0,
                          allow_small_or_imprecise_dtypes=True).then_inc(starts_made, 1)

                def scatter(i):
                    for s in range(SUB):
                        if s == 0:
                            pool.wait_ge(y_done, i + 2)
                            pool.sem_inc(held, 1)
                        pool.indirect_dma_start(out, bass.IndirectOffsetOnAxis(token[:, s:s + 1], 0),
                                                y_sb[:, s, :], None, bounds_check=T - 1,
                                                oob_is_err=False).then_inc(y_stored, 16)

                with pool.Fori(0, NTILES) as i:
                    scatter(i)
                pool.wait_ge(y_stored, 16 * SUB * NTILES)

            @block.tensor
            def _(pe):
                pe.sem_inc(down_done, RING)
                pe.sem_inc(up_done, 1)

                def transposes(i):
                    pe.wait_ge(xn_loaded, 16 * i + 16)
                    pe.wait_ge(xt_lo_done, DH * i + 1)
                    for d in range(DH):
                        for s in range(SUB):
                            last = nc.tensor.transpose(t_ps[:, d, s * P:(s + 1) * P],
                                                       xn[:, s, d * P:(d + 1) * P], consts.ident[:, :])
                        last.then_inc(transposed, 1)

                def up(i, s, net):
                    g = i * STEPS + s
                    j = s % HB
                    if s == 0:
                        pe.wait_ge(xt_lo_done, DH * i + DH + 1)
                    pe.wait_ge(h_act, g + 1)
                    terms = [(a, b, d) for d in range(DH) for a, b in
                             ((up_hi, xt_lo), (up_lo, xt_hi), (up_hi, xt_hi))]
                    for n, (a, b, d) in enumerate(terms):
                        last = nc.tensor.matmul(up_ps[:, s % RING, :], a[:, net, d, j * P:(j + 1) * P],
                                                b[:, d, :], start=n == 0, stop=n == len(terms) - 1)
                    last.then_inc(up_done, 1)

                def down(i, s, net):
                    g = i * STEPS + s
                    j = s % HB
                    if s == 0:
                        pe.wait_ge(y_done, i + 1)
                    pe.wait_ge(h_lo_done, g + RING + 1)
                    for t in range(SUB):
                        for n, (a, b) in enumerate(((h_hi, dn_lo), (h_lo, dn_hi), (h_hi, dn_hi))):
                            last = nc.tensor.matmul(y_ps[:, t, :], a[:, s % RING, t * P:(t + 1) * P],
                                                    b[:, net, j, :],
                                                    start=s == 0 and n == 0 and t % 2 == 0,
                                                    stop=s == STEPS - 1 and n == 2, skip_group_check=True)
                    last.then_inc(down_done, 1)

                def steps(i, of, net, more):
                    for s in of:
                        if s < STEPS:
                            up(i, s, net if s >= HB else 0)
                        if s == STEPS - 1 and more:
                            transposes(i + 1)
                        if s >= LAG:
                            down(i, s - LAG, net if s - LAG >= HB else 0)

                expert = pe.alloc_register(f"{tag}_expert")

                def expert_steps(i, more):
                    pe.reg_load(expert, flag_u[0:1, bass.ds(i, 1)])
                    with pe.If_lt(expert, 1):
                        steps(i, range(HB, STEPS + LAG), 1, more)
                    with pe.Else():
                        steps(i, range(HB, STEPS + LAG), 2, more)

                pe.wait_ge(xn_loaded, 16)
                transposes(0)
                pe.wait_ge(w_lo, 1)
                steps(0, range(LAG), 0, True)
                pe.wait_ge(w_lo, 2)
                steps(0, range(LAG, HB), 0, True)
                pe.wait_ge(h_act, RING + HB - 2)
                for e in range(2):
                    pe.wait_ge(w_lo, 2 * e + 4)
                    pe.wait_ge(const_hid, e + 1)
                    terms = [(j, w) for j in range(HB) for w in (dn_hi, dn_lo)]
                    for n, (j, w) in enumerate(terms):
                        last = nc.tensor.matmul(up_ps[:, e, 0:D], c_wide[:, e, j, :],
                                                f32(w[:, 1 + e, j, :]), start=n == 0, stop=n == len(terms) - 1)
                    last.then_inc(const_y, 1)
                pe.wait_ge(tiles_known, 4)
                pe.wait_ge(const_done, 3)
                pe.wait_ge(w_lo, 2 * NETS)
                expert_steps(0, True)
                with pe.Fori(1, NTILES - 1) as i:
                    steps(i, range(HB), 0, True)
                    expert_steps(i, True)
                steps(NTILES - 1, range(HB), 0, False)
                expert_steps(NTILES - 1, False)

            @block.scalar
            def _(act):
                act.sem_inc(h_act, RING)

                def split(i):
                    for d in range(DH):
                        act.wait_ge(transposed, DH * i + d + 1)
                        if d == 0:
                            act.wait_ge(up_done, STEPS * i + 1)
                        nc.scalar.activation(xt_hi[:, d, :], t_ps[:, d, :], ACT.Copy).then_inc(xt_hi_done, 1)

                def hidden(i, s):
                    g = i * STEPS + s
                    act.wait_ge(up_done, g + 2)
                    act.wait_ge(h_lo_done, g + 1)
                    bias = b_up[:, 0, s:s + 1] if s < HB else b_tile[:, i, s - HB:s - HB + 1] if isinstance(i, int) \
                        else b_tile[:, bass.ds(i, 1), s - HB:s - HB + 1].rearrange("p a b -> p (a b)")
                    nc.scalar.activation(h_f[:, s % RING, :], up_ps[:, s % RING, :], ACT.Relu,
                                         bias=bias).then_inc(h_act, 1)

                act.wait_ge(b_loaded, 16 * 7)
                split(0)
                for s in range(HB):
                    hidden(0, s)
                act.wait_ge(tiles_known, 4)
                for s in range(HB, STEPS):
                    hidden(0, s)
                split(1)
                with act.Fori(1, NTILES - 1) as i:
                    for s in range(STEPS):
                        hidden(i, s)
                    split(i + 1)
                for s in range(STEPS):
                    hidden(NTILES - 1, s)

            @block.vector
            def _(dve):
                dve.sem_inc(h_lo_done, RING)
                dve.sem_inc(y_done, 1)
                dve.sem_inc(xt_lo_done, 1)
                def weight(n):
                    net, down = divmod(n, 2)
                    hi, lo = (dn_hi, dn_lo) if down else (up_hi, up_lo)
                    raw = w_raw[:, n % 2, :].rearrange("p (c n) -> p c n", c=HB if down else DH)
                    dve.wait_ge(w_loaded[n % 2], 16 * (n // 2 + 1))
                    nc.vector.tensor_copy(hi[:, net, :, :], raw).then_inc(w_hi, 1)
                    dve.wait_ge(w_hi, n + 1)
                    nc.vector.tensor_tensor(lo[:, net, :, :], raw, f32(hi[:, net, :, :]), ALU.subtract).then_inc(w_lo, 1)

                def know_tiles():
                    dve.wait_ge(b_loaded, 16 * 7)
                    dve.wait_ge(starts_made, 1)
                    nc.vector.tensor_scalar(flag[:, :], start[:, :], n0[:, 0:1], None, ALU.is_ge).then_inc(tiles_known, 1)
                    dve.wait_ge(tiles_known, 1)
                    nc.vector.tensor_copy(flag_u[:, :], flag[:, :])
                    nc.vector.tensor_scalar(nflag[:, :], flag[:, :], -1.0, 1.0, ALU.mult, ALU.add).then_inc(tiles_known, 1)
                    dve.wait_ge(tiles_known, 2)
                    wide = [P, NTILES, HB]
                    nc.vector.tensor_tensor(b_tile[:, :, :], b_up[:, 1:2, :].broadcast_to(wide),
                                            nflag[:, :].unsqueeze(2).broadcast_to(wide), ALU.mult)
                    nc.vector.tensor_tensor(c_wide[:, 0, :, :].rearrange("p a b -> p (a b)")[:, 0:NTILES * HB].rearrange("p (a b) -> p a b", b=HB),
                                            b_up[:, 2:3, :].broadcast_to(wide),
                                            flag[:, :].unsqueeze(2).broadcast_to(wide), ALU.mult).then_inc(tiles_known, 1)
                    dve.wait_ge(tiles_known, 3)
                    nc.vector.tensor_tensor(b_tile[:, :, :], b_tile[:, :, :],
                                            c_wide[:, 0, :, :].rearrange("p a b -> p (a b)")[:, 0:NTILES * HB].rearrange("p (a b) -> p a b", b=HB),
                                            ALU.add).then_inc(tiles_known, 1)
                    dve.wait_ge(tiles_known, 4)
                    nc.vector.tensor_relu(c_hid[:, :, :], b_up[:, 1:3, :]).then_inc(c_hid_done, 1)
                    dve.wait_ge(c_hid_done, 1)
                    for e in range(2):
                        nc.vector.tensor_copy(c_wide[:, e, :, :],
                                              c_hid[:, e, :].unsqueeze(2).broadcast_to([P, HB, P])).then_inc(const_hid, 1)

                def split(i):
                    for d in range(DH):
                        dve.wait_ge(xt_hi_done, DH * i + d + 1)
                        nc.vector.tensor_tensor(xt_lo[:, d, :], t_ps[:, d, :], f32(xt_hi[:, d, :]),
                                                ALU.subtract).then_inc(xt_lo_done, 1)

                def base(i):
                    at = slice(i, i + 1) if isinstance(i, int) else bass.ds(i, 1)
                    dve.wait_ge(base_step, 3 * i + 1)
                    nc.vector.tensor_scalar(k_tile[:, :], konst[:, 0, :], nflag[:, at], None, ALU.mult).then_inc(base_step, 1)
                    dve.wait_ge(base_step, 3 * i + 2)
                    nc.vector.scalar_tensor_tensor(k_tile[:, :], konst[:, 1, :], flag[:, at], k_tile[:, :],
                                                   ALU.mult, ALU.add).then_inc(base_step, 1)
                    dve.wait_ge(res_loaded, 16 * i + 16)
                    dve.wait_ge(base_step, 3 * i + 3)
                    nc.vector.tensor_tensor(res[:, :, 0:D], res[:, :, 0:D],
                                            k_tile[:, :].unsqueeze(1).broadcast_to([P, SUB, D]), ALU.add).then_inc(base_step, 1)

                def hidden(i, s):
                    g = i * STEPS + s
                    dve.wait_ge(h_act, g + RING + 1)
                    dve.wait_ge(down_done, g + 1)
                    nc.vector.tensor_copy(h_hi[:, s % RING, :], h_f[:, s % RING, :]).then_inc(h_hi_done, 1)
                    dve.wait_ge(h_hi_done, g + 1)
                    nc.vector.tensor_tensor(h_lo[:, s % RING, :], h_f[:, s % RING, :], f32(h_hi[:, s % RING, :]),
                                            ALU.subtract).then_inc(h_lo_done, 1)

                def finish(i):
                    dve.wait_ge(down_done, STEPS * i + STEPS + RING)
                    dve.wait_ge(base_step, 3 * i + 4)
                    dve.wait_ge(y_stored, 16 * SUB * i)
                    nc.vector.tensor_copy(token[:, :], res[:, :, 2 * D:2 * D + 1].rearrange("p s c -> p (s c)").bitcast(U32))
                    nc.vector.tensor_tensor(y_sb[:, :, :], y_ps[:, :, :], res[:, :, 0:D], ALU.add).then_inc(y_done, 1)

                def constants():
                    for e in range(2):
                        dve.wait_ge(const_y, 2)
                        if e == 0:
                            nc.vector.tensor_tensor(row_b[:, 1, :], row_b[:, 1, :], row_b[:, 2, :], ALU.add).then_inc(const_done, 1)
                        dve.wait_ge(const_done, 1 + e)
                        nc.vector.scalar_tensor_tensor(konst[:, e, :], up_ps[:, 1 - e, 0:D], 1.0, row_b[:, 1, :],
                                                       ALU.mult, ALU.add).then_inc(const_done, 1)
                    dve.wait_ge(const_done, 3)
                    nc.vector.tensor_tensor(konst[:, :, :], konst[:, :, :], row_b[:, 0:1, :].broadcast_to([P, 2, D]),
                                            ALU.add).then_inc(base_step, 1)

                def blocks(i):
                    for s in range(STEPS):
                        hidden(i, s)
                        if s == HB - 1:
                            base(i)

                weight(0)
                split(0)
                weight(1)
                for s in range(STEPS):
                    hidden(0, s)
                    if s == 1:
                        know_tiles()
                    if s in (2, 4, 5, 7):
                        weight((2, 4, 5, 7).index(s) + 2)
                    if s == HB - 1:
                        constants()
                        base(0)
                split(1)
                finish(0)
                with dve.Fori(1, NTILES - 1) as i:
                    blocks(i)
                    split(i + 1)
                    finish(i)
                blocks(NTILES - 1)
                finish(NTILES - 1)


class Constants:

    def __init__(self, nc, ctx):
        m = Memory(nc, ctx, "c")
        self.ident = m.sb("ident", [P, P])
        self.ident_bf = m.sb("ident_bf", [P, P], BF16)
        self.before = m.sb("before", [P, P])
        self.ones = m.sb("ones", [P, P])
        self.minus_half = m.sb("minus_half", [P, 16])
        self.head_rows = m.sb("head_rows", [P, 8])
        self.mask_q = m.sb("mask_q", [P, 512], BF16)
        self.mask_k = m.sb("mask_k", [P, 512], BF16)
        self.made = m.sem("made")
        self.zeroed = m.sem("zeroed")

    def make(self, nc):
        with nc.Block() as block:
            @block.gpsimd
            def _(pool):
                pool.memset(self.ident[:, :], 0.0).then_inc(self.zeroed, 1)
                pool.memset(self.ones[:, :], 1.0).then_inc(self.zeroed, 1)
                pool.wait_ge(self.zeroed, 2)
                pool.affine_select(out=self.ident[:, :], in_=self.ident[:, :], compare_op=ALU.not_equal, fill=1.0,
                                   base=0, pattern=[[-1, P]], channel_multiplier=1).then_inc(self.made, 1)
                pool.affine_select(out=self.before[:, :], in_=self.ones[:, :], compare_op=ALU.is_gt, fill=0.0,
                                   base=0, pattern=[[1, P]], channel_multiplier=-1).then_inc(self.made, 1)
                pool.wait_ge(self.made, 2)
                pool.tensor_copy(self.ident_bf[:, :], self.ident[:, :]).then_inc(self.made, 1)
                pool.memset(self.minus_half[:, :], -0.5).then_inc(self.made, 1)
                pool.affine_select(out=self.head_rows[:, :], in_=self.ones[:, 0:8], compare_op=ALU.is_ge, fill=0.0,
                                   base=0, pattern=[[-16, 8]], channel_multiplier=1).then_inc(self.made, 1)
                pool.wait_ge(self.made, 5)
                pool.affine_select(out=self.head_rows[:, :], in_=self.head_rows[:, :], compare_op=ALU.is_ge, fill=0.0,
                                   base=15, pattern=[[16, 8]], channel_multiplier=-1).then_inc(self.made, 1)
                pool.memset(self.mask_q[:, :], 0.0).then_inc(self.zeroed, 1)
                pool.memset(self.mask_k[:, :], 0.0).then_inc(self.zeroed, 1)
                pool.wait_ge(self.zeroed, 4)
                pool.affine_select(out=self.mask_q[:, :], in_=self.mask_q[:, :], compare_op=ALU.is_ge, fill=MASKED,
                                   base=0, pattern=[[0, 4], [-1, P]], channel_multiplier=1).then_inc(self.made, 1)
                pool.affine_select(out=self.mask_k[:, :], in_=self.mask_k[:, :], compare_op=ALU.is_ge, fill=MASKED,
                                   base=0, pattern=[[0, 4], [1, P]], channel_multiplier=-1).then_inc(self.made, 1)
                pool.wait_ge(self.made, 8)


NT = S // P
HEADS = 16
HD = D // HEADS
WIN = 256
KT = WIN // P
HW = 64
PAIRS = HEADS // 2
OW = 32
GROUPS = HEADS // 4


class LayerNorm:

    def __init__(self, m, name, consts, n):
        self.n, self.consts = n, consts
        self.stat = m.sb(f"{name}_stat", [P, n, 6])
        self.mv = m.sb(f"{name}_mv", [P, n, 2])
        self.rstd = m.sb(f"{name}_rstd", [P, n])
        self.stats_done = m.sem(f"{name}_stats")
        self.aggr_done = m.sem(f"{name}_aggr")
        self.eps_added = m.sem(f"{name}_eps")
        self.rstd_done = m.sem(f"{name}_rstd")
        self.done = m.sem(f"{name}_done")
        self.held = m.sem(f"{name}_held")

    def stats(self, nc, dve, i, x):
        for t in range(self.n):
            nc.vector.bn_stats(self.stat[:, t, :], x[:, t, :]).then_inc(self.stats_done, 1)
        dve.wait_ge(self.stats_done, self.n * i + self.n)
        dve.sem_inc(self.held, 1)
        for t in range(self.n):
            nc.vector.bn_aggr(self.mv[:, t, :], self.stat[:, t, :]).then_inc(self.aggr_done, 1)

    def power(self, nc, pool, i):
        pool.wait_ge(self.aggr_done, self.n * i + self.n)
        pool.sem_inc(self.held, 1)
        nc.gpsimd.tensor_scalar(self.rstd[:, :], self.mv[:, :, 1:2].rearrange("p n a -> p (n a)"), EPS, None,
                                ALU.add).then_inc(self.eps_added, 1)
        pool.wait_ge(self.eps_added, i + 1)
        nc.gpsimd.tensor_tensor(self.rstd[:, :], self.rstd[:, :], self.consts.minus_half[:, 0:self.n],
                                ALU.pow).then_inc(self.rstd_done, 1)

    def apply(self, nc, dve, i, x, out):
        dve.wait_ge(self.rstd_done, i + 1)
        for t in range(self.n):
            nc.vector.tensor_scalar(out[:, t, :], x[:, t, :], self.mv[:, t, 0:1], self.rstd[:, t:t + 1],
                                    ALU.subtract, ALU.mult).then_inc(self.done, 1)


class Route:

    def __init__(self, nc, m, consts, rows, count0, buffers=1):
        self.consts, self.rows, self.count0 = consts, rows, count0
        self.ln = LayerNorm(m, "route", consts, NT)
        self.row = m.sb("row", [P, buffers, NT, ROW])
        self.gate = m.sb("gate", [P, 2, D])
        self.gate_d = m.sb("gate_d", [P, D])
        self.prod = m.sb("prod", [P, D])
        self.score = m.sb("score", [P, NT])
        self.to1 = m.sb("to1", [P, NT])
        self.total = m.sb("total", [P, NT])
        self.upto = m.sb("upto", [P, NT])
        self.carry = m.sb("carry", [P, 1])
        self.place = m.sb("place", [P, NT])
        self.back = m.sb("back", [P, NT])
        self.ones_n = m.sb("ones_n", [P, NT])
        self.slot = m.sb("slot", [P, NT], U32)
        self.fill = m.sb("fill", [P, SUB, ROW])
        self.n0 = m.sb("n0", [P, 1])
        self.n0_u = m.sb("n0_u", [P, 1], U32)
        self.gate_loaded = m.sem("gate_loaded")
        self.gate_done = m.sem("gate_done")
        self.x_done = m.sem("x_done")
        self.scored = m.sem("scored")
        self.chosen = m.sem("chosen")
        self.counted = m.sem("counted")
        self.step = m.sem("slot_step")
        self.slots_done = m.sem("slots_done")
        self.sent = m.sem("sent")
        self.held = m.sem("slots_held")
        self.numbered = m.sem("numbered")
        self.finished = m.sem("finished")
        self.end_written = m.sem("end_written")

    def load(self, eng, gate_w):
        for e in range(2):
            eng.dma_start(self.gate[:, e, :], gate_w[e:e + 1, :].broadcast_to([P, D])).then_inc(self.gate_loaded, 16)

    def prepare_pool(self, nc, pool):
        nc.gpsimd.iota(self.place[:, :], pattern=[[P, NT]], base=0, channel_multiplier=1,
                       allow_small_or_imprecise_dtypes=True).then_inc(self.numbered, 1)

    def prepare(self, nc, dve):
        dve.wait_ge(self.gate_loaded, 32)
        nc.vector.tensor_tensor(self.gate_d[:, :], self.gate[:, 1, :], self.gate[:, 0, :], ALU.subtract).then_inc(self.gate_done, 1)
        nc.vector.memset(self.carry[:, :], 0.0).then_inc(self.gate_done, 1)
        nc.vector.memset(self.ones_n[:, :], 1.0).then_inc(self.gate_done, 1)
        nc.vector.memset(self.row[:, :, :, 2 * D:ROW], 0.0).then_inc(self.gate_done, 1)
        nc.vector.memset(self.fill[:, :, :], 0.0).then_inc(self.gate_done, 1)
        dve.wait_ge(self.gate_done, 5)
        nc.vector.memset(self.fill[:, :, 2 * D:2 * D + 1].bitcast(U32), 2 * T).then_inc(self.gate_done, 1)
        dve.wait_ge(self.gate_done, 6)
        dve.wait_ge(self.numbered, 1)

    def vector_stats(self, nc, dve, i, k=0):
        dve.wait_ge(self.x_done, NT * i + NT)
        self.ln.stats(nc, dve, i, self.row[:, k, :, 0:D])

    def vector_norm(self, nc, dve, i, k=0):
        self.ln.apply(nc, dve, i, self.row[:, k, :, 0:D], self.row[:, k, :, D:2 * D])

    def vector_choose(self, nc, dve, i, k=0):
        for t in range(NT):
            self.vector_score(nc, dve, i, t, k)
        self.vector_compare(nc, dve, i)

    def vector_score(self, nc, dve, i, t, k=0):
        dve.wait_ge(self.ln.done, NT * i + t + 1)
        dve.wait_ge(self.scored, NT * i + t)
        nc.vector.tensor_tensor_reduce(self.prod[:, :], self.row[:, k, t, D:2 * D], self.gate_d[:, :], 1.0, 0.0,
                                       ALU.mult, ALU.add, self.score[:, t:t + 1]).then_inc(self.scored, 1)

    def vector_compare(self, nc, dve, i):
        dve.wait_ge(self.scored, NT * i + NT)
        nc.vector.tensor_scalar(self.to1[:, :], self.score[:, :], 0.0, None, ALU.is_gt).then_inc(self.chosen, 1)

    def tensor(self, nc, pe, i, ps):
        pe.wait_ge(self.chosen, i + 1)
        nc.tensor.matmul(ps[:, 0, :], self.consts.before[:, :], self.to1[:, :], start=True, stop=True)
        nc.tensor.matmul(ps[:, 1, :], self.consts.ones[:, :], self.to1[:, :], start=True, stop=True).then_inc(self.counted, 1)

    def vector_slots(self, nc, dve, i, ps, k=0):
        N = 9
        n = [0]

        def link(ins):
            n[0] += 1
            ins.then_inc(self.step, 1)
            dve.wait_ge(self.step, N * i + n[0])

        dve.wait_ge(self.counted, i + 1)
        link(nc.vector.tensor_copy(self.total[:, :], ps[:, 1, :]))
        link(nc.vector.tensor_tensor_scan(self.upto[:, :], self.ones_n[:, :], self.total[:, :], self.carry[:, 0:1],
                                          ALU.mult, ALU.add))
        link(nc.vector.tensor_copy(self.carry[:, :], self.upto[:, NT - 1:NT]))
        link(nc.vector.tensor_tensor(self.upto[:, :], self.upto[:, :], self.total[:, :], ALU.subtract))
        link(nc.vector.tensor_tensor(self.upto[:, :], self.upto[:, :], ps[:, 0, :], ALU.add))
        link(nc.vector.tensor_tensor(self.upto[:, :], self.place[:, :], self.upto[:, :], ALU.subtract))
        link(nc.vector.tensor_scalar(self.back[:, :], self.place[:, :], -1.0, float(SLOTS - 1), ALU.mult, ALU.add))
        link(nc.vector.tensor_tensor(self.back[:, :], self.back[:, :], self.to1[:, :], ALU.mult))
        link(nc.vector.tensor_tensor(self.upto[:, :], self.upto[:, :], self.back[:, :], ALU.add))
        nc.vector.tensor_copy(self.row[:, k, :, 2 * D:2 * D + 1].rearrange("p t a -> p (t a)").bitcast(U32), self.place[:, :])
        nc.vector.tensor_copy(self.slot[:, :], self.upto[:, :]).then_inc(self.slots_done, 1)
        dve.wait_ge(self.slots_done, 2 * i + 1)
        nc.vector.tensor_scalar(self.place[:, :], self.place[:, :], float(S), None, ALU.add).then_inc(self.slots_done, 1)
        dve.wait_ge(self.slots_done, 2 * i + 2)

    def pool(self, nc, pool, i, k=0):
        pool.wait_ge(self.slots_done, 2 * i + 1)
        pool.sem_inc(self.held, 1)
        for t in range(NT):
            pool.indirect_dma_start(self.rows[:, :], bass.IndirectOffsetOnAxis(self.slot[:, t:t + 1], 0),
                                    self.row[:, k, t, :], None, bounds_check=SLOTS - 1,
                                    oob_is_err=False).then_inc(self.sent, 16)

    def vector_end(self, nc, dve, rounds):
        nc.vector.tensor_scalar(self.n0[:, :], self.carry[:, :], -1.0, float(T), ALU.mult, ALU.add).then_inc(self.finished, 1)
        dve.wait_ge(self.finished, 1)
        nc.vector.tensor_copy(self.n0_u[:, :], self.n0[:, :]).then_inc(self.finished, 1)

    def sync_end(self, nc, sp, rounds):
        sp.wait_ge(self.finished, 2)
        sp.wait_ge(self.sent, 16 * NT * rounds)
        sp.dma_start(self.count0, self.n0[0:1, 0:1]).then_inc(self.end_written, 16)
        first = sp.value_load(self.n0_u[0:1, 0:1], min_val=0, max_val=T)
        sp.dma_start(self.rows[bass.ds(first, TILE), :].rearrange("(s p) c -> p s c", p=P),
                     self.fill[:, :, :]).then_inc(self.end_written, 16)
        sp.wait_ge(self.end_written, 32)


def attention(nc, tag, consts, x, wq, wk, wv, wo, gate_w, rows, count0):
    with ExitStack() as ctx:
        m = Memory(nc, ctx, tag)
        x_in = m.sb("x_in", [P, NT, D])
        x_res = m.sb("x_res", [P, NT, D])
        xn = m.sb("xn", [P, NT, D])
        xt_hi = m.sb("xt_hi", [P, DH, S], F32R)
        xt_lo = m.sb("xt_lo", [P, DH, S], F32R)
        w_hi = m.sb("w_hi", [P, 4, DH, D], F32R)
        w_lo = m.sb("w_lo", [P, 4, DH, D], F32R)
        qp = m.sb("qp", [P, 2, HEADS, HW], F32R)
        kp = m.sb("kp", [P, HEADS, HW], F32R)
        qc = m.sb("qc", [P, 2, D], F32R)
        kc = m.sb("kc", [P, D], F32R)
        qht = m.sb("qht", [P, 2, 2, P], F32R)
        km = m.sb("km", [P, 2, 8, WIN], F32R)
        kz = m.sb("kz", [P, HEADS, WIN], F32R)
        qpt = m.sb("qpt", [P, PAIRS, S], F32R)
        va = m.sb("va", [P, KT, HEADS, OW])
        pt = m.sb("pt", [P, 4, 512])
        ot = m.sb("ot", [P, GROUPS, S])
        w_raw = ot[:, 0:DH, :]
        rden = m.sb("rden", [P, 2, HEADS])
        o_sb = m.sb("o_sb", [P, 2, D])
        o_hi = m.sb("o_hi", [P, 2, DH, P], F32R)
        o_lo = m.sb("o_lo", [P, 2, DH, P], F32R)
        bank = m.ps("bank", [P, 8, 512])
        ln = LayerNorm(m, "ln", consts, NT)
        route = Route(nc, m, consts, rows, count0)
        row = route.row[:, 0]

        names = """w_in w_hi_done w_lo_done zero_done x_loaded res_loaded xt_t xt_hi_done xt_lo_done
            kv_p kv_act kp_lo km_t km_done kz_t kz_done q_p q_act q_lo qh_t qh_done s_p s_max qp_t qp_done
            st_p exp_done pv_p ot_done on_t norm_r norm_done of_t of_hi of_lo out_p"""
        g = {n: m.sem(n) for n in names.split()}
        held = m.sem("held")
        HALVES = 2
        XT = DH * HALVES
        pairs_of = [2 if t % 2 == 0 else 4 for t in range(NT)]
        SP_N = sum(pairs_of)
        UNITS = 3
        U = HEADS * UNITS
        COUNT_AT = U - 8
        count_ps = bank[:, 4, 0:2 * NT].rearrange("p (a t) -> p a t", a=2)

        with nc.Block() as block:

            @block.sync
            def _(sp):
                def load(i):
                    sp.wait_ge(ln.done, NT * i)
                    sp.sem_inc(held, 1)
                    sp.dma_start(x_in[:, :, :], x[bass.ds(i * S, S), :].rearrange("(t p) c -> p t c", p=P)).then_inc(g["x_loaded"], 16)

                def load_res(i):
                    sp.wait_ge(route.x_done, NT * i)
                    sp.sem_inc(held, 1)
                    sp.dma_start(x_res[:, :, :], x[bass.ds(i * S, S), :].rearrange("(t p) c -> p t c", p=P)).then_inc(g["res_loaded"], 16)

                for n, w in enumerate((wq, wk, wv, wo)):
                    sp.dma_start(w_raw[:, :, n * D:(n + 1) * D], w.rearrange("(c p) n -> p c n", p=P)).then_inc(g["w_in"], 16)
                route.load(sp, gate_w)
                load(0)
                with sp.Fori(0, B - 1) as i:
                    load_res(i)
                    load(i + 1)
                load_res(B - 1)
                route.sync_end(nc, sp, B)

            @block.gpsimd
            def _(pool):
                route.prepare_pool(nc, pool)
                ln.power(nc, pool, 0)
                ln.power(nc, pool, 1)
                with pool.Fori(1, B - 1) as i:
                    ln.power(nc, pool, i + 1)
                    route.ln.power(nc, pool, i - 1)
                    route.pool(nc, pool, i - 1)
                for i in (B - 2, B - 1):
                    route.ln.power(nc, pool, i)
                    route.pool(nc, pool, i)
                pool.wait_ge(route.sent, 16 * NT * B)

            @block.tensor
            def _(pe):
                mm = nc.tensor.matmul

                def xt(i, chunks=range(XT)):
                    for c in chunks:
                        half, d = divmod(c, DH)
                        if c == 0:
                            pe.wait_ge(ln.done, NT * i + NT)
                        if c >= 2:
                            pe.wait_ge(g["xt_lo_done"], XT * i + c - 1)
                        for t in range(4):
                            last = nc.tensor.transpose(bank[:, 6 + c % 2, t * P:(t + 1) * P],
                                                       xn[:, 4 * half + t, d * P:(d + 1) * P], consts.ident[:, :])
                        last.then_inc(g["xt_t"], 1)

                def project(out, t, w):
                    terms = [(a, b, d) for d in range(DH) for a, b in ((xt_hi, w_lo), (xt_lo, w_hi), (xt_hi, w_hi))]
                    for n, (a, b, d) in enumerate(terms):
                        last = mm(out, a[:, d, t * P:(t + 1) * P], b[:, w, d, :], start=n == 0, stop=n == len(terms) - 1)
                    return last

                def key_products(i, kt):
                    if kt == 0:
                        pe.wait_ge(g["xt_lo_done"], XT * i + DH)
                    project(bank[:, 2 * kt, 0:D], kt, 1)
                    project(bank[:, 2 * kt + 1, 0:D], kt, 2).then_inc(g["kv_p"], 1)

                def keys(i):
                    key_products(i, 1)
                    pe.wait_ge(route.x_done, NT * i)
                    for kt in range(KT):
                        pe.wait_ge(g["kp_lo"], KT * i + kt + 1)
                        for e in range(2):
                            last = nc.tensor.transpose(bank[:, 5 - kt, e * P:(e + 1) * P], f32(kc[:, e * P:(e + 1) * P]), consts.ident[:, :])
                        last.then_inc(g["km_t"], 1)
                        for h in range(2):
                            if kt:
                                pe.wait_ge(g["kz_done"], 4 * KT * i + 2 * (h + 1))
                            for p in range(4):
                                last = nc.tensor.transpose(bank[:, 6 + h, p * P:(p + 1) * P],
                                                           f32(kp[:, 2 * (4 * h + p):2 * (4 * h + p) + 2, :].rearrange("p a b -> p (a b)")), consts.ident[:, :])
                            last.then_inc(g["kz_t"], 1)

                def q_project(i, t):
                    if t == 0:
                        pe.wait_ge(g["xt_lo_done"], XT * i + XT)
                        pe.wait_ge(g["km_done"], 2 * KT * i + 2)
                    else:
                        pe.wait_ge(g["q_lo"], NT * i + t)
                    project(bank[:, 5, 0:D], t, 0).then_inc(g["q_p"], 1)

                def q_heads(i, t):
                    pe.wait_ge(g["q_act"], 2 * (NT * i + t) + 1)
                    if t:
                        pe.wait_ge(g["qh_done"], NT * i + t)
                    else:
                        pe.wait_ge(g["km_done"], 2 * KT * i + 2 * KT)
                    for e in range(2):
                        last = nc.tensor.transpose(bank[:, 4, e * P:(e + 1) * P], f32(qc[:, t % 2, e * P:(e + 1) * P]), consts.ident[:, :])
                    last.then_inc(g["qh_t"], 1)

                def scores(i, t, pairs):
                    if pairs[0] == 0:
                        pe.wait_ge(g["qh_done"], NT * i + t + 1)
                    nk = P * (1 + t % 2)
                    per = 512 // nk
                    for j in pairs:
                        n = sum(pairs_of[:t]) + j
                        if n >= 2:
                            pe.wait_ge(g["s_max"], SP_N * i + n - 1)
                        for b in range(2):
                            h0 = (2 * j + b) * per
                            out = bank[:, 2 * (n % 2) + b, :]
                            mm(out.rearrange("p (h k) -> p h k", k=nk), qht[:, t % 2, h0 // 8, :],
                               km[:, h0 // 8, h0 % 8:h0 % 8 + per, 0:nk], start=True, stop=False)
                            last = mm(out.rearrange("p (h k) -> p h k", k=nk)[:, :, nk - P:nk], consts.ident_bf[:, :],
                                      consts.mask_q[:, 0:per * P].rearrange("p (h k) -> p h k", k=P), start=False, stop=True)
                        last.then_inc(g["s_p"], 1)

                def q_packed(i, t):
                    for h in range(2):
                        if h == 0:
                            pe.wait_ge(g["s_max"], SP_N * i + sum(pairs_of[:t + 1]))
                            pe.wait_ge(g["q_lo"], NT * i + t + 1)
                        if t == 0:
                            pe.wait_ge(g["kz_done"], 4 * KT * (i + 1))
                            pe.wait_ge(g["km_done"], 2 * KT * (i + 1))
                        else:
                            pe.wait_ge(g["qp_done"], 2 * (NT * i + t) + h - 1)
                        for p in range(4):
                            last = nc.tensor.transpose(bank[:, 6 + h, p * P:(p + 1) * P],
                                                       f32(qp[:, t % 2, 2 * (4 * h + p):2 * (4 * h + p) + 2, :].rearrange("p a b -> p (a b)")), consts.ident[:, :])
                        last.then_inc(g["qp_t"], 1)

                qpt_v = qpt[:, :, :].rearrange("p a (w e c) -> p a w e c", e=2, c=P)

                def unit(i, n):
                    h, u = divmod(n, UNITS)
                    kt, odd, masked = ((0, 0, True), (0, 1, False), (1, 1, True))[u]
                    if n == 0:
                        pe.wait_ge(g["qp_done"], 2 * NT * (i + 1))
                    if n >= 4:
                        pe.wait_ge(g["exp_done"], U * i + n - 3)
                    out = bank[:, n % 4, :]
                    if masked:
                        mm(out, consts.ident_bf[:, :], consts.mask_k[:, :], start=True, stop=False)
                    mm(out.rearrange("p (w c) -> p w c", c=P), kz[:, h, kt * P:(kt + 1) * P], qpt_v[:, h // 2, :, odd, :],
                       start=not masked, stop=True).then_inc(g["st_p"], 1)

                def values(i, n):
                    h, u = divmod(n, UNITS)
                    q, r = divmod(h, 4)
                    if r == 0 and u == 0 and q >= 2:
                        pe.wait_ge(g["ot_done"], 2 * GROUPS * i + 2 * q - 2)
                    pe.wait_ge(g["exp_done"], U * i + n + 1)
                    odd = 1 if u else 0
                    mm(bank[OW * r:OW * r + OW, 4 + 2 * (q % 2) + odd, :], va[:, 1 if u == 2 else 0, h, :], pt[:, n % 4, :],
                       start=u < 2, stop=u != 1).then_inc(g["pv_p"], 1)

                ot_v = ot[:, :, :].rearrange("p g (e w c) -> p g e w c", e=2, c=P)

                def heads_out(i, t):
                    if t == 0:
                        pe.wait_ge(g["ot_done"], 2 * GROUPS * (i + 1))
                    if t >= 2:
                        pe.wait_ge(g["norm_done"], NT * i + t - 1)
                    for q in range(GROUPS):
                        last = nc.tensor.transpose(bank[:, t % 2, q * P:(q + 1) * P], ot_v[:, q, t % 2, t // 2, :], consts.ident[:, :])
                    last.then_inc(g["on_t"], 1)

                def attn_t(i, t):
                    pe.wait_ge(g["norm_done"], NT * i + t + 1)
                    if t >= 2:
                        pe.wait_ge(g["of_lo"], NT * i + t - 1)
                    for d in range(DH):
                        last = nc.tensor.transpose(bank[:, 2 + t % 2, d * P:(d + 1) * P], o_sb[:, t % 2, d * P:(d + 1) * P], consts.ident[:, :])
                    last.then_inc(g["of_t"], 1)

                def out_project(i, t):
                    pe.wait_ge(g["of_lo"], NT * i + t + 1)
                    if t >= 2:
                        pe.wait_ge(route.x_done, NT * i + t - 1)
                    terms = [(a, b, d) for d in range(DH) for a, b in ((o_hi, w_lo), (o_lo, w_hi), (o_hi, w_hi))]
                    for n, (a, b, d) in enumerate(terms):
                        last = mm(bank[:, 4 + t % 2, 0:D], a[:, t % 2, d, :], b[:, 3, d, :], start=n == 0, stop=n == len(terms) - 1)
                    last.then_inc(g["out_p"], 1)

                pe.wait_ge(g["w_lo_done"], 1)
                pe.wait_ge(g["zero_done"], 5)
                def queries(i, t):
                    scores(i, t, [0])
                    if t + 1 < NT:
                        q_project(i, t + 1)
                    scores(i, t, [1])
                    if t:
                        q_packed(i, t - 1)
                    if pairs_of[t] > 2:
                        scores(i, t, [2])
                    if t + 1 < NT:
                        q_heads(i, t + 1)
                    if pairs_of[t] > 2:
                        scores(i, t, [3])

                def begin(i):
                    keys(i)
                    q_project(i, 0)
                    q_heads(i, 0)
                    for t in range(2):
                        queries(i, t)

                def rest(i, more, route_of):
                    for t in range(2, NT):
                        queries(i, t)
                    q_packed(i, NT - 1)
                    for n in range(U + 2):
                        if n == COUNT_AT and route_of is not None:
                            pe.wait_ge(g["ot_done"], 2 * GROUPS * i + 2 * (GROUPS - 1))
                            route.tensor(nc, pe, route_of, count_ps)
                        if n < U:
                            unit(i, n)
                        if n >= 2:
                            values(i, n - 2)
                    heads_out(i, 0)
                    for t in range(NT + 1):
                        if t + 1 < NT:
                            heads_out(i, t + 1)
                        if t < NT:
                            attn_t(i, t)
                        elif more:
                            key_products(i + 1, 0)
                        if t:
                            out_project(i, t - 1)
                        if more and t % 2 == 1:
                            xt(i + 1, [t // 2])

                xt(0)
                key_products(0, 0)
                begin(0)
                rest(0, True, None)
                begin(1)
                with pe.Fori(1, B - 1) as i:
                    rest(i, True, i - 1)
                    begin(i + 1)
                rest(B - 1, False, B - 2)
                route.tensor(nc, pe, B - 1, count_ps)

            @block.scalar
            def _(act):
                copy = lambda o, a: nc.scalar.activation(o, a, ACT.Copy)

                def xt(i, chunks=range(XT)):
                    for c in chunks:
                        half, d = divmod(c, DH)
                        act.wait_ge(g["xt_t"], XT * i + c + 1)
                        copy(xt_hi[:, d, half * 512:half * 512 + 512], bank[:, 6 + c % 2, :]).then_inc(g["xt_hi_done"], 1)

                def keys(i):
                    for kt in range(KT):
                        act.wait_ge(g["kv_p"], KT * i + kt + 1)
                        if kt:
                            act.wait_ge(g["kz_t"], 2 * KT * i + 2)
                        kb = bank[:, 2 * kt, 0:D].rearrange("p (h c) -> p h c", c=HD)
                        copy(kp[:, :, :].rearrange("p h (a c) -> p h a c", a=2)[:, :, :, 0:HD],
                             kb.unsqueeze(2).broadcast_to([P, HEADS, 2, HD]))
                        copy(kc[:, :], bank[:, 2 * kt, 0:D])
                        copy(va[:, kt, :, 0:HD], bank[:, 2 * kt + 1, 0:D].rearrange("p (h c) -> p h c", c=HD)).then_inc(g["kv_act"], 1)
                    for kt in range(KT):
                        for h in range(2):
                            act.wait_ge(g["kz_t"], 2 * KT * i + 2 * kt + h + 1)
                            for r in range(2):
                                copy(kz[HW * r:HW * r + HW, 8 * h + r:8 * h + r + 7:2, kt * P:(kt + 1) * P],
                                     bank[HW * r:HW * r + HW, 6 + h, :].rearrange("p (a k) -> p a k", k=P)).then_inc(g["kz_done"], 1)

                def q_plain(i, t):
                    act.wait_ge(g["q_p"], NT * i + t + 1)
                    copy(qc[:, t % 2, :], bank[:, 5, 0:D]).then_inc(g["q_act"], 1)

                def q_twice(i, t):
                    if t >= 2:
                        act.wait_ge(g["qp_t"], 2 * (NT * i + t) - 2)
                    src = bank[:, 5, 0:D].rearrange("p (h c) -> p h c", c=HD)
                    copy(qp[:, t % 2, :, 0:2 * HD].rearrange("p h (a c) -> p h a c", a=2),
                         src.unsqueeze(2).broadcast_to([P, HEADS, 2, HD])).then_inc(g["q_act"], 1)

                def q_heads(i, t):
                    act.wait_ge(g["qh_t"], NT * i + t + 1)
                    if t >= 2:
                        act.wait_ge(g["s_p"], SP_N * i + sum(pairs_of[:t - 1]))
                    copy(qht[:, t % 2, :, :], bank[:, 4, 0:2 * P].rearrange("p (e c) -> p e c", c=P)).then_inc(g["qh_done"], 1)

                def q_packed(i, t):
                    for h in range(2):
                        act.wait_ge(g["qp_t"], 2 * (NT * i + t) + h + 1)
                        copy(qpt[:, 4 * h:4 * h + 4, t * P:(t + 1) * P], bank[:, 6 + h, :].rearrange("p (a k) -> p a k", k=P)).then_inc(g["qp_done"], 1)

                act.wait_ge(g["w_lo_done"], 1)
                def queries(i, t):
                    if t + 1 < NT:
                        q_plain(i, t + 1)
                    if t:
                        q_packed(i, t - 1)
                    if t + 1 < NT:
                        q_twice(i, t + 1)
                        q_heads(i, t + 1)

                def begin(i):
                    keys(i)
                    q_plain(i, 0)
                    q_twice(i, 0)
                    q_heads(i, 0)
                    for t in range(2):
                        queries(i, t)

                def rest(i, more):
                    for t in range(2, NT):
                        queries(i, t)
                    q_packed(i, NT - 1)
                    for n in range(U):
                        act.wait_ge(g["st_p"], U * i + n + 1)
                        if n >= 4:
                            act.wait_ge(g["pv_p"], U * i + n - 3)
                        nc.scalar.activation(pt[:, n % 4, :], bank[:, n % 4, :], ACT.Exp, scale=HD ** -0.5).then_inc(g["exp_done"], 1)
                    for t in range(NT):
                        act.wait_ge(g["of_t"], NT * i + t + 1)
                        if t >= 2:
                            act.wait_ge(g["out_p"], NT * i + t - 1)
                        copy(o_hi[:, t % 2, :, :], bank[:, 2 + t % 2, 0:D].rearrange("p (d c) -> p d c", c=P)).then_inc(g["of_hi"], 1)
                        if more and t % 2 == 1:
                            xt(i + 1, [t // 2])

                xt(0)
                begin(0)
                with act.Fori(0, B - 1) as i:
                    rest(i, True)
                    begin(i + 1)
                rest(B - 1, False)

            @block.vector
            def _(dve):
                tt = nc.vector.tensor_tensor

                def stats_in(i):
                    dve.wait_ge(g["x_loaded"], 16 * i + 16)
                    ln.stats(nc, dve, i, x_in)

                def norm_in(i):
                    dve.wait_ge(g["xt_t"], XT * i)
                    ln.apply(nc, dve, i, x_in, xn)

                dve.wait_ge(g["w_in"], 64)
                raw = w_raw.rearrange("p d (w n) -> p w d n", n=D)
                for w in range(4):
                    nc.vector.tensor_copy(w_hi[:, w, :, :], raw[:, w]).then_inc(g["w_hi_done"], 1)
                dve.wait_ge(g["w_hi_done"], 4)
                for w in range(4):
                    last = tt(w_lo[:, w, :, :], raw[:, w], f32(w_hi[:, w, :, :]), ALU.subtract)
                last.then_inc(g["w_lo_done"], 1)
                nc.vector.memset(f32(qp[:, :, :, :]), 0.0).then_inc(g["zero_done"], 1)
                nc.vector.memset(f32(kp[:, :, :]), 0.0).then_inc(g["zero_done"], 1)
                nc.vector.memset(f32(kz[:, :, :]), 0.0).then_inc(g["zero_done"], 1)
                nc.vector.memset(va[:, :, :, :], 0.0).then_inc(g["zero_done"], 1)
                dve.wait_ge(g["zero_done"], 4)
                nc.vector.memset(f32(kp[:, :, 3 * HD:3 * HD + 1]), 1.0)
                nc.vector.memset(va[:, :, :, HD:HD + 1], 1.0).then_inc(g["zero_done"], 1)
                stats_in(0)
                route.prepare(nc, dve)
                norm_in(0)

                def xt(i, chunks=range(XT)):
                    for c in chunks:
                        half, d = divmod(c, DH)
                        dve.wait_ge(g["xt_hi_done"], XT * i + c + 1)
                        tt(xt_lo[:, d, half * 512:half * 512 + 512], bank[:, 6 + c % 2, :],
                           f32(xt_hi[:, d, half * 512:half * 512 + 512]), ALU.subtract).then_inc(g["xt_lo_done"], 1)

                def keys(i):
                    for kt in range(KT):
                        dve.wait_ge(g["kv_act"], KT * i + kt + 1)
                        tt(kp[:, :, HD:2 * HD], bank[:, 2 * kt, 0:D].rearrange("p (h c) -> p h c", c=HD),
                           f32(kp[:, :, 0:HD]), ALU.subtract).then_inc(g["kp_lo"], 1)
                        dve.wait_ge(g["km_t"], KT * i + kt + 1)
                        for e in range(2):
                            tt(km[:, e, :, kt * P:(kt + 1) * P],
                               bank[:, 5 - kt, e * P:(e + 1) * P].unsqueeze(1).broadcast_to([P, 8, P]),
                               consts.head_rows[:, :].unsqueeze(2).broadcast_to([P, 8, P]), ALU.mult).then_inc(g["km_done"], 1)

                def q_low(i, t):
                    dve.wait_ge(g["q_act"], 2 * (NT * i + t) + 2)
                    tt(qp[:, t % 2, :, 2 * HD:3 * HD], bank[:, 5, 0:D].rearrange("p (h c) -> p h c", c=HD),
                       f32(qp[:, t % 2, :, 0:HD]), ALU.subtract).then_inc(g["q_lo"], 1)

                def greatest(i, t):
                    nk = P * (1 + t % 2)
                    hp = 1024 // nk
                    for j in range(pairs_of[t]):
                        n = sum(pairs_of[:t]) + j
                        dve.wait_ge(g["s_p"], SP_N * i + n + 1)
                        if t >= 2 and j == 0:
                            dve.wait_ge(g["qp_t"], 2 * (NT * i + t) - 2)
                        nc.vector.tensor_reduce(
                            qp[:, t % 2, j * hp:(j + 1) * hp, 3 * HD:3 * HD + 1].rearrange("p h a -> p (h a)"),
                            bank[:, 2 * (n % 2):2 * (n % 2) + 2, :].rearrange("p b (h k) -> p (b h) k", k=nk),
                            AX.X, ALU.max, negate=True).then_inc(g["s_max"], 1)

                def rest(i, more, route_of):
                    for t in range(2, NT):
                        greatest(i, t)
                        if t + 1 < NT:
                            q_low(i, t + 1)
                    if more:
                        stats_in(i + 1)
                    if route_of is not None:
                        route.vector_stats(nc, dve, route_of)
                    if more:
                        norm_in(i + 1)
                    if route_of is not None:
                        route.vector_norm(nc, dve, route_of)
                        route.vector_choose(nc, dve, route_of)
                    for q in range(GROUPS):
                        if q == GROUPS - 1 and route_of is not None:
                            route.vector_slots(nc, dve, route_of, count_ps)
                        for e in range(2):
                            dve.wait_ge(g["pv_p"], U * i + 4 * UNITS * (q + 1))
                            nc.vector.tensor_copy(ot[:, q, e * 512:e * 512 + 512], bank[:, 4 + 2 * (q % 2) + e, :]).then_inc(g["ot_done"], 1)

                    def norm_out(t):
                        dve.wait_ge(g["on_t"], NT * i + t + 1)
                        v = bank[:, t % 2, :].rearrange("p (h c) -> p h c", c=OW)
                        if t >= 2:
                            dve.wait_ge(g["norm_done"], NT * i + t - 1)
                        nc.vector.reciprocal(rden[:, t % 2, :].unsqueeze(2), v[:, :, HD:HD + 1]).then_inc(g["norm_r"], 1)
                        dve.wait_ge(g["norm_r"], NT * i + t + 1)
                        if t >= 2:
                            dve.wait_ge(g["of_t"], NT * i + t - 1)
                        tt(o_sb[:, t % 2, :].rearrange("p (h c) -> p h c", c=HD), v[:, :, 0:HD],
                           rden[:, t % 2, :].unsqueeze(2).broadcast_to([P, HEADS, HD]), ALU.mult).then_inc(g["norm_done"], 1)

                    def attn_low(t):
                        dve.wait_ge(g["of_hi"], NT * i + t + 1)
                        if t >= 2:
                            dve.wait_ge(g["out_p"], NT * i + t - 1)
                        tt(o_lo[:, t % 2, :, :], bank[:, 2 + t % 2, 0:D].rearrange("p (d c) -> p d c", c=P),
                           f32(o_hi[:, t % 2, :, :]), ALU.subtract).then_inc(g["of_lo"], 1)

                    def new_x(t):
                        dve.wait_ge(g["out_p"], NT * i + t + 1)
                        if t == 0:
                            dve.wait_ge(g["res_loaded"], 16 * i + 16)
                            dve.wait_ge(route.sent, 16 * NT * i)
                        tt(row[:, t, 0:D], bank[:, 4 + t % 2, 0:D], x_res[:, t, :], ALU.add).then_inc(route.x_done, 1)

                    for t in range(NT + 2):
                        if t < NT:
                            norm_out(t)
                        if 1 <= t <= NT:
                            attn_low(t - 1)
                        if t >= 2:
                            new_x(t - 2)
                        if more and t and t % 2 == 0:
                            xt(i + 1, [t // 2 - 1])

                def begin(i):
                    keys(i)
                    q_low(i, 0)
                    for t in range(2):
                        greatest(i, t)
                        q_low(i, t + 1)

                xt(0)
                begin(0)
                rest(0, True, None)
                begin(1)
                with dve.Fori(1, B - 1) as i:
                    rest(i, True, i - 1)
                    begin(i + 1)
                rest(B - 1, False, B - 2)
                route.vector_stats(nc, dve, B - 1)
                route.vector_norm(nc, dve, B - 1)
                route.vector_choose(nc, dve, B - 1)
                route.vector_slots(nc, dve, B - 1, count_ps)
                route.vector_end(nc, dve, B)


ORDER = 2
FREQS = 3
ENC = 2 * FREQS + 1
FO = 64
BLK = 32
NBLK = S // BLK
LAGS = S // P
PADB = 3
BW = NBLK + 4
SEQW = B * BW
FW = (P + BLK) * LAGS
CH = 4
CHUNKS = BLK // CH


def filters(nc, tag, times, phases, freqs, w1, b1, w2, b2, w3, b3, decay, arranged):
    TWO_PI = 6.283185
    ROUND = 1.5 * 2 ** 23
    with ExitStack() as ctx:
        m = Memory(nc, ctx, tag)
        t_row = m.sb("t_row", [P, S])
        ph = m.sb("ph", [ENC, 3])
        fr = m.sb("fr", [ENC, ORDER])
        turn = m.sb("turn", [ENC, ORDER, S])
        near = m.sb("near", [ENC, ORDER, S])
        enc = m.sb("enc", [ENC, ORDER, S])
        w1_sb = m.sb("w1", [ENC, ORDER, FO])
        w2_sb = m.sb("w2", [FO, ORDER, FO])
        w3_sb = m.sb("w3", [FO, ORDER, D])
        b12 = m.sb("b12", [FO, 2, ORDER])
        b3_sb = m.sb("b3", [P, ORDER, DH])
        dec = m.sb("dec", [P, ORDER, DH])
        ndec = m.sb("ndec", [P, ORDER, DH])
        h1 = m.sb("h1", [FO, S])
        h2 = m.sb("h2", [FO, S])
        win = m.sb("win", [P, ORDER, DH, S])
        flt = m.sb("flt", [P, DH, S + BLK])
        arr = m.sb("arr", [P, DH, P + BLK, LAGS])
        h_ps = m.ps("h_ps", [P, 2, 512])
        f_ps = m.ps("f_ps", [P, DH, 2, 512])
        loaded, fr_set, turned, enc_done, l1_p, l1_done, l2_p, l2_done, l3_p, win_done, flt_done, zeroed, arr_done, \
            stored, ndec_done, sine_done = (m.sem(n) for n in ("loaded fr_set turned enc_done l1_p l1_done l2_p l2_done l3_p win_done "
                                                    "flt_done zeroed arr_done stored ndec_done sine_done").split())
        LOADS = 12

        with nc.Block() as block:

            @block.sync
            def _(sp):
                sp.dma_start(t_row[:, :], times.broadcast_to([P, S])).then_inc(loaded, 16)
                sp.dma_start(ph[:, :], phases).then_inc(loaded, 16)
                for k in range(2):
                    sp.dma_start(fr[FREQS * k:FREQS * k + FREQS, :], freqs).then_inc(loaded, 16)
                sp.dma_start(w1_sb[:, :, :], w1.rearrange("o k n -> k o n")).then_inc(loaded, 16)
                sp.dma_start(w2_sb[:, :, :], w2.rearrange("o k n -> k o n")).then_inc(loaded, 16)
                sp.dma_start(w3_sb[:, :, :], w3.rearrange("o k n -> k o n")).then_inc(loaded, 16)
                sp.dma_start(b12[:, 0, :], b1).then_inc(loaded, 16)
                sp.dma_start(b12[:, 1, :], b2).then_inc(loaded, 16)
                sp.dma_start(b3_sb[:, :, :], b3).then_inc(loaded, 16)
                sp.dma_start(dec[:, :, :], decay).then_inc(loaded, 16)
                sp.dma_start(fr[2 * FREQS:ENC, :], freqs[0:1, :]).then_inc(loaded, 16)
                for o in range(ORDER):
                    for d in range(DH):
                        sp.wait_ge(arr_done, DH * o + d + 1)
                        for q in range(4):
                            sp.dma_start(arranged[o, d, :, q, :, :], arr[BLK * q:BLK * q + BLK, d, :, :].rearrange("p a b -> p (a b)")).then_inc(stored, 16)
                sp.wait_ge(stored, 64 * ORDER * DH)

            @block.vector
            def _(dve):
                dve.wait_ge(loaded, 16 * LOADS)
                nc.vector.tensor_scalar(fr[:, :], fr[:, :], ph[:, 2:3], None, ALU.mult).then_inc(fr_set, 1)
                dve.wait_ge(fr_set, 1)
                nc.vector.tensor_scalar(ndec[:, :, :], dec[:, :, :], -1.0, None, ALU.mult).then_inc(ndec_done, 1)
                nc.vector.memset(flt[:, :, S:S + BLK], 0.0).then_inc(zeroed, 1)
                dve.wait_ge(ndec_done, 1)
                nc.vector.tensor_tensor(ndec[:, :, :], ndec[:, :, :], dec[:, :, :], ALU.min).then_inc(ndec_done, 1)
                dve.wait_ge(ndec_done, 2)
                nc.vector.tensor_scalar(ndec[:, :, :], ndec[:, :, :], float(S), None, ALU.mult).then_inc(ndec_done, 1)
                for o in range(ORDER):
                    n = 4 * o
                    nc.vector.tensor_scalar(turn[:, o, :], t_row[0:ENC, :], fr[:, o:o + 1], ph[:, 0:1], ALU.mult, ALU.add).then_inc(turned, 1)
                    dve.wait_ge(turned, n + 1)
                    nc.vector.tensor_scalar(near[:, o, :], turn[:, o, :], ROUND, None, ALU.add).then_inc(turned, 1)
                    dve.wait_ge(turned, n + 2)
                    nc.vector.tensor_scalar(near[:, o, :], near[:, o, :], -ROUND, None, ALU.add).then_inc(turned, 1)
                    dve.wait_ge(turned, n + 3)
                    nc.vector.tensor_tensor(turn[:, o, :], turn[:, o, :], near[:, o, :], ALU.subtract).then_inc(turned, 1)
                dve.wait_ge(turned, 4 * ORDER)
                nc.vector.tensor_scalar(near[:, 0, :], t_row[0:ENC, :], ph[:, 1:2], None, ALU.mult).then_inc(turned, 1)
                dve.wait_ge(turned, 4 * ORDER + 1)
                for o in range(ORDER):
                    dve.wait_ge(sine_done, o + 1)
                    nc.vector.tensor_tensor(enc[:, o, :], enc[:, o, :], near[:, 0, :], ALU.add).then_inc(enc_done, 1)
                for o in range(ORDER):
                    for d in range(DH):
                        dve.wait_ge(l3_p, DH * o + d + 1)
                        dve.wait_ge(win_done, DH * o + d + 1)
                        if o:
                            dve.wait_ge(arr_done, DH * (o - 1) + d + 1)
                        nc.vector.scalar_tensor_tensor(flt[:, d, 0:S], f_ps[:, d, :, :].rearrange("p a b -> p (a b)"),
                                                       b3_sb[:, o, d:d + 1], win[:, o, d, :], ALU.add, ALU.mult).then_inc(flt_done, 1)
                        dve.wait_ge(flt_done, DH * o + d + 1)
                        dve.wait_ge(zeroed, 1)
                        if o:
                            dve.wait_ge(stored, 64 * DH)
                        for k in range(LAGS):
                            last = nc.vector.tensor_copy(arr[:, d, :, k:k + 1].rearrange("p w a -> p (w a)"), flt[:, d, P * k:P * k + P + BLK])
                        last.then_inc(arr_done, 1)

            @block.scalar
            def _(act):
                act.wait_ge(loaded, 16 * LOADS)
                act.wait_ge(ndec_done, 3)
                for o in range(ORDER):
                    for d in range(DH):
                        nc.scalar.activation(win[:, o, d, :], t_row[:, :], ACT.Exp, scale=ndec[:, o, d:d + 1]).then_inc(win_done, 1)
                for o in range(ORDER):
                    act.wait_ge(turned, 4 * o + 4)
                    nc.scalar.activation(enc[:, o, :], turn[:, o, :], ACT.Sin, scale=TWO_PI).then_inc(sine_done, 1)
                for o in range(ORDER):
                    for h in range(2):
                        act.wait_ge(l1_p, 2 * o + h + 1)
                        if o:
                            act.wait_ge(l2_p, 2 * o)
                        nc.scalar.activation(h1[:, h * 512:h * 512 + 512], h_ps[0:FO, h, :], ACT.Gelu, bias=b12[:, 0, o:o + 1]).then_inc(l1_done, 1)
                    for h in range(2):
                        act.wait_ge(l2_p, 2 * o + h + 1)
                        if o:
                            act.wait_ge(l3_p, DH * o)
                        nc.scalar.activation(h2[:, h * 512:h * 512 + 512], h_ps[0:FO, h, :], ACT.Gelu, bias=b12[:, 1, o:o + 1]).then_inc(l2_done, 1)

            @block.tensor
            def _(pe):
                mm = nc.tensor.matmul
                for o in range(ORDER):
                    pe.wait_ge(enc_done, o + 1)
                    if o:
                        pe.wait_ge(l2_done, 2 * o)
                    for h in range(2):
                        mm(h_ps[0:FO, h, :], w1_sb[:, o, :], enc[:, o, h * 512:h * 512 + 512], start=True, stop=True).then_inc(l1_p, 1)
                    for h in range(2):
                        pe.wait_ge(l1_done, 2 * o + 2)
                        mm(h_ps[0:FO, h, :], w2_sb[:, o, :], h1[:, h * 512:h * 512 + 512], start=True, stop=True).then_inc(l2_p, 1)
                    for d in range(DH):
                        pe.wait_ge(l2_done, 2 * o + 2)
                        if o:
                            pe.wait_ge(flt_done, DH * (o - 1) + d + 1)
                        for h in range(2):
                            last = mm(f_ps[:, d, h, :], w3_sb[:, o, d * P:(d + 1) * P], h2[:, h * 512:h * 512 + 512], start=True, stop=True)
                        last.then_inc(l3_p, 1)


def projections(nc, tag, consts, x, in_w, in_b, conv_w, conv_b, gate_w, gate_b, v_blocks, gates):
    MB = (ORDER + 1) * DH
    with ExitStack() as ctx:
        m = Memory(nc, ctx, tag)
        x_in = m.sb("x_in", [P, NT, D])
        xt_hi = m.sb("xt_hi", [P, DH, S], F32R)
        xt_lo = m.sb("xt_lo", [P, DH, S], F32R)
        iw_hi = m.sb("iw_hi", [P, DH, 3 * D], F32R)
        iw_lo = m.sb("iw_lo", [P, DH, 3 * D], F32R)
        gw_hi = m.sb("gw_hi", [P, ORDER, DH, D], F32R)
        gw_lo = m.sb("gw_lo", [P, ORDER, DH, D], F32R)
        cols = m.sb("cols", [P, MB + ORDER * DH * 5])
        in_bc = cols[:, 0:MB]
        cw = cols[:, MB:MB + 12].rearrange("p (o d k) -> p o d k", o=ORDER, d=DH)
        cb = cols[:, MB + 12:MB + 16].rearrange("p (o d) -> p o d", o=ORDER)
        gb = cols[:, MB + 16:MB + 20].rearrange("p (o d) -> p o d", o=ORDER)
        vb = m.sb("vb", [P, DH, BLK, B, BW])
        vt = m.sb("vt", [P, S])
        vs = m.sb("vs", [P, DH, NBLK, BLK])
        u = m.sb("u", [P, 2, S + 2])
        tap = m.sb("tap", [P, 2, S])
        xc = m.sb("xc", [P, ORDER, DH, S])
        xc_hi = m.sb("xc_hi", [P, ORDER, DH, S], F32R)
        xc_lo = m.sb("xc_lo", [P, ORDER, DH, S], F32R)
        sg = m.sb("sg", [P, 2, S])
        gate = (tap, sg)
        w_raw = xc[:, 0].rearrange("p d s -> p (d s)")
        w_raw2 = xc[:, 1].rearrange("p d s -> p (d s)")
        bank = m.ps("bank", [P, 8, 512])
        ln = LayerNorm(m, "ln", consts, NT)
        names = """w_in c_in w_hi w_lo zeroed x_loaded xt_t xt_hi_done xt_lo_done v_p v_act v_blk u_p u_act tap0 tap1
            xc_done xc_hi_done xc_lo_done g_p sg_done g_done v_put v_stored"""
        g = {n: m.sem(n) for n in names.split()}
        held = m.sem("held")
        g_stored = [[m.sem(f"g_stored{o}{d}") for d in range(DH)] for o in range(ORDER)]
        XT = 2 * DH

        with nc.Block() as block:

            @block.sync
            def _(sp):
                sp.dma_start(w_raw[:, 0:DH * 3 * D].rearrange("p (c n) -> p c n", c=DH),
                             in_w.rearrange("(c p) n -> p c n", p=P)).then_inc(g["w_in"], 16)
                for o in range(ORDER):
                    sp.dma_start(w_raw2[:, o * DH * D:(o + 1) * DH * D].rearrange("p (c n) -> p c n", c=DH),
                                 gate_w[o].rearrange("(c p) n -> p c n", p=P)).then_inc(g["w_in"], 16)
                for dst, src in ((in_bc, in_b), (cw, conv_w), (cb, conv_b), (gb, gate_b)):
                    sp.dma_start(dst, src).then_inc(g["c_in"], 16)

                def load(i):
                    if not isinstance(i, int):
                        sp.wait_ge(g["xt_t"], XT * i)
                        sp.sem_inc(held, 1)
                    sp.dma_start(x_in[:, :, :], x[bass.ds(i * S, S), :].rearrange("(t p) c -> p t c", p=P)).then_inc(g["x_loaded"], 16)

                def store(i):
                    for n in range(ORDER * DH):
                        o, d = divmod(n, DH)
                        sp.wait_ge(g["g_done"], ORDER * DH * i + n + 1)
                        sp.sem_inc(held, 1)
                        sp.dma_start(gates[o, d, :, bass.ds(i * S, S)], gate[o][:, d, :]).then_inc(g_stored[o][d], 16)

                load(0)
                with sp.Fori(0, B - 1) as i:
                    load(i + 1)
                    store(i)
                sp.wait_ge(g["v_put"], DH * B)
                for d in range(DH):
                    sp.dma_start(v_blocks[d], vb[:, d].rearrange("p c b k -> p (c b k)")).then_inc(g["v_stored"], 16)
                store(B - 1)
                sp.wait_ge(g["v_stored"], 16 * DH)
                for o in range(ORDER):
                    for d in range(DH):
                        sp.wait_ge(g_stored[o][d], 16 * B)

            @block.gpsimd
            def _(pool):
                every = vb[:, :, :, :, :].rearrange("p a b c k -> p (a b c) k")
                pool.memset(every[:, :, 0:PADB], 0.0)
                pool.memset(every[:, :, PADB + NBLK:BW], 0.0).then_inc(g["zeroed"], 1)
                ln.power(nc, pool, 0)
                with pool.Fori(0, B - 1) as i:
                    ln.power(nc, pool, i + 1)

            @block.tensor
            def _(pe):
                mm = nc.tensor.matmul

                def xt(i):
                    for c in range(XT):
                        half, d = divmod(c, DH)
                        if c == 0:
                            pe.wait_ge(ln.done, NT * i + NT)
                        pe.wait_ge(g["xt_lo_done"], XT * i + c + 1)
                        for t in range(4):
                            last = nc.tensor.transpose(bank[:, 6 + c % 2, t * P:(t + 1) * P],
                                                       x_in[:, 4 * half + t, d * P:(d + 1) * P], consts.ident[:, :])
                        last.then_inc(g["xt_t"], 1)

                def product(out, hi, lo, w_h, w_l, h, col):
                    terms = [(a, b, d) for d in range(DH) for a, b in ((w_h, lo), (w_l, hi), (w_h, hi))]
                    for n, (a, b, d) in enumerate(terms):
                        last = mm(out, a[:, d, col:col + P], b[:, d, h * 512:h * 512 + 512], start=n == 0, stop=n == len(terms) - 1)
                    return last

                def control(i, o, d, at):
                    for h in range(2):
                        last = product(bank[:, at + h, :], xt_hi, xt_lo, iw_hi, iw_lo, h, (1 + o) * D + d * P)
                    last.then_inc(g["u_p"], 1)

                def value(i, d, at):
                    for h in range(2):
                        last = product(bank[:, at + h, :], xt_hi, xt_lo, iw_hi, iw_lo, h, d * P)
                    last.then_inc(g["v_p"], 1)

                def gates_of(i, o, d, at):
                    if d == 0:
                        pe.wait_ge(g["xc_lo_done"], 4 * i + 2 * o + 2)
                    for h in range(2):
                        last = product(bank[:, at + h, :], xc_hi[:, o], xc_lo[:, o], gw_hi[:, o], gw_lo[:, o], h, d * P)
                    last.then_inc(g["g_p"], 1)

                def sequence(i, more):
                    pe.wait_ge(g["xt_lo_done"], XT * i + XT + 2)
                    pe.wait_ge(g["sg_done"], 4 * i + 1)
                    control(i, 0, 0, 0)
                    pe.wait_ge(g["sg_done"], 4 * i + 4)
                    control(i, 0, 1, 2)
                    pe.wait_ge(g["sg_done"], 4 * i + 3)
                    value(i, 0, 4)
                    pe.wait_ge(g["u_act"], 4 * i + 1)
                    value(i, 1, 0)
                    pe.wait_ge(g["u_act"], 4 * i + 2)
                    control(i, 1, 0, 2)
                    pe.wait_ge(g["v_act"], DH * i + 1)
                    control(i, 1, 1, 4)
                    pe.wait_ge(g["v_act"], DH * i + 2)
                    gates_of(i, 0, 0, 0)
                    pe.wait_ge(g["u_act"], 4 * i + 3)
                    gates_of(i, 0, 1, 2)
                    pe.wait_ge(g["u_act"], 4 * i + 4)
                    gates_of(i, 1, 0, 4)
                    if more:
                        xt(i + 1)
                    pe.wait_ge(g["sg_done"], 4 * i + 6)
                    gates_of(i, 1, 1, 2)

                pe.sem_inc(g["g_p"], 4)
                pe.wait_ge(g["w_lo"], 3)
                xt(0)
                with pe.Fori(0, B - 1) as i:
                    sequence(i, True)
                sequence(B - 1, False)

            @block.scalar
            def _(act):
                act.wait_ge(g["c_in"], 64)
                act.wait_ge(g["w_lo"], 3)
                act.wait_ge(g["zeroed"], 1)
                act.sem_inc(g["sg_done"], 4)
                both = lambda at: bank[:, at:at + 2, :].rearrange("p a b -> p (a b)")

                def xt(i):
                    for c in range(XT):
                        half, d = divmod(c, DH)
                        act.wait_ge(g["xt_t"], XT * i + c + 1)
                        nc.scalar.activation(xt_hi[:, d, half * 512:half * 512 + 512], bank[:, 6 + c % 2, :], ACT.Copy).then_inc(g["xt_hi_done"], 1)

                def control(i, o, d, at):
                    k = 2 * o + d
                    act.wait_ge(g["u_p"], 4 * i + k + 1)
                    act.wait_ge(g["xc_done"], 4 * i + o * (d + 1))
                    nc.scalar.activation(u[:, d, 1:S + 1], both(at), ACT.Identity,
                                         bias=in_bc[:, DH + k:DH + k + 1]).then_inc(g["u_act"], 1)
                    act.wait_ge(g["u_act"], 4 * i + k + 1)
                    if o == 0:
                        act.wait_ge(g_stored[0][d], 16 * i)
                    nc.scalar.activation(tap[:, d, :], u[:, d, 0:S], ACT.Identity, bias=cb[:, o, d:d + 1],
                                         scale=cw[:, o, d, 0:1]).then_inc(g["tap0"], 1)

                def value(i, d, at):
                    act.wait_ge(g["v_p"], DH * i + d + 1)
                    act.wait_ge(g["v_blk"], DH * i + d)
                    nc.scalar.activation(vt[:, :], both(at), ACT.Identity, bias=in_bc[:, d:d + 1]).then_inc(g["v_act"], 1)

                def high(i, o, d):
                    act.wait_ge(g["xc_done"], 4 * i + 2 * o + d + 1)
                    act.wait_ge(g["g_p"], 4 * i + 2 * o + 2)
                    nc.scalar.activation(xc_hi[:, o, d, :], xc[:, o, d, :], ACT.Copy).then_inc(g["xc_hi_done"], 1)

                def gates_of(i, o, d, at):
                    act.wait_ge(g["g_p"], 4 * i + 2 * o + d + 5)
                    if o == 0:
                        act.wait_ge(g["xc_done"], 4 * i + d + 3)
                    else:
                        act.wait_ge(g_stored[1][d], 16 * i)
                    nc.scalar.activation(gate[o][:, d, :], both(at), ACT.Sigmoid, bias=gb[:, o, d:d + 1]).then_inc(g["sg_done"], 1)

                def put(i):
                    for d in range(DH):
                        act.wait_ge(g["v_blk"], DH * i + d + 1)
                        at = slice(i, i + 1) if isinstance(i, int) else bass.ds(i, 1)
                        nc.scalar.activation(vb[:, d, :, at, PADB:PADB + NBLK].rearrange("p c b k -> p c (b k)"),
                                             vs[:, d, :, :].rearrange("p k c -> p c k"), ACT.Copy).then_inc(g["v_put"], 1)

                def sequence(i, more):
                    control(i, 0, 0, 0)
                    control(i, 0, 1, 2)
                    high(i, 0, 0)
                    value(i, 0, 4)
                    high(i, 0, 1)
                    value(i, 1, 0)
                    if not more:
                        put(i)
                    control(i, 1, 0, 2)
                    control(i, 1, 1, 4)
                    high(i, 1, 0)
                    high(i, 1, 1)
                    gates_of(i, 0, 0, 0)
                    gates_of(i, 0, 1, 2)
                    if more:
                        xt(i + 1)
                    if more:
                        put(i)
                    gates_of(i, 1, 0, 4)
                    gates_of(i, 1, 1, 2)

                xt(0)
                with act.Fori(0, B - 1) as i:
                    sequence(i, True)
                sequence(B - 1, False)

            @block.vector
            def _(dve):
                tt = nc.vector.tensor_tensor
                stt = nc.vector.scalar_tensor_tensor
                dve.sem_inc(g["xt_lo_done"], 2)

                def stats(i):
                    dve.wait_ge(g["x_loaded"], 16 * i + 16)
                    ln.stats(nc, dve, i, x_in)

                dve.wait_ge(g["w_in"], 48)
                raw_i = w_raw[:, 0:DH * 3 * D].rearrange("p (c n) -> p c n", c=DH)
                raw_g = w_raw2[:, 0:ORDER * DH * D].rearrange("p (o c n) -> p o c n", o=ORDER, c=DH)
                nc.vector.tensor_copy(iw_hi[:, :, :], raw_i).then_inc(g["w_hi"], 1)
                for o in range(ORDER):
                    nc.vector.tensor_copy(gw_hi[:, o], raw_g[:, o]).then_inc(g["w_hi"], 1)
                dve.wait_ge(g["w_hi"], 3)
                tt(iw_lo[:, :, :], raw_i, f32(iw_hi[:, :, :]), ALU.subtract).then_inc(g["w_lo"], 1)
                for o in range(ORDER):
                    tt(gw_lo[:, o], raw_g[:, o], f32(gw_hi[:, o]), ALU.subtract).then_inc(g["w_lo"], 1)
                nc.vector.memset(u[:, :, :], 0.0).then_inc(g["w_hi"], 1)
                stats(0)
                ln.apply(nc, dve, 0, x_in, x_in)
                dve.wait_ge(g["w_hi"], 4)
                dve.wait_ge(g["w_lo"], 3)
                dve.wait_ge(g["zeroed"], 1)

                def xt(i):
                    for c in range(XT):
                        half, d = divmod(c, DH)
                        dve.wait_ge(g["xt_hi_done"], XT * i + c + 1)
                        tt(xt_lo[:, d, half * 512:half * 512 + 512], bank[:, 6 + c % 2, :],
                           f32(xt_hi[:, d, half * 512:half * 512 + 512]), ALU.subtract).then_inc(g["xt_lo_done"], 1)

                def control(i, o, d):
                    k = 4 * i + 2 * o + d
                    dve.wait_ge(g["tap0"], k + 1)
                    stt(xc[:, o, d, :], u[:, d, 1:S + 1], cw[:, o, d, 1:2], tap[:, d, :], ALU.mult, ALU.add).then_inc(g["tap1"], 1)
                    dve.wait_ge(g["tap1"], k + 1)
                    stt(xc[:, o, d, :], u[:, d, 2:S + 2], cw[:, o, d, 2:3], xc[:, o, d, :], ALU.mult, ALU.add).then_inc(g["xc_done"], 1)

                def low(i, o, d):
                    dve.wait_ge(g["xc_hi_done"], 4 * i + 2 * o + d + 1)
                    tt(xc_lo[:, o, d, :], xc[:, o, d, :], f32(xc_hi[:, o, d, :]), ALU.subtract).then_inc(g["xc_lo_done"], 1)

                def blocks(i, d):
                    dve.wait_ge(g["v_act"], DH * i + d + 1)
                    dve.wait_ge(g["v_put"], DH * i)
                    nc.vector.transpose(vs[:, d, :, :], vt[:, :].rearrange("p (k s) -> p k s", s=BLK)).then_inc(g["v_blk"], 1)

                def gated(i, o, d):
                    dve.wait_ge(g["sg_done"], 4 * i + 2 * o + d + 5)
                    tt(gate[o][:, d, :], gate[o][:, d, :], xc[:, o, d, :], ALU.mult).then_inc(g["g_done"], 1)

                def sequence(i, more):
                    dve.wait_ge(g["g_done"], 4 * i)
                    control(i, 0, 0)
                    control(i, 0, 1)
                    low(i, 0, 0)
                    blocks(i, 0)
                    low(i, 0, 1)
                    blocks(i, 1)
                    control(i, 1, 0)
                    control(i, 1, 1)
                    if more:
                        stats(i + 1)
                    low(i, 1, 0)
                    low(i, 1, 1)
                    if more:
                        ln.apply(nc, dve, i + 1, x_in, x_in)
                    gated(i, 0, 0)
                    gated(i, 0, 1)
                    if more:
                        xt(i + 1)
                    gated(i, 1, 0)
                    gated(i, 1, 1)

                xt(0)
                with dve.Fori(0, B - 1) as i:
                    sequence(i, True)
                sequence(B - 1, False)


def convolutions(nc, tag, arranged, v_blocks, gates, v_mid, v_out):
    ROUNDS = ORDER * DH
    PER = CHUNKS
    with ExitStack() as ctx:
        m = Memory(nc, ctx, tag)
        tp = m.sb("tp", [P, 2, 4, CH, BLK * LAGS])
        vi = m.sb("vi", [P, 2, 4, CH * SEQW])
        yc = m.sb("yc", [P, 2, BLK, B * NBLK])
        yt = m.sb("yt", [P, 2, S])
        gt = m.sb("gt", [P, 4, S])
        vn = m.sb("vn", [P, 2, S])
        vb = m.sb("vb", [P, BLK, B, BW])
        y_ps = m.ps("y_ps", [P, 4, 2, B * NBLK])
        t_loaded = [m.sem(f"t_loaded{n}") for n in range(2)]
        v_loaded = [m.sem(f"v_loaded{n}") for n in range(2)]
        y_p, y_act, yt_done, vn_done, vb_done, mid_stored, zeroed, held = (
            m.sem(n) for n in "y_p y_act yt_done vn_done vb_done mid_stored zeroed held".split())
        act_moved, dve_moved, mid_first = m.sem("act_moved"), m.sem("dve_moved"), m.sem("mid_first")
        g_loaded = [m.sem(f"g_loaded{n}") for n in range(4)]
        out_stored = [m.sem(f"out_stored{n}") for n in range(2)]

        with nc.Block() as block:

            @block.sync
            def _(sp):
                def chunk(r, c, k):
                    o, d = divmod(r, DH)
                    n = r * PER + c
                    if isinstance(c, int) and n < 2:
                        pass
                    else:
                        sp.wait_ge(y_p, n - 1)
                        sp.sem_inc(held, 1)
                    def windows():
                        src = bass.AP(arranged.tensor, r * P * FW + c * (4 * CH * FW),
                                      [[LAGS, P], [FW, 4 * CH], [1, BLK * LAGS]])
                        sp.dma_start(tp[:, k].rearrange("p q c n -> p (q c) n"), src).then_inc(t_loaded[k], 16)

                    def inputs():
                        src = bass.AP((v_mid if o else v_blocks).tensor, d * P * BLK * SEQW + c * (CH * SEQW),
                                      [[BLK * SEQW, BLK], [BLK * BLK * SEQW, 4], [1, CH * SEQW]])
                        sp.dma_start(vi[0:BLK, k], src).then_inc(v_loaded[k], 16)

                    if o and isinstance(c, int) and c == 0:
                        sp.wait_ge(mid_first, 16 * (r - DH + 1))
                    inputs()
                    windows()

                for r in range(ROUNDS):
                    for k in range(2):
                        chunk(r, k, k)
                    if r >= DH:
                        sp.wait_ge(mid_stored, 16 * (r - DH + 1))
                    with sp.Fori(1, PER // 2) as i:
                        for k in range(2):
                            chunk(r, i * 2 + k, k)

            @block.tensor
            def _(pe):
                for r in range(ROUNDS):
                    def pair(i, r=r):
                        for k in range(2):
                            n = r * PER + i * 2 + k
                            pe.wait_ge(t_loaded[k], 16 * (r * PER // 2) + i * 16 + 16)
                            pe.wait_ge(v_loaded[k], 16 * (r * PER // 2) + i * 16 + 16)
                            pe.wait_ge(act_moved, 2 * n + 2)
                            pe.wait_ge(dve_moved, 2 * n + 2)
                            pe.wait_ge(y_act, n * 2 + 2)
                            for c in range(CH):
                                bk, at = 2 * k + c // 2, c % 2
                                for j in range(LAGS):
                                    w = NBLK - 4 * j
                                    for q in range(4):
                                        out = y_ps[BLK * q:BLK * q + BLK, bk, at, :].rearrange("p (b i) -> p b i", b=B)[:, :, 4 * j:NBLK]
                                        lhs = tp[:, k, q, c, :].rearrange("p (w l) -> p w l", l=LAGS)[:, :, LAGS - 1 - j]
                                        rhs = vi[:, k, q, c * SEQW:(c + 1) * SEQW].rearrange("p (b i) -> p b i", b=B)[:, :, 0:w]
                                        last = nc.tensor.matmul(out, lhs, rhs, start=j == 0, stop=j == LAGS - 1, skip_group_check=True)
                            last.then_inc(y_p, 1)
                    with pe.Fori(0, PER // 2) as i:
                        pair(i)

            @block.scalar
            def _(act):
                def move(r, c, k):
                    act.wait_ge(v_loaded[k], (c - k) * 8 + (16 * (r * PER // 2) + 16))
                    for a, qs in ((1, 4), (2, 2)):
                        nc.scalar.activation(vi[BLK * a:BLK * a + BLK, k, 0:qs, 0:CH * SEQW - a],
                                             vi[0:BLK, k, 0:qs, a:CH * SEQW], ACT.Copy).then_inc(act_moved, 1)

                def sums(r, c, k):
                    act.wait_ge(y_p, c + (r * PER + 1))
                    for h in range(2):
                        at = c * CH + 2 * h
                        at = slice(at, at + 2) if isinstance(c, int) else bass.ds(at, 2)
                        nc.scalar.activation(yc[:, r % 2, at, :], y_ps[:, 2 * k + h, :, :], ACT.Copy).then_inc(y_act, 1)

                act.sem_inc(y_act, 4)
                move(0, 0, 0)
                for r in range(ROUNDS):
                    if r >= 2:
                        act.wait_ge(yt_done, B * (r - 1))
                    with act.Fori(0, PER // 2 - 1) as i:
                        for k in range(2):
                            move(r, i * 2 + (k + 1), 1 - k)
                            sums(r, i * 2 + k, k)
                    move(r, PER - 1, 1)
                    sums(r, PER - 2, 0)
                    if r + 1 < ROUNDS:
                        move(r + 1, 0, 0)
                    sums(r, PER - 1, 1)

            @block.gpsimd
            def _(pool):
                every = vb[:, :, :, :].rearrange("p a b k -> p (a b) k")
                pool.memset(every[:, :, 0:PADB], 0.0)
                pool.memset(every[:, :, PADB + NBLK:BW], 0.0).then_inc(zeroed, 1)
                def load(n):
                    r, b = divmod(n, B)
                    o, d = divmod(r, DH)
                    if n >= 4:
                        pool.wait_ge(vn_done, n - 4 + 3)
                    pool.dma_start(gt[:, n % 4, :], gates[o, d, :, b * S:(b + 1) * S]).then_inc(g_loaded[n % 4], 16)

                for n in range(4):
                    load(n)
                for n in range(ROUNDS * B):
                    r, b = divmod(n, B)
                    o, d = divmod(r, DH)
                    if o:
                        pool.wait_ge(vn_done, n + 3)
                        pool.dma_start(v_out[d, :, b * S:(b + 1) * S], vn[:, n % 2, :]).then_inc(out_stored[n % 2], 16)
                    if n + 4 < ROUNDS * B:
                        load(n + 4)
                    if o == 0 and b == B - 1:
                        pool.wait_ge(vb_done, B * (r + 1))
                        cut = 2 * CH
                        pool.dma_start(v_mid[d, :, 0:cut * SEQW], vb[:, 0:cut].rearrange("p a b c -> p (a b c)")).then_inc(mid_first, 16)
                        pool.wait_ge(mid_first, 16 * (r + 1))
                        pool.dma_start(v_mid[d, :, cut * SEQW:], vb[:, cut:].rearrange("p a b c -> p (a b c)")).then_inc(mid_stored, 16)
                for k in range(2):
                    pool.wait_ge(out_stored[k], 16 * (B // 2) * DH)
                pool.wait_ge(mid_first, 16 * DH)
                pool.wait_ge(mid_stored, 16 * DH)

            @block.vector
            def _(dve):
                dve.sem_inc(vn_done, 2)
                dve.wait_ge(zeroed, 1)

                def move(n):
                    k = n % 2
                    dve.wait_ge(v_loaded[k], 16 * (n // 2) + 16)
                    for a, qs in ((3, 0), (2, 2)):
                        nc.vector.tensor_copy(vi[BLK * a:BLK * a + BLK, k, qs:4, 0:CH * SEQW - a],
                                              vi[0:BLK, k, qs:4, a:CH * SEQW]).then_inc(dve_moved, 1)

                def sequence(r, b):
                    o, d = divmod(r, DH)
                    k = b % 2
                    n = B * r + b
                    if b == 0:
                        dve.wait_ge(y_act, 4 + 2 * PER * (r + 1))
                        if o == 0 and r:
                            dve.wait_ge(mid_first, 16 * r)
                            dve.wait_ge(mid_stored, 16 * r)
                    dve.wait_ge(vn_done, n + 1)
                    nc.vector.transpose(yt[:, k, :].rearrange("p (i c) -> p i c", c=BLK),
                                        yc[:, r % 2, :, b * NBLK:(b + 1) * NBLK].rearrange("p c i -> p i c")).then_inc(yt_done, 1)
                    dve.wait_ge(yt_done, n + 1)
                    dve.wait_ge(g_loaded[n % 4], 16 * (n // 4) + 16)
                    if o:
                        dve.wait_ge(out_stored[k], 16 * (B // 2) * (r - DH) + (b - k) * 8)
                    else:
                        dve.wait_ge(vb_done, n)
                    nc.vector.tensor_tensor(vn[:, k, :].rearrange("p (i s) -> p i s", s=BLK),
                                            yt[:, k, :].rearrange("p (i s) -> p i s", s=BLK)[:, :, ::-1],
                                            gt[:, n % 4, :].rearrange("p (i s) -> p i s", s=BLK), ALU.mult).then_inc(vn_done, 1)
                    if o == 0:
                        dve.wait_ge(vn_done, n + 3)
                        nc.vector.transpose(vb[:, :, b, PADB:PADB + NBLK].rearrange("p c k -> p k c"),
                                            vn[:, k, :].rearrange("p (k s) -> p k s", s=BLK)).then_inc(vb_done, 1)

                after = (1, 2, 2, 2, 1, 0, 0, 0)
                move(0)
                for r in range(ROUNDS):
                    for c in range(PER):
                        if r * PER + c + 1 < ROUNDS * PER:
                            move(r * PER + c + 1)
                        if r:
                            for b in range(sum(after[:c]), sum(after[:c + 1])):
                                sequence(r - 1, b)
                for b in range(B):
                    sequence(ROUNDS - 1, b)


def hyena_out(nc, tag, consts, x, v, out_w, out_b, gate_w, rows, count0):
    with ExitStack() as ctx:
        m = Memory(nc, ctx, tag)
        x_res = m.sb("x_res", [P, 2, NT, D])
        vt = m.sb("vt", [P, 2, DH, S])
        v_hi = m.sb("v_hi", [P, 2, DH, S], F32R)
        v_lo = m.sb("v_lo", [P, 2, DH, S], F32R)
        w_hi = m.sb("w_hi", [P, DH, D], F32R)
        w_lo = m.sb("w_lo", [P, DH, D], F32R)
        w_raw = m.sb("w_raw", [P, DH, D])
        brow = m.sb("brow", [1, D])
        b_hi = m.sb("b_hi", [1, D], F32R)
        b_lo = m.sb("b_lo", [1, D], F32R)
        one = m.sb("one", [1, P], F32R)
        bank = m.ps("bank", [P, NT // 2, 2, D])
        route_ps = m.ps("route_ps", [P, 512])
        route = Route(nc, m, consts, rows, count0, buffers=2)
        w_in, w_hi_done, w_lo_done, v_hi_done, v_lo_done, out_p, held = (
            m.sem(n) for n in "w_in w_hi_done w_lo_done v_hi_done v_lo_done out_p held".split())
        x_loaded = [m.sem(f"x_loaded{k}") for k in range(2)]
        v_loaded = [m.sem(f"v_loaded{k}") for k in range(2)]

        count_ps = route_ps[:, 0:2 * NT].rearrange("p (a t) -> p a t", a=2)

        def sequences(engine, step):
            with engine.Fori(0, (B - 2) // 2) as i:
                for k in range(2):
                    step(i * 2 + (1 + k), (1 + k) % 2)

        with nc.Block() as block:

            @block.sync
            def _(sp):
                sp.dma_start(w_raw[:, :, :], out_w.rearrange("(c p) n -> p c n", p=P)).then_inc(w_in, 16)
                sp.dma_start(brow[:, :], out_b.rearrange("(a n) -> a n", a=1)).then_inc(w_in, 16)
                route.load(sp, gate_w)

                def load_v(b, k):
                    sp.dma_start(vt[:, k], v[:, :, bass.ds(b * S, S)].rearrange("d p s -> p d s")).then_inc(v_loaded[k], 16)

                def load_x(b, k):
                    sp.dma_start(x_res[:, k], x[bass.ds(b * S, S), :].rearrange("(t p) c -> p t c", p=P)).then_inc(x_loaded[k], 16)

                for k in range(2):
                    load_v(k, k)
                    load_x(k, k)
                with sp.Fori(1, B // 2) as i:
                    for k in range(2):
                        b = i * 2 + k
                        sp.wait_ge(v_lo_done, b - 1)
                        sp.sem_inc(held, 1)
                        load_v(b, k)
                        sp.wait_ge(route.x_done, NT * b - NT)
                        sp.sem_inc(held, 1)
                        load_x(b, k)
                route.sync_end(nc, sp, B)

            @block.gpsimd
            def _(pool):
                route.prepare_pool(nc, pool)
                route.ln.power(nc, pool, 0)

                def step(i, k):
                    route.ln.power(nc, pool, i)
                    route.pool(nc, pool, i - 1, 1 - k)
                sequences(pool, step)
                step(B - 1, (B - 1) % 2)
                route.pool(nc, pool, B - 1, (B - 1) % 2)
                pool.wait_ge(route.sent, 16 * NT * B)

            @block.tensor
            def _(pe):
                def products(i, k):
                    pe.wait_ge(v_lo_done, i + 1)
                    terms = [(a, c, d) for d in range(DH) for a, c in ((v_hi, w_lo), (v_lo, w_hi), (v_hi, w_hi))]
                    for t in range(NT):
                        if t % 2 == 0 and not (isinstance(i, int) and i == 0):
                            pe.wait_ge(route.x_done, NT * i - NT + t + 2)
                        out = bank[:, t // 2, t % 2, :]
                        nc.tensor.matmul(out, one[:, :], b_lo[:, :], start=t % 2 == 0, stop=False, skip_group_check=True)
                        nc.tensor.matmul(out, one[:, :], b_hi[:, :], start=False, stop=False, skip_group_check=True)
                        for n, (a, c, d) in enumerate(terms):
                            last = nc.tensor.matmul(out, a[:, k, d, t * P:(t + 1) * P], c[:, d, :],
                                                    start=False, stop=n == len(terms) - 1, skip_group_check=True)
                        last.then_inc(out_p, 1)

                def step(i, k):
                    products(i, k)
                    route.tensor(nc, pe, i - 1, count_ps)

                pe.wait_ge(w_lo_done, 1)
                products(0, 0)
                sequences(pe, step)
                step(B - 1, (B - 1) % 2)
                route.tensor(nc, pe, B - 1, count_ps)

            @block.scalar
            def _(act):
                def high(i, k):
                    act.wait_ge(v_loaded[k], (i - k) * 8 + 16)
                    if not isinstance(i, int):
                        act.wait_ge(out_p, NT * i - NT)
                    nc.scalar.activation(v_hi[:, k], vt[:, k], ACT.Copy).then_inc(v_hi_done, 1)

                for k in range(2):
                    high(k, k)
                with act.Fori(1, B // 2) as i:
                    for k in range(2):
                        high(i * 2 + k, k)

            @block.vector
            def _(dve):
                tt = nc.vector.tensor_tensor
                dve.wait_ge(w_in, 32)
                nc.vector.tensor_copy(w_hi[:, :, :], w_raw[:, :, :])
                nc.vector.tensor_copy(one[:, :], consts.ones[0:1, :])
                nc.vector.tensor_copy(b_hi[:, :], brow[:, :]).then_inc(w_hi_done, 1)
                dve.wait_ge(w_hi_done, 1)
                tt(b_lo[:, :], brow[:, :], f32(b_hi[:, :]), ALU.subtract)
                tt(w_lo[:, :, :], w_raw[:, :, :], f32(w_hi[:, :, :]), ALU.subtract).then_inc(w_lo_done, 1)

                def low(i, k):
                    dve.wait_ge(v_hi_done, i + 1)
                    tt(v_lo[:, k], vt[:, k], f32(v_hi[:, k]), ALU.subtract).then_inc(v_lo_done, 1)


                def sums(i, k):
                    if not isinstance(i, int) or i:
                        dve.wait_ge(route.sent, 16 * NT * i - 16 * NT)
                    dve.wait_ge(x_loaded[k], (i - k) * 8 + 16)
                    for t in range(0, NT, 2):
                        dve.wait_ge(out_p, NT * i + t + 2)
                        tt(route.row[:, k, t:t + 2, 0:D], bank[:, t // 2, :, :], x_res[:, k, t:t + 2, :], ALU.add).then_inc(route.x_done, 2)
                    route.vector_stats(nc, dve, i, k)

                def choose(i, k):
                    route.vector_norm(nc, dve, i, k)
                    route.vector_choose(nc, dve, i, k)

                def step(i, k, more=True):
                    if more:
                        low(i + 1, 1 - k)
                    sums(i, k)
                    route.vector_slots(nc, dve, i - 1, count_ps, 1 - k)
                    choose(i, k)

                low(0, 0)
                route.prepare(nc, dve)
                low(1, 1)
                sums(0, 0)
                choose(0, 0)
                sequences(dve, step)
                step(B - 1, (B - 1) % 2, False)
                dve.wait_ge(route.sent, 16 * NT * (B - 1))
                route.vector_slots(nc, dve, B - 1, count_ps, (B - 1) % 2)
                route.vector_end(nc, dve, B)


def hybrid_block(nc, x, wq, wk, wv, wo, times, phases, freqs, mlp_w1, mlp_b1, mlp_w2, mlp_b2, mlp_w3, mlp_b3, decay,
                 in_w, in_b, conv_w, conv_b, hy_gate_w, hy_gate_b, hy_out_w, hy_out_b,
                 gate_w, w1, b1, w2, b2, sw1, sb1, sw2, sb2, out):
    def scratch(name, shape):
        return nc.dram_tensor(name, shape, F32).ap()
    arranged = scratch("arranged", [ORDER, DH, CHUNKS, 4, CH, FW])
    v_blocks = scratch("v_blocks", [DH, P, BLK * SEQW])
    v_mid = scratch("v_mid", [DH, P, BLK * SEQW])
    v_out = scratch("v_out", [DH, P, T])
    gates = scratch("gates", [ORDER, DH, P, T])
    rows_a, rows_b = scratch("rows_a", [SLOTS, ROW]), scratch("rows_b", [SLOTS, ROW])
    count_a, count_b = scratch("count_a", [1, 1]), scratch("count_b", [1, 1])
    x_mid = scratch("x_mid", [T, D])
    with ExitStack() as ctx:
        consts = Constants(nc, ctx)
        consts.make(nc)
        filters(nc, "flt", times, phases, freqs, mlp_w1, mlp_b1, mlp_w2, mlp_b2, mlp_w3, mlp_b3, decay, arranged)
        attention(nc, "att", consts, x, wq, wk, wv, wo, gate_w, rows_a, count_a)
        feed_forward(nc, "ffa", consts, rows_a, count_a, w1, b1, w2, b2, sw1, sb1, sw2, sb2, x_mid)
        projections(nc, "prj", consts, x_mid, in_w, in_b, conv_w, conv_b, hy_gate_w, hy_gate_b, v_blocks, gates)
        convolutions(nc, "cnv", arranged, v_blocks, gates, v_mid, v_out)
        hyena_out(nc, "hyo", consts, x_mid, v_out, hy_out_w, hy_out_b, gate_w, rows_b, count_b)
        feed_forward(nc, "ffb", consts, rows_b, count_b, w1, b1, w2, b2, sw1, sb1, sw2, sb2, out)


def kernel(**inputs):
    import concourse.bacc as bacc
    from concourse.bass_utils import run_bass_kernel_spmd

    a = {name.split("_", 1)[1]: np.asarray(v) for name, v in inputs.items()}

    def columns(v):
        return np.moveaxis(v.reshape(v.shape[:-1] + (-1, P)), -1, 0)
    phases = np.zeros((ENC, 3), np.float32)
    phases[FREQS:2 * FREQS, 0] = 0.25
    phases[2 * FREQS, 1] = 1
    phases[:2 * FREQS, 2] = 1
    args = {
        "x": a["attn_a_hidden_states"].reshape(T, D),
        "wq": a["attn_a_Wq"].T, "wk": a["attn_a_Wk"].T, "wv": a["attn_a_Wv"].T, "wo": a["attn_a_Wo"].T,
        "times": np.linspace(0, 1, S, dtype=np.float32)[::-1][None], "phases": phases,
        "freqs": a["attn_b_freqs"].T,
        "mlp_w1": a["attn_b_mlp_w1"], "mlp_b1": a["attn_b_mlp_b1"].T,
        "mlp_w2": a["attn_b_mlp_w2"], "mlp_b2": a["attn_b_mlp_b2"].T,
        "mlp_w3": a["attn_b_mlp_w3"], "mlp_b3": columns(a["attn_b_mlp_b3"]), "decay": columns(a["attn_b_decay"]),
        "in_w": a["attn_b_in_proj_w"], "in_b": columns(a["attn_b_in_proj_b"]),
        "conv_w": columns(a["attn_b_conv_w"][:, :, 0]).transpose(0, 1, 3, 2), "conv_b": columns(a["attn_b_conv_b"]),
        "hy_gate_w": a["attn_b_gate_w"], "hy_gate_b": columns(a["attn_b_gate_b"]),
        "hy_out_w": a["attn_b_out_proj_w"], "hy_out_b": a["attn_b_out_proj_b"],
        "gate_w": a["ffn_gate_w"], "w1": a["ffn_w1"], "b1": a["ffn_b1"].reshape(2, HB, P).transpose(0, 2, 1),
        "w2": a["ffn_w2"], "b2": a["ffn_b2"],
        "sw1": a["ffn_sw1"], "sb1": a["ffn_sb1"].reshape(HB, P).T, "sw2": a["ffn_sw2"], "sb2": a["ffn_sb2"],
    }
    nc = bacc.Bacc("TRN2", target_bir_lowering=False, num_devices=1)
    arrays, aps = {}, []
    for name, v in args.items():
        arrays[f"in_{name}"] = np.ascontiguousarray(v)
        aps.append(nc.dram_tensor(f"in_{name}", v.shape, mybir.dt.from_np(v.dtype), kind="ExternalInput").ap())
    aps.append(nc.dram_tensor("out", [T, D], F32, kind="ExternalOutput").ap())
    hybrid_block(nc, *aps)
    r = run_bass_kernel_spmd(nc, [arrays], core_ids=[0])
    return r.results[0]["out"].reshape(B, S, D)
```
